# Optimizing a Trainium2 kernel written in Bass

```python
import numpy as np
import jax
import jax.numpy as jnp

def _softmax(x, axis=-1):
    return jax.nn.softmax(x, axis=axis)

def _gelu(x):
    return jax.nn.gelu(x, approximate=True)

def _silu(x):
    return jax.nn.silu(x)

def _sigmoid(x):
    return jax.nn.sigmoid(x)

def _layernorm(x, axis=-1, eps=1e-05):
    m = jnp.mean(x, axis=axis, keepdims=True)
    v = jnp.var(x, axis=axis, keepdims=True)
    return (x - m) / jnp.sqrt(v + eps)

def _scatter_add(tgt, idx, src, axis=0):
    return tgt.at[idx].add(src)

def _segment_sum(src, seg, n):
    return jax.ops.segment_sum(src, seg, n)
kernel_name = 'mk_seq_preln_d1_jaxref_r8_652569'

def setup_inputs(seed: int=0):
    np.random.seed(seed)
    _w = jnp.asarray

    def _L0_attn_setup():
        import jax, jax.numpy as jnp
        import numpy as np
        B, C, D, H = (2, 256, 128, 16)
        HE = D // H
        key = jax.random.key(seed)
        k1, k2, k3, k4, k5 = jax.random.split(key, 5)
        s = 0.02
        return {'x': jax.random.normal(k1, (B, C, D), dtype=jnp.float32), 'Wqkv': jax.random.normal(k2, (HE, 3 * HE), dtype=jnp.float32) * s, 'bqkv': jax.random.normal(k3, (3 * HE,), dtype=jnp.float32) * s, 'Wr': jax.random.normal(k4, (D, D), dtype=jnp.float32) * s, 'br': jax.random.normal(k5, (D,), dtype=jnp.float32) * s}
    _L0_attn_in = _L0_attn_setup()

    def _L0_ffn_setup():
        import jax, jax.numpy as jnp
        import numpy as np
        NUM_HEADS = 16
        TOP_K = 2
        ROPE_BASE = 10000.0
        LN_EPS = 1e-05

        def _rope_sin_cos(S, D, dtype):
            inv_freq = 1.0 / ROPE_BASE ** (jnp.arange(0, D, 2, dtype=jnp.float32) / D)
            freqs = jnp.arange(S, dtype=jnp.float32)[:, None] * inv_freq[None, :]
            sin = jnp.sin(freqs).astype(dtype)[None, :, None, :]
            cos = jnp.cos(freqs).astype(dtype)[None, :, None, :]
            return (sin, cos)

        def _apply_rope(x, sin, cos):
            x1, x2 = (x[..., 0::2], x[..., 1::2])
            r1 = x1 * cos - x2 * sin
            r2 = x1 * sin + x2 * cos
            return jnp.stack([r1, r2], axis=-1).reshape(x.shape)

        def _layer_norm(x, w, b):
            mu = jnp.mean(x, axis=-1, keepdims=True)
            var = jnp.mean(jnp.square(x - mu), axis=-1, keepdims=True)
            return (x - mu) * jax.lax.rsqrt(var + LN_EPS) * w + b
        key = jax.random.key(seed)
        ks = jax.random.split(key, 8)
        B, S, E, NE = (2, 256, 128, 8)
        s = 0.02
        return {'x': jax.random.normal(ks[0], (B, S, E), dtype=jnp.float32), 'in_proj_w': jax.random.normal(ks[1], (3 * E, E), dtype=jnp.float32) * s, 'in_proj_b': jnp.zeros((3 * E,), dtype=jnp.float32), 'out_proj_w': jax.random.normal(ks[2], (E, E), dtype=jnp.float32) * s, 'out_proj_b': jnp.zeros((E,), dtype=jnp.float32), 'gate_w': jax.random.normal(ks[3], (NE, E), dtype=jnp.float32) * s, 'gate_b': jnp.zeros((NE,), dtype=jnp.float32), 'expert_w': jax.random.normal(ks[4], (NE, E, E), dtype=jnp.float32) * s, 'expert_b': jnp.zeros((NE, E), dtype=jnp.float32), 'ln1_w': jnp.ones((E,), dtype=jnp.float32), 'ln1_b': jnp.zeros((E,), dtype=jnp.float32), 'ln2_w': jnp.ones((E,), dtype=jnp.float32), 'ln2_b': jnp.zeros((E,), dtype=jnp.float32)}
    _L0_ffn_in = _L0_ffn_setup()
    _d = {'L0_attn_x': _L0_attn_in['x'], 'L0_attn_Wqkv': _L0_attn_in['Wqkv'], 'L0_attn_bqkv': _L0_attn_in['bqkv'], 'L0_attn_Wr': _L0_attn_in['Wr'], 'L0_attn_br': _L0_attn_in['br'], 'L0_ffn_in_proj_w': _L0_ffn_in['in_proj_w'], 'L0_ffn_in_proj_b': _L0_ffn_in['in_proj_b'], 'L0_ffn_out_proj_w': _L0_ffn_in['out_proj_w'], 'L0_ffn_out_proj_b': _L0_ffn_in['out_proj_b'], 'L0_ffn_gate_w': _L0_ffn_in['gate_w'], 'L0_ffn_gate_b': _L0_ffn_in['gate_b'], 'L0_ffn_expert_w': _L0_ffn_in['expert_w'], 'L0_ffn_expert_b': _L0_ffn_in['expert_b'], 'L0_ffn_ln1_w': _L0_ffn_in['ln1_w'], 'L0_ffn_ln1_b': _L0_ffn_in['ln1_b'], 'L0_ffn_ln2_w': _L0_ffn_in['ln2_w'], 'L0_ffn_ln2_b': _L0_ffn_in['ln2_b']}
    _x0 = _d['L0_attn_x']
    _d['L0_attn_x'] = jax.random.normal(jax.random.fold_in(jax.random.key(seed), 1), (4, 1024, 128), dtype=_x0.dtype)
    del _x0
    return _d

def reference(L0_attn_x, L0_attn_Wqkv, L0_attn_bqkv, L0_attn_Wr, L0_attn_br, L0_ffn_in_proj_w, L0_ffn_in_proj_b, L0_ffn_out_proj_w, L0_ffn_out_proj_b, L0_ffn_gate_w, L0_ffn_gate_b, L0_ffn_expert_w, L0_ffn_expert_b, L0_ffn_ln1_w, L0_ffn_ln1_b, L0_ffn_ln2_w, L0_ffn_ln2_b):

    def _L0_attn_ref(x, Wqkv, bqkv, Wr, br):
        import jax, jax.numpy as jnp
        import numpy as np
        B, C, D, H = (2, 256, 128, 16)
        HE = D // H
        b, c, d = x.shape
        h, he = (H, HE)
        xh = x.reshape(b, c, h, he).transpose(0, 2, 1, 3)
        qkv = jnp.einsum('bhce,ef->bhcf', xh, Wqkv) + bqkv
        q, k, v = jnp.split(qkv, 3, axis=-1)
        att = jnp.einsum('bhqe,bhke->bhqk', q, k) / jnp.sqrt(jnp.float32(he))
        mask = jnp.tril(jnp.ones((c, c), dtype=att.dtype), k=-1)
        att = jax.nn.softmax(att * mask, axis=-1)
        out = jnp.einsum('bhqk,bhke->bhqe', att, v)
        out = out.transpose(0, 2, 1, 3).reshape(b, c, d)
        out = out @ Wr + br
        return out

    def _L0_ffn_ref(x, in_proj_w, in_proj_b, out_proj_w, out_proj_b, gate_w, gate_b, expert_w, expert_b, ln1_w, ln1_b, ln2_w, ln2_b):
        import jax, jax.numpy as jnp
        import numpy as np
        NUM_HEADS = 16
        TOP_K = 2
        ROPE_BASE = 10000.0
        LN_EPS = 1e-05

        def _rope_sin_cos(S, D, dtype):
            inv_freq = 1.0 / ROPE_BASE ** (jnp.arange(0, D, 2, dtype=jnp.float32) / D)
            freqs = jnp.arange(S, dtype=jnp.float32)[:, None] * inv_freq[None, :]
            sin = jnp.sin(freqs).astype(dtype)[None, :, None, :]
            cos = jnp.cos(freqs).astype(dtype)[None, :, None, :]
            return (sin, cos)

        def _apply_rope(x, sin, cos):
            x1, x2 = (x[..., 0::2], x[..., 1::2])
            r1 = x1 * cos - x2 * sin
            r2 = x1 * sin + x2 * cos
            return jnp.stack([r1, r2], axis=-1).reshape(x.shape)

        def _layer_norm(x, w, b):
            mu = jnp.mean(x, axis=-1, keepdims=True)
            var = jnp.mean(jnp.square(x - mu), axis=-1, keepdims=True)
            return (x - mu) * jax.lax.rsqrt(var + LN_EPS) * w + b
        B, S, E = x.shape
        H = NUM_HEADS
        D = E // H
        xh = x.reshape(B, S, H, D)
        sin, cos = _rope_sin_cos(S, D, x.dtype)
        q_in = _apply_rope(xh, sin, cos).reshape(B, S, E)
        k_in = q_in
        v_in = x
        Wq, Wk, Wv = jnp.split(in_proj_w, 3, axis=0)
        bq, bk, bv = jnp.split(in_proj_b, 3, axis=0)
        q = (q_in @ Wq.T + bq).reshape(B, S, H, D)
        k = (k_in @ Wk.T + bk).reshape(B, S, H, D)
        v = (v_in @ Wv.T + bv).reshape(B, S, H, D)
        scale = 1.0 / jnp.sqrt(jnp.asarray(D, dtype=x.dtype))
        scores = jnp.einsum('bqhd,bkhd->bhqk', q, k) * scale
        causal = jnp.tril(jnp.ones((S, S), dtype=bool))
        scores = jnp.where(causal[None, None], scores, jnp.asarray(-jnp.inf, dtype=scores.dtype))
        attn = jax.nn.softmax(scores, axis=-1)
        ctx = jnp.einsum('bhqk,bkhd->bqhd', attn, v).reshape(B, S, E)
        attn_out = ctx @ out_proj_w.T + out_proj_b
        x1 = _layer_norm(x + attn_out, ln1_w, ln1_b)
        gates = jax.nn.softmax(x1 @ gate_w.T + gate_b, axis=-1)
        _, top_idx = jax.lax.top_k(gates, TOP_K)
        top_gates = jnp.take_along_axis(gates, top_idx, axis=-1)
        expert_outputs = jnp.einsum('bsd,efd->bsef', x1, expert_w) + expert_b[None, None]
        sel = jnp.take_along_axis(expert_outputs, top_idx[..., None], axis=2)
        moe_out = jnp.sum(sel * top_gates[..., None], axis=2)
        return _layer_norm(x1 + moe_out, ln2_w, ln2_b)
    x = L0_attn_x
    x = x + _L0_attn_ref(_layernorm(x, axis=-1), L0_attn_Wqkv, L0_attn_bqkv, L0_attn_Wr, L0_attn_br)
    x = x + _L0_ffn_ref(_layernorm(x, axis=-1), L0_ffn_in_proj_w, L0_ffn_in_proj_b, L0_ffn_out_proj_w, L0_ffn_out_proj_b, L0_ffn_gate_w, L0_ffn_gate_b, L0_ffn_expert_w, L0_ffn_expert_b, L0_ffn_ln1_w, L0_ffn_ln1_b, L0_ffn_ln2_w, L0_ffn_ln2_b)
    return x

_drawn_inputs = setup_inputs


def setup_inputs(seed=0):
    import zlib

    import numpy as np

    out = dict(_drawn_inputs(seed))
    spreads = {'L0_ffn_in_proj_b': (0.0, 0.556),
     'L0_ffn_out_proj_b': (0.0, 0.1),
     'L0_ffn_gate_b': (0.0, 0.405),
     'L0_ffn_expert_b': (0.0, 0.749),
     'L0_ffn_ln1_w': (1.0, 0.2),
     'L0_ffn_ln1_b': (0.0, 0.1),
     'L0_ffn_ln2_w': (1.0, 0.2),
     'L0_ffn_ln2_b': (0.0, 0.1)}
    factors = {'L0_attn_Wqkv': 8.0,
     'L0_attn_bqkv': 8.0,
     'L0_attn_Wr': 8.0,
     'L0_attn_br': 2.812,
     'L0_ffn_in_proj_w': 8.0,
     'L0_ffn_out_proj_w': 4.673}
    for name, (base, spread) in spreads.items():
        noise = np.random.default_rng([zlib.crc32(name.encode()), seed]).standard_normal(out[name].shape)
        drawn = base * np.exp(spread * noise) if base else spread * noise
        out[name] = jnp.asarray(drawn.astype(out[name].dtype))
    for name, factor in factors.items():
        out[name] = (out[name] * factor).astype(out[name].dtype)
    return out
```

```python
from contextlib import ExitStack

import concourse.bass as bass
from concourse import mybir

B, S, D, H = 4, 1024, 128, 16
HE = D // H
NE = 8
P = 128
T = S // P
TQ = 2
NQ = T // TQ
QW = TQ * P
HG = 4
NG = H // HG
VW = 32
NPART = 3
KROWS = NPART * NPART * HE
SROW = KROWS
KPAD = 96
SCALE = float(HE) ** -0.5
EPS = 1e-5
NEG = -1e30
LIMIT = 110.0 / SCALE
SQUARE_LIMIT = 1e16

KINDS = [
    [[(0, 0, 0, 512)], [(0, 512, 512, 512)]],
    [[(1, 0, 512, 512)], [(1, 512, 128, 384), (7, 896, 896, 128)]],
    [[(2, 0, 512, 512)], [(2, 512, 256, 256), (6, 768, 768, 256)]],
    [[(3, 0, 512, 512)], [(3, 512, 384, 128), (5, 640, 640, 384)]],
    [[(4, 0, 512, 512)]],
]
DIAGONALS = [(0, 0), (512, 384), (512, 256), (512, 128), (0, 512)]
UG = 18
UB = UG * NG
GG = 9
GB = GG * NG
NSC = 2
FILLS = 10
NPB = 9
PV_LAG = 5

F32 = mybir.dt.float32
BF16 = mybir.dt.bfloat16
I32 = mybir.dt.int32
ACT = mybir.ActivationFunctionType
ALU = mybir.AluOpType
AX = mybir.AxisListType


def unit_kind(n):
    u = n % UG
    if u < 16:
        return u // 4, [(u % 4, 0)]
    return 4, [(2 * (u - 16), 0), (2 * (u - 16) + 1, 512)]


def group_of(g):
    return (g // 2, g % 2) if g < 8 else (4, 0)


def groups_before(kind):
    return min(2 * kind + 2, GG)


class Jobs:

    def __init__(self, names, before):
        assert len(names) % 2 == 0 and before % 2 == 0
        self.index = {name: i for i, name in enumerate(names)}
        self.n, self.before = len(names), before

    def bank(self, name):
        return self.index[name] % 2

    def done(self, b, name):
        return self.before + b * self.n + self.index[name] + 1

    def freed(self, b, name):
        return self.before // 2 + b * (self.n // 2) + self.index[name] // 2


def build(nc, x_d, wqkv_d, bqk_d, bv_d, wr_d, br_d, win_d, binqk_d, binv_d, wo_d, bo_d, wg_d, bg_d, we_d, be_d,
          l1w_d, l1b_d, l2w_d, l2b_d, cos_d, sin_d, ident_d, hide_d, later_d, headsum_d, iota8_d, out_d):
    ctx = ExitStack()
    with ctx:
        def sb(name, shape, dt=F32):
            return ctx.enter_context(nc.sbuf_tensor(name, shape, dt))

        def sem(name):
            return ctx.enter_context(nc.semaphore(name))

        def dram(name, shape, dt=F32):
            return nc.dram_tensor(f"{name}_dram", shape, dt, kind="Internal").ap()

        parts_d = [dram(f"parts{a}", [B, 2, NPART, P, S], BF16) for a in range(2)]
        shift_d = [dram(f"shift{a}", [B, 2, H, S], BF16) for a in range(2)]
        values_d = [dram(f"values{a}", [B, NG, P, T, HG * VW]) for a in range(2)]
        num_d = [dram(f"num{a}", [B, NG, P, S]) for a in range(2)]
        suffix_d = dram("suffix", [B, P, T, H * 9])
        x2_d = dram("x2", [B, P, T, D])
        xn_d = dram("xn", [B, P, T, D])

        ident = sb("ident", [P, P])
        ident_b = sb("ident_b", [P, P], BF16)
        hide = [sb(f"hide{a}", [P, P], BF16) for a in range(2)]
        later = sb("later", [P, P])
        ones = sb("ones", [P, P])
        headsum = sb("headsum", [P, H], BF16)
        wqkv = sb("wqkv", [P, 3, P])
        bqk = sb("bqk", [P, 2])
        bv = sb("bv", [P, D])
        wr = sb("wr", [P, D])
        br = sb("br", [P, D])
        win = sb("win", [P, 3, P])
        binqk = sb("binqk", [P, 2])
        binv = sb("binv", [P, D])
        wo = sb("wo", [P, D])
        bo = sb("bo", [P, D])
        wg = sb("wg", [P, NE])
        bg = sb("bg", [P, NE])
        we = sb("we", [P, NE * D])
        be = sb("be", [NE, D])
        l1w = sb("l1w", [P, D])
        l1b = sb("l1b", [P, D])
        l2w = sb("l2w", [P, D])
        l2b = sb("l2b", [P, D])
        cos = sb("cos", [P, T, HE // 2])
        sin = sb("sin", [P, T, HE // 2])
        iota8 = sb("iota8", [P, NE])

        qs = [sb(f"qs{i}", [KPAD, HG, S], BF16) for i in range(2)]
        ks = [sb(f"ks{i}", [KPAD, HG, S], BF16) for i in range(2)]
        vs = [sb(f"vs{i}", [P, T, HG * VW]) for i in range(2)]
        probs = [sb(f"probs{i}", [P, S]) for i in range(NPB)]
        num = [sb(f"num{i}", [P, S]) for i in range(2)]
        mx = sb("mx", [P, HG * T])
        mxn = sb("mxn", [HG * T, P])
        mxr = sb("mxr", [HG * T, P])
        mxp = sb("mxp", [HG * T, 2, P], BF16)

        xrow = sb("xrow", [P, T, D])
        xnorm = sb("xnorm", [P, T, D])
        rope = sb("rope", [P, T, D])
        stats = sb("stats", [P, T, 6])
        mv = sb("mv", [P, T, 2])
        var = sb("var", [P, T])
        lnv = sb("lnv", [P, T])
        r0 = sb("r0", [P, T])
        rt = sb("rt", [P, T])
        rstd = sb("rstd", [P, T])
        xT = sb("xT", [P, 2, QW])
        qk = sb("qk", [P, 2, QW])
        qkr = sb("qkr", [P, 2, QW])
        part = [sb(f"part{i}", [P, NPART, 2, QW], BF16) for i in range(2)]
        sq = sb("sq", [P, 3, QW], BF16)
        nrm = sb("nrm", [H, 3, S])
        kmx = sb("kmx", [H, T])
        c2 = sb("c2", [H, S])
        cl = sb("cl", [H, S])
        cc = sb("cc", [H, S])
        gm = sb("gm", [H, 2])
        gm1 = sb("gm1", [1, 1])
        ns = cc
        shb = sb("shb", [H, 2, S], BF16)
        flags = sb("flags", [1, 2 * B], I32)
        vq = [sb(f"vq{i}", [P, TQ, H * VW]) for i in range(2)]
        vc = sb("vc", [P, T, H * 9])
        vsum = sb("vsum", [P, T, H * 9])
        sfx = sb("sfx", [P, T, H * 9])
        sh2 = sb("sh2", [H, 2, S], BF16)
        esum, em = c2, cl
        emr = sb("emr", [P, T, H])
        nt = [sb(f"nt{i}", [P, NG, QW]) for i in range(2)]
        tot = sb("tot", [P, H, 9])
        rden = sb("rden", [P, H])
        att = sb("att", [P, D])
        attT = sb("attT", [P, D])
        x2 = sb("x2s", [P, T, D])
        x1 = sb("x1", [P, T, D])
        x1T = rope
        gl = sb("gl", [P, T, NE])
        ga = sb("ga", [P, T, NE])
        gb = sb("gb", [P, T, NE])
        gmask = sb("gmask", [P, T, NE])
        gidx = sb("gidx", [P, T])
        gsum = sb("gsum", [P, T])
        G = sb("G", [P, T, NE])
        GT = nrm[0:NE, 0, :].rearrange("e (t s) -> e t s", t=T)
        moe = sb("moe", [P, D])
        yout = sb("yout", [P, T, D])
        rtmp = [w[:, 4 * i:4 * i + 4, :].rearrange("p t d -> p (t d)") for w in (yout, x1) for i in range(2)]

        scores = ctx.enter_context(nc.psum_tensor("scores", [P, NSC, 2, 512], F32))
        acc = ctx.enter_context(nc.psum_tensor("acc", [P, 2, 512], F32))
        side = ctx.enter_context(nc.psum_tensor("side", [P, 2, 512], F32))

        weights_in = sem("weights_in")
        filled = sem("filled")
        narrowed = sem("narrowed")
        passed = [sem(f"passed_{e}") for e in ("sync", "pool", "tensor")]
        dve_step = sem("dve_step")
        act_step = sem("act_step")
        side_done = sem("side_done")
        side_free = [sem(f"side_free{i}") for i in range(2)]
        x_in = sem("x_in")
        var_ready = sem("var_ready")
        r0_ready = sem("r0_ready")
        rows_ready = sem("rows_ready")
        part_ready = sem("part_ready")
        part_out = [sem(f"part_out{i}") for i in range(2)]
        sq_ready = sem("sq_ready")
        vq_out = [sem(f"vq_out{i}") for i in range(2)]
        square_ready = sem("square_ready")
        root_ready = sem("root_ready")
        gap_ready = sem("gap_ready")
        shift_ready = sem("shift_ready")
        shift_out = sem("shift_out")
        flag_ready = sem("flag_ready")
        vsum_ready = sem("vsum_ready")
        sfx_out = sem("sfx_out")
        qs_in = [sem(f"qs_in{i}") for i in range(2)]
        vs_in = [sem(f"vs_in{i}") for i in range(2)]
        scores_ready = sem("scores_ready")
        probs_raw = sem("probs_raw")
        probs_ready = sem("probs_ready")
        group_done = sem("group_done")
        acc_read = sem("acc_read")
        num_out = [sem(f"num_out{i}") for i in range(2)]
        m_in = sem("m_in")
        m_scores = sem("m_scores")
        m_read = sem("m_read")
        m_rows = sem("m_rows")
        m_turned = sem("m_turned")
        m_parts = sem("m_parts")
        m_out = sem("m_out")
        sh2_in = sem("sh2_in")
        sfx_in = sem("sfx_in")
        nt_in = [sem(f"nt_in{i}") for i in range(2)]
        xn_in = sem("xn_in")
        esum_ready = sem("esum_ready")
        em_ready = sem("em_ready")
        att_ready = sem("att_ready")
        rows_out = sem("rows_out")
        x1_ready = sem("x1_ready")
        gates_shifted = sem("gates_shifted")
        gates_exp = sem("gates_exp")
        G_ready = sem("G_ready")
        y_ready = sem("y_ready")
        y_out = sem("y_out")

        def projection_jobs(a):
            kinds = ("xT", "qk", "v", "norm", "diag") if a else ("xT", "qk", "v", "norm")
            return [(k, j) for j in range(NQ) for k in kinds]

        def combination_jobs():
            return [(k, t) for t in range(T) for k in ("num", "att", "out")]

        P1 = Jobs(projection_jobs(0) + [("suffix", k) for k in range(3)] + [("gap", 0)], 0)
        P2 = Jobs([("em", 0), ("pad", 0)] + combination_jobs() + projection_jobs(1) + [("gap", 0), ("pad", 1)],
                  B * P1.n)
        P3 = Jobs(combination_jobs() + [("x1T", j) for j in range(NQ)] + [("gate", 0), ("GT", 0), ("GT", 1)]
                  + [(k, t) for t in range(T) for k in ("bias", "e0", "e1")] + [("pad", 0)],
                  B * (P1.n + P2.n))

        WEIGHTS = [(wqkv, wqkv_d), (bqk, bqk_d), (wr, wr_d), (win, win_d), (binqk, binqk_d), (wo, wo_d),
                   (wg, wg_d), (we, we_d), (be, be_d), (ident, ident_d), (later, later_d)]
        NARROW = [(ident_b, xnorm[:, 0, :], ident_d), (hide[0], xnorm[:, 1, :], hide_d[0]),
                  (hide[1], xnorm[:, 2, :], hide_d[1]), (headsum, xnorm[:, 3, 0:H], headsum_d)]
        ROWS = [(bv, bv_d), (binv, binv_d), (br, br_d), (bo, bo_d), (bg, bg_d), (l1w, l1w_d), (l1b, l1b_d),
                (l2w, l2w_d), (l2b, l2b_d), (iota8, iota8_d)]
        n_weights = len(WEIGHTS) + len(NARROW) + len(ROWS) + 2
        QS_DMAS = 2 * NPART + 1
        M_DMAS = 2 * NPART

        block = ctx.enter_context(nc.Block())

        @block.sync
        def _(sp):
            def wait(semaphore, value):
                sp.wait_ge(semaphore, value)
                sp.sem_inc(passed[0], 1)

            def bc(ap):
                return ap.unsqueeze(0).broadcast_to([P, ap.shape[0]])

            sp.wait_ge(filled, FILLS)
            for t, d in WEIGHTS:
                sp.dma_start(t[:], d).then_inc(weights_in, 16)
            for _t, landing, d in NARROW:
                sp.dma_start(landing, d).then_inc(weights_in, 16)
            for t, d in ROWS:
                sp.dma_start(t[:, :], bc(d)).then_inc(weights_in, 16)
            for t, d in ((cos, cos_d), (sin, sin_d)):
                sp.dma_start(t[:, :, :], d.rearrange("(t p) f -> p t f", p=P)).then_inc(weights_in, 16)

            def rows_of(dst, b):
                return dst[b].rearrange("(t p) d -> p t d", p=P)

            def after(jobs, b, *names):
                for name in names:
                    wait(side_free[jobs.bank(name)], jobs.freed(b, name) + 1)

            def projected_out(jobs, a, b):
                n = (a * B + b) * NQ
                for j in range(NQ):
                    wait(part_ready, n + j + 1)
                    for c in range(2):
                        sp.dma_start(parts_d[a][b, c].rearrange("i p s -> p i s")[:, :, j * QW:(j + 1) * QW],
                                     part[j % 2][:, :, c, :]).then_inc(part_out[j % 2], 16)
                    after(jobs, b, ("v", j))
                    for g in range(NG):
                        sp.dma_start(values_d[a][b, g][:, j * TQ:(j + 1) * TQ, :],
                                     vq[j % 2][:, :, g * HG * VW:(g + 1) * HG * VW]).then_inc(vq_out[j % 2], 16)
                wait(shift_ready, a * B + b + 1)
                sp.dma_start(shift_d[a][b].rearrange("i h s -> h i s"), shb[:, :, :]).then_inc(shift_out, 16)

            def parts_in(a, b, g, u, landed):
                heads = slice(g * HG * HE, (g + 1) * HG * HE)
                for i in range(NPART):
                    r = slice(i * NPART * HE, (i + 1) * NPART * HE)
                    q1 = parts_d[a][b, 0, i, heads].rearrange("(e h) s -> e (h s)", e=HE)
                    k3 = parts_d[a][b, 1, :, heads].rearrange("j (e h) s -> j e (h s)", e=HE)
                    sp.dma_start(qs[u][r, :, :].rearrange("r h s -> r (h s)"),
                                 q1.unsqueeze(0).broadcast_to([NPART, HE, HG * S])).then_inc(landed, 16)
                    sp.dma_start(ks[u][r, :, :].rearrange("r h s -> r (h s)"), k3).then_inc(landed, 16)

            def attention_dma(a, b):
                def load(g):
                    u = g % 2
                    n = (a * B + b) * NG + g
                    if g >= 2:
                        wait(group_done, (n - 1) * GG)
                    else:
                        wait(group_done, (a * B + b) * NG * GG)
                    parts_in(a, b, g, u, qs_in[u])
                    sp.dma_start(qs[u][SROW:SROW + 2, :, :],
                                 shift_d[a][b, :, g * HG:(g + 1) * HG]).then_inc(qs_in[u], 16)
                    sp.dma_start(vs[u][:, :, :], values_d[a][b, g]).then_inc(vs_in[u], 16)

                def store(g):
                    n = (a * B + b) * NG + g
                    wait(acc_read, 2 * n + 2)
                    sp.dma_start(num_d[a][b, g], num[g % 2][:, :]).then_inc(num_out[g % 2], 16)

                load(0)
                load(1)
                for g in range(NG):
                    if g >= 1:
                        store(g - 1)
                    if g + 1 < NG and g >= 1:
                        load(g + 1)
                store(NG - 1)

            def exact_dma(a, b):
                for g in range(NG):
                    if g >= 1:
                        wait(m_out, 16 * 2 * g)
                    parts_in(a, b, g, 0, m_in)
                    wait(m_parts, g + 1)
                    for i in range(2):
                        sp.dma_start(shift_d[a][b, i, g * HG:(g + 1) * HG].rearrange("h (t s) -> (h t) s", t=T),
                                     mxp[:, i, :]).then_inc(m_out, 16)
                wait(m_out, 16 * 2 * NG)
                for s in (m_in, m_scores, m_read, m_rows, m_turned, m_parts, m_out):
                    sp.sem_clear(s)

            def flag_of(a, b):
                wait(flag_ready, a * B + b + 1)
                return sp.value_load(flags[0:1, bass.ds(b + a * B, 1)], min_val=0, max_val=1)

            def attention_phase(a):
                with sp.Fori(0, B) as b:
                    for i in range(2):
                        wait(part_out[i], 16 * 2 * 2 * (a + 1) * B)
                        wait(vq_out[i], 16 * NG * 2 * (a + 1) * B)
                    wait(shift_out, 16 * (a + 1) * B)
                    wait(group_done, (a * B + b) * GB)
                    with sp.If(flag_of(a, b)):
                        exact_dma(a, b)
                    attention_dma(a, b)

            with sp.Fori(0, B) as b:
                wait(rows_ready, b)
                sp.dma_start(xrow[:, :, :], rows_of(x_d, b)).then_inc(x_in, 16)
                projected_out(P1, 0, b)
                after(P1, b, ("suffix", 1), ("suffix", 2))
                sp.dma_start(suffix_d[b], sfx[:, :, :]).then_inc(sfx_out, 16)
            attention_phase(0)
            for i in range(2):
                wait(num_out[i], 16 * B * NG // 2)
            wait(sfx_out, 16 * B)

            def numerators_in(a, b, j):
                n = (a * B + b) * NQ + j
                if j >= 2:
                    wait(att_ready, (a * B + b) * T + (j - 1) * TQ)
                else:
                    wait(att_ready, (a * B + b) * T)
                sp.dma_start(nt[j % 2][:, :, :],
                             num_d[a][b].rearrange("g p s -> p g s")[:, :, j * QW:(j + 1) * QW]).then_inc(nt_in[j % 2], 16)

            with sp.Fori(0, B) as b:
                wait(rows_ready, B + b)
                sp.dma_start(xrow[:, :, :], rows_of(x_d, b)).then_inc(x_in, 16)
                sp.dma_start(sh2[:, :, :], shift_d[0][b].rearrange("i h s -> h i s")).then_inc(sh2_in, 16)
                sp.dma_start(sfx[:, :, :], suffix_d[b]).then_inc(sfx_in, 16)
                for j in range(NQ):
                    numerators_in(0, b, j)
                wait(rows_ready, B + b + 1)
                sp.dma_start(x2_d[b], x2[:, :, :]).then_inc(rows_out, 16)
                sp.dma_start(xn_d[b], xnorm[:, :, :]).then_inc(rows_out, 16)
                projected_out(P2, 1, b)
            attention_phase(1)
            for i in range(2):
                wait(num_out[i], 2 * 16 * B * NG // 2)
            wait(rows_out, 32 * B)
            with sp.Fori(0, B) as b:
                wait(y_ready, b)
                sp.dma_start(xrow[:, :, :], xn_d[b]).then_inc(xn_in, 16)
                sp.dma_start(x2[:, :, :], x2_d[b]).then_inc(xn_in, 16)
                for j in range(NQ):
                    numerators_in(1, b, j)
                wait(y_ready, b + 1)
                sp.dma_start(rows_of(out_d, b), yout[:, :, :]).then_inc(y_out, 16)
            wait(y_out, 16 * B)

        @block.tensor
        def _(pe):
            pe.wait_ge(weights_in, 16 * n_weights)
            pe.wait_ge(filled, FILLS)
            pe.wait_ge(narrowed, len(NARROW))

            def start_job(jobs, b, name):
                i = jobs.bank(name)
                pe.wait_ge(side_free[i], jobs.freed(b, name))
                return side[:, i, :]

            def after(jobs, b, *names):
                for name in names:
                    pe.wait_ge(side_free[jobs.bank(name)], jobs.freed(b, name) + 1)

            def empty_job(jobs, b, name):
                bank = start_job(jobs, b, name)
                pe.transpose(bank[:, 0:P], ident[:, :], ident[:, :]).then_inc(side_done, 1)

            def transposed(bank, col, src, rows, last=False):
                if rows < P:
                    pe.sem_inc(passed[2], 1)
                ins = pe.transpose(bank[0:src.shape[1], col:col + rows], src, ident[0:rows, 0:rows])
                if last:
                    ins.then_inc(side_done, 1)

            def project(jobs, a, b, w, rows, rotated):
                n = (a * B + b) * NQ
                for j in range(NQ):
                    bank = start_job(jobs, b, ("xT", j))
                    if j == 0:
                        pe.wait_ge(rows_ready, a * B + b + 1)
                    for t in range(TQ):
                        transposed(bank, t * P, rows[:, j * TQ + t, :], P, last=(rotated is None and t == TQ - 1))
                    if rotated is not None:
                        for t in range(TQ):
                            transposed(bank, QW + t * P, rotated[:, j * TQ + t, :], P, last=(t == TQ - 1))
                    bank = start_job(jobs, b, ("qk", j))
                    after(jobs, b, ("xT", j))
                    src = xT[:, 0 if rotated is None else 1, :]
                    for c in range(2):
                        ins = pe.matmul(bank[:, c * QW:(c + 1) * QW], w[:, c, :], src, start=True, stop=True)
                    ins.then_inc(side_done, 1)
                    bank = start_job(jobs, b, ("v", j))
                    for t in range(TQ):
                        ins = pe.matmul(bank[:, t * D:(t + 1) * D], xT[:, 0, t * P:(t + 1) * P], w[:, 2, :],
                                        start=True, stop=True)
                    ins.then_inc(side_done, 1)
                    bank = start_job(jobs, b, ("norm", j))
                    pe.wait_ge(sq_ready, n + j + 1)
                    pe.matmul(bank[0:H, :], headsum[:, :], sq[:, 0:2, :].rearrange("p c s -> p (c s)"),
                              start=True, stop=True).then_inc(side_done, 1)
                    if a == 1:
                        bank = start_job(jobs, b, ("diag", j))
                        pe.matmul(bank[0:H, 0:QW], headsum[:, :], sq[:, 2, :], start=True, stop=True)\
                          .then_inc(side_done, 1)

            def gap(jobs, a, b):
                bank = start_job(jobs, b, ("gap", 0))
                pe.wait_ge(gap_ready, a * B + b + 1)
                transposed(bank, 0, gm[:, 0:1], H, last=True)

            def scores_unit(a, b, n):
                g, u = n // UG, (n // UG) % 2
                gn = (a * B + b) * UB + n
                kind, heads = unit_kind(n)
                if n % UG == 0:
                    pe.wait_ge(qs_in[u], 16 * QS_DMAS * ((a * B + b) * 2 + g // 2 + 1))
                if n >= NSC:
                    pe.wait_ge(probs_raw, gn - NSC + 1)
                else:
                    pe.wait_ge(probs_raw, (a * B + b) * UB)
                buf = scores[:, n % NSC, :, :]
                for h, c0 in heads:
                    for pieces in KINDS[kind]:
                        for kt, col, q0, w in pieces:
                            c = c0 + col
                            ins = pe.matmul(buf[:, c // 512, c % 512:c % 512 + w],
                                            ks[u][:, h, kt * P:(kt + 1) * P], qs[u][:, h, q0:q0 + w],
                                            start=True, stop=True)
                ins.then_inc(scores_ready, 1)

            def value_group(a, b, gi):
                hg, g = gi // GG, gi % GG
                u = hg % 2
                kind, pos = group_of(g)
                base = (a * B + b) * UB + hg * UG
                if g == 0:
                    pe.wait_ge(vs_in[u], 16 * ((a * B + b) * 2 + hg // 2 + 1))
                pe.wait_ge(probs_ready, base + min(4 * kind + 4, UG))
                if g < 2:
                    pe.wait_ge(acc_read, 2 * ((a * B + b) * NG + hg) - 1 + g if (hg or g) else 2 * (a * B + b) * NG)
                for kt, col, q0, w in KINDS[kind][pos]:
                    for h in range(HG):
                        if kind < 4:
                            un, c = hg * UG + 4 * kind + h, col
                        else:
                            un, c = hg * UG + 16 + h // 2, (h % 2) * 512
                        ins = pe.matmul(acc[h * VW:(h + 1) * VW, q0 // 512, q0 % 512:q0 % 512 + w],
                                        vs[u][:, kt, h * VW:(h + 1) * VW], probs[un % NPB][:, c:c + w],
                                        start=(kt == 0), stop=(kt, q0) in ((3, 384), (4, 512)), skip_group_check=True)
                ins.then_inc(group_done, 1)

            def attention(a, b):
                gi = 0
                for n in range(UB):
                    scores_unit(a, b, n)
                    if n >= PV_LAG and (n - PV_LAG) % 2 == 0:
                        value_group(a, b, gi)
                        gi += 1
                while gi < GB:
                    value_group(a, b, gi)
                    gi += 1

            def exact(a, b):
                k = 0
                for g in range(NG):
                    pe.wait_ge(m_in, 16 * M_DMAS * (g + 1))
                    for h in range(HG):
                        for t in range(T):
                            if k >= NSC:
                                pe.wait_ge(m_read, k - NSC + 1)
                            elif g == 0:
                                pe.wait_ge(probs_raw, (a * B + b) * UB)
                            w = (t + 1) * P
                            for c in range(0, w, 512):
                                cw = min(512, w - c)
                                last = c + cw == w
                                buf = scores[:, k % NSC, c // 512, :]
                                q1 = qs[0][0:KROWS, h, t * P:(t + 1) * P]
                                seen = cw - P if last else cw
                                if seen:
                                    pe.matmul(buf[:, 0:seen], q1, ks[0][0:KROWS, h, c:c + seen],
                                              start=True, stop=True)
                                if last:
                                    pe.matmul(buf[:, seen:cw], q1, ks[0][0:KROWS, h, c + seen:c + cw],
                                              start=True, stop=False)
                                    pe.matmul(buf[:, seen:cw], ident_b[:, :], hide[a][:, :], start=False,
                                              stop=True).then_inc(m_scores, 1)
                            k += 1
                    pe.wait_ge(m_rows, g + 1)
                    pe.transpose(acc[0:HG * T, 0, 0:P], mx[:, :], ident[:, :]).then_inc(m_turned, 1)

            def flag_of(a, b):
                pe.wait_ge(flag_ready, a * B + b + 1)
                return pe.value_load(flags[0:1, bass.ds(b + a * B, 1)], min_val=0, max_val=1)

            def attention_phase(a):
                with pe.Fori(0, B) as b:
                    pe.wait_ge(acc_read, 2 * (a * B + b) * NG)
                    with pe.If(flag_of(a, b)):
                        exact(a, b)
                    attention(a, b)

            def combine(jobs, a, b, w):
                for t in range(T):
                    j = t // TQ
                    bank = start_job(jobs, b, ("num", t))
                    if t % TQ == 0:
                        pe.wait_ge(nt_in[j % 2], 16 * ((a * B + b) * 2 + j // 2 + 1))
                    for g in range(NG):
                        transposed(bank, g * P, nt[j % 2][:, g, (t % TQ) * P:(t % TQ + 1) * P], P, last=(g == NG - 1))
                    bank = start_job(jobs, b, ("att", t))
                    pe.wait_ge(att_ready, (a * B + b) * T + t + 1)
                    transposed(bank, 0, att[:, :], P, last=True)
                    bank = start_job(jobs, b, ("out", t))
                    after(jobs, b, ("att", t))
                    pe.matmul(bank[:, 0:D], attT[:, :], w[:, :], start=True, stop=True).then_inc(side_done, 1)

            with pe.Fori(0, B) as b:
                project(P1, 0, b, wqkv, xnorm, None)
                for k in range(3):
                    bank = start_job(P1, b, ("suffix", k))
                    if k == 0:
                        pe.wait_ge(vsum_ready, b + 1)
                    for i, t in enumerate(range(3 * k, min(3 * k + 3, T))):
                        o = bank[:, i * 144:(i + 1) * 144]
                        ins = pe.matmul(o, later[:, :], vc[:, t, :], start=True, stop=(t == T - 1))
                        if t < T - 1:
                            ins = pe.matmul(o, ones[:, :], vsum[:, t, :], start=False, stop=True)
                    ins.then_inc(side_done, 1)
                gap(P1, 0, b)
            attention_phase(0)
            with pe.Fori(0, B) as b:
                bank = start_job(P2, b, ("em", 0))
                pe.wait_ge(em_ready, b + 1)
                for t in range(T):
                    transposed(bank, t * H, em[:, t * P:(t + 1) * P], H, last=(t == T - 1))
                empty_job(P2, b, ("pad", 0))
                combine(P2, 0, b, wr)
                project(P2, 1, b, win, xnorm, rope)
                gap(P2, 1, b)
                empty_job(P2, b, ("pad", 1))
            attention_phase(1)
            with pe.Fori(0, B) as b:
                combine(P3, 1, b, wo)
                pe.wait_ge(x1_ready, b + 1)
                for j in range(NQ):
                    bank = start_job(P3, b, ("x1T", j))
                    for t in range(TQ):
                        transposed(bank, t * P, x1[:, j * TQ + t, :], P, last=(t == TQ - 1))
                bank = start_job(P3, b, ("gate", 0))
                after(P3, b, ("x1T", 2), ("x1T", 3))
                for t in range(T):
                    ins = pe.matmul(bank[:, t * NE:(t + 1) * NE], x1T[:, t, :], wg[:, :], start=True, stop=True)
                ins.then_inc(side_done, 1)
                pe.wait_ge(G_ready, b + 1)
                for i in range(2):
                    bank = start_job(P3, b, ("GT", i))
                    for t in range(4):
                        transposed(bank, t * P, G[:, 4 * i + t, :], P, last=(t == 3))
                after(P3, b, ("GT", 0), ("GT", 1))
                for t in range(T):
                    bank = start_job(P3, b, ("bias", t))
                    pe.matmul(bank[:, 0:D], GT[:, t, :], be[:, :], start=True, stop=True).then_inc(side_done, 1)
                    for i in range(2):
                        bank = start_job(P3, b, (f"e{i}", t))
                        pe.matmul(bank, x1T[:, t, :], we[:, i * 512:(i + 1) * 512], start=True, stop=True)\
                          .then_inc(side_done, 1)
                empty_job(P3, b, ("pad", 0))

        @block.scalar
        def _(act):
            step = [0]

            def link(ins):
                step[0] += 1
                ins.then_inc(act_step, 1)
                act.wait_ge(act_step, step[0])

            def fresh():
                act.sem_clear(act_step)
                step[0] = 0

            def first_root(k):
                act.wait_ge(var_ready, k + 1)
                link(act.activation(lnv[:, :], var[:, :], ACT.Ln))
                act.activation(r0[:, :], lnv[:, :], ACT.Exp, scale=-0.5).then_inc(r0_ready, 1)

            def root(a, b):
                act.wait_ge(square_ready, a * B + b + 1)
                link(act.activation(cl[:, :], c2[:, :], ACT.Ln))
                act.activation(cc[:, :], cl[:, :], ACT.Exp, scale=0.5).then_inc(root_ready, 1)

            def attention(a, b):
                for n in range(UB):
                    gn = (a * B + b) * UB + n
                    act.wait_ge(scores_ready, gn + 1)
                    if n >= NPB:
                        m = n - NPB
                        act.wait_ge(group_done, ((a * B + b) * NG + m // UG) * GG + groups_before(unit_kind(m)[0]))
                    else:
                        act.wait_ge(group_done, (a * B + b) * GB)
                    act.activation(probs[n % NPB][:, :], scores[:, n % NSC, :, :].rearrange("p c s -> p (c s)"),
                                   ACT.Exp, scale=SCALE).then_inc(probs_raw, 1)

            with act.Fori(0, B) as b:
                fresh()
                first_root(b)
                root(0, b)
            with act.Fori(0, B) as b:
                attention(0, b)
            with act.Fori(0, B) as b:
                fresh()
                act.wait_ge(esum_ready, b + 1)
                act.activation(em[:, :], esum[:, :], ACT.Exp, scale=SCALE).then_inc(em_ready, 1)
                first_root(B + b)
                root(1, b)
            with act.Fori(0, B) as b:
                attention(1, b)
            with act.Fori(0, B) as b:
                fresh()
                first_root(2 * B + 2 * b)
                act.wait_ge(gates_shifted, b + 1)
                act.activation(ga[:, :, :], gl[:, :, :], ACT.Exp).then_inc(gates_exp, 1)
                first_root(2 * B + 2 * b + 1)

        @block.gpsimd
        def _(pool):
            def ones_of(v):
                return v[:, :, :].rearrange("p t (h v) -> p (t h) v", v=VW)[:, :, HE:HE + 1]

            fills = [(ones[:, :], 1.0), (qs[0][64:KPAD, :, :], 0.0), (qs[1][64:KPAD, :, :], 0.0),
                     (ks[0][64:KPAD, :, :], 1.0), (ks[1][64:KPAD, :, :], 1.0), (vq[0][:, :, :], 0.0),
                     (vq[1][:, :, :], 0.0), (vc[:, :, :], 1.0), (ones_of(vq[0]), 1.0), (ones_of(vq[1]), 1.0)]
            assert len(fills) == FILLS
            for i, (tile, value) in enumerate(fills):
                if i:
                    pool.wait_ge(filled, i)
                pool.memset(tile, value).then_inc(filled, 1)

            for a in range(2):
                with pool.Fori(0, B) as b:
                    for n in range(UB):
                        gn = (a * B + b) * UB + n
                        kind, _heads = unit_kind(n)
                        c0, step = DIAGONALS[kind]
                        buf = probs[n % NPB]
                        if step:
                            first = min(c0, S - 2 * step)
                            diag = buf[:, first:first + 2 * step].rearrange("p (k s) -> p k s", k=2)
                            diag = diag[:, :, c0 - first:c0 - first + P]
                        else:
                            diag = buf[:, c0:c0 + P].unsqueeze(1)
                        pool.wait_ge(probs_raw, gn + 1)
                        pool.sem_inc(passed[1], 1)
                        pool.affine_select(out=diag, in_=diag, compare_op=ALU.is_ge, fill=0.0, base=a - 1,
                                           pattern=[[0, diag.shape[1]], [1, P]], channel_multiplier=-1)\
                            .then_inc(probs_ready, 1)

        @block.vector
        def _(dve):
            step = [0]

            def link(ins):
                step[0] += 1
                ins.then_inc(dve_step, 1)
                dve.wait_ge(dve_step, step[0])

            def fresh():
                dve.sem_clear(dve_step)
                step[0] = 0

            def bank_of(jobs, b, name):
                dve.wait_ge(side_done, jobs.done(b, name))
                return side[:, jobs.bank(name), :]

            def freeing(ins, jobs, b, name):
                ins.then_inc(side_free[jobs.bank(name)], 1)
                dve.wait_ge(side_free[jobs.bank(name)], jobs.freed(b, name) + 1)

            def skip(jobs, b, name):
                bank_of(jobs, b, name)
                freeing(dve.memset(gsum[0:1, 0:1], 0.0), jobs, b, name)

            def tt(out, in0, in1, op):
                return dve.tensor_tensor(out, in0, in1, op)

            def layernorm(src, k):
                for t in range(T):
                    link(dve.bn_stats(stats[:, t, :], src[:, t, :]))
                    link(dve.bn_aggr(mv[:, t, :], stats[:, t, :]))
                dve.tensor_scalar(var[:, :], mv[:, :, 1], EPS, None, ALU.add).then_inc(var_ready, 1)
                dve.wait_ge(var_ready, k + 1)
                dve.wait_ge(r0_ready, k + 1)
                link(tt(rt[:, :], r0[:, :], r0[:, :], ALU.mult))
                link(tt(rt[:, :], rt[:, :], var[:, :], ALU.mult))
                link(dve.tensor_scalar(rt[:, :], rt[:, :], -0.5, 1.5, ALU.mult, ALU.add))
                link(tt(rstd[:, :], r0[:, :], rt[:, :], ALU.mult))

            def normalised(dst, src, t):
                return dve.tensor_scalar(dst[:, t, :], src[:, t, :], mv[:, t, 0:1], rstd[:, t:t + 1],
                                         ALU.subtract, ALU.mult)

            def over_tiles(row):
                return row[:, :].unsqueeze(1).broadcast_to([P, T, row.shape[1]])

            def project(jobs, a, b, bias, vbias):
                n = (a * B + b) * NQ
                for j in range(NQ):
                    c = slice(j * QW, (j + 1) * QW)
                    uses = (a * B + b) * 2 + j // 2
                    p = part[j % 2]
                    bank = bank_of(jobs, b, ("xT", j))
                    freeing(dve.tensor_copy(xT[:, 0:a + 1, :].rearrange("p c s -> p (c s)"), bank[:, 0:(a + 1) * QW]),
                            jobs, b, ("xT", j))
                    bank = bank_of(jobs, b, ("qk", j))
                    link(dve.tensor_scalar(qk[:, 0, :], bank[:, 0:QW], bias[:, 0:1], None, ALU.add))
                    freeing(dve.tensor_scalar(qk[:, 1, :], bank[:, QW:2 * QW], bias[:, 1:2], None, ALU.add),
                            jobs, b, ("qk", j))
                    dve.wait_ge(part_out[j % 2], 16 * 2 * uses)
                    link(dve.tensor_copy(p[:, 0, :, :], qk[:, :, :]))
                    link(tt(qkr[:, :, :], qk[:, :, :], p[:, 0, :, :], ALU.subtract))
                    link(dve.tensor_copy(p[:, 1, :, :], qkr[:, :, :]))
                    tt(p[:, 2, :, :], qkr[:, :, :], p[:, 1, :, :], ALU.subtract).then_inc(part_ready, 1)
                    if a == 1:
                        link(tt(sq[:, 2, :], qk[:, 0, :], qk[:, 1, :], ALU.mult))
                    tt(sq[:, 0:2, :], qk[:, :, :], qk[:, :, :], ALU.mult).then_inc(sq_ready, 1)
                    bank = bank_of(jobs, b, ("v", j))
                    dve.wait_ge(vq_out[j % 2], 16 * NG * uses)
                    v = vq[j % 2][:, :, :].rearrange("p t (h v) -> p t h v", v=VW)[:, :, :, 0:HE]
                    vb = vbias[:, :].rearrange("p (h f) -> p h f", f=HE).unsqueeze(1).broadcast_to([P, TQ, H, HE])
                    freeing(tt(v, bank[:, 0:TQ * D].rearrange("p (t h f) -> p t h f", t=TQ, f=HE), vb, ALU.add),
                            jobs, b, ("v", j))
                    if a == 0:
                        link(dve.tensor_copy(vc[:, j * TQ:(j + 1) * TQ, :].rearrange("p t (h f) -> p (t h) f", f=9)[:, :, 0:HE],
                                             vq[j % 2][:, :, :].rearrange("p t (h v) -> p (t h) v", v=VW)[:, :, 0:HE]))
                    bank = bank_of(jobs, b, ("norm", j))
                    freeing(dve.tensor_copy(nrm[:, 0:2, c], bank[0:H, :].rearrange("h (c s) -> h c s", c=2)),
                            jobs, b, ("norm", j))
                    if a == 1:
                        bank = bank_of(jobs, b, ("diag", j))
                        freeing(dve.tensor_copy(nrm[:, 2, c], bank[0:H, 0:QW]), jobs, b, ("diag", j))

            def bound(jobs, a, b):
                n = a * B + b
                link(dve.tensor_reduce(kmx[:, :], nrm[:, 1, :].rearrange("h (t s) -> h t s", t=T), AX.X, ALU.max))
                for t in range(1, T):
                    link(tt(kmx[:, t:t + 1], kmx[:, t:t + 1], kmx[:, t - 1:t], ALU.max))
                link(tt(c2[:, :].rearrange("h (t s) -> h t s", t=T), nrm[:, 0, :].rearrange("h (t s) -> h t s", t=T),
                        kmx[:, :].unsqueeze(2).broadcast_to([H, T, P]), ALU.mult))
                dve.tensor_scalar(c2[:, :], c2[:, :], 1e-12, None, ALU.max).then_inc(square_ready, 1)
                dve.wait_ge(square_ready, n + 1)
                link(dve.tensor_reduce(gm[:, 1:2], c2[:, :], AX.X, ALU.max))
                link(dve.tensor_scalar(gm[:, 1:2], gm[:, 1:2], 1.0 / SQUARE_LIMIT, None, ALU.mult))
                dve.wait_ge(root_ready, n + 1)
                if a == 1:
                    link(dve.scalar_tensor_tensor(out=c2[:, :], in0=cc[:, :], scalar=1.02, in1=nrm[:, 2, :],
                                                  op0=ALU.mult, op1=ALU.subtract))
                    link(dve.scalar_tensor_tensor(out=ns[:, :], in0=cc[:, :], scalar=1.02, in1=nrm[:, 2, :],
                                                  op0=ALU.mult, op1=ALU.add))
                    link(dve.tensor_scalar(ns[:, :], ns[:, :], -0.5, None, ALU.mult))
                else:
                    link(dve.tensor_scalar(c2[:, :], cc[:, :], 1.02, None, ALU.mult))
                    link(dve.tensor_scalar(ns[:, :], cc[:, :], -0.51, None, ALU.mult))
                link(dve.tensor_reduce(gm[:, 0:1], c2[:, :], AX.X, ALU.max))
                link(dve.tensor_scalar(gm[:, 0:1], gm[:, 0:1], 1.0 / LIMIT, None, ALU.mult))
                tt(gm[:, 0:1], gm[:, 0:1], gm[:, 1:2], ALU.max).then_inc(gap_ready, 1)
                dve.wait_ge(gap_ready, n + 1)
                dve.wait_ge(shift_out, 16 * n)
                link(dve.tensor_copy(shb[:, 0, :], ns[:, :]))
                tt(shb[:, 1, :], ns[:, :], shb[:, 0, :], ALU.subtract).then_inc(shift_ready, 1)
                bank = bank_of(jobs, b, ("gap", 0))
                freeing(dve.tensor_reduce(gm1[:, :], bank[0:1, 0:H], AX.X, ALU.max), jobs, b, ("gap", 0))
                dve.tensor_scalar(flags[0:1, bass.ds(b + a * B, 1)], gm1[:, :], 1.0, None, ALU.is_gt)\
                   .then_inc(flag_ready, 1)

            def exact(a, b):
                k = 0
                for g in range(NG):
                    if g >= 1:
                        dve.wait_ge(m_turned, g)
                    for h in range(HG):
                        for t in range(T):
                            dve.wait_ge(m_scores, k + 1)
                            dve.reduce_max(mx[:, h * T + t:h * T + t + 1],
                                           scores[:, k % NSC, :, :].rearrange("p c s -> p (c s)")[:, 0:(t + 1) * P],
                                           AX.X).then_inc(m_read, 1)
                            k += 1
                    dve.wait_ge(m_read, k)
                    dve.tensor_scalar(mx[:, :], mx[:, :], 0.0 if a == 0 else NEG, None, ALU.max).then_inc(m_rows, 1)
                    dve.wait_ge(m_turned, g + 1)
                    link(dve.tensor_scalar(mxn[:, :], acc[0:HG * T, 0, 0:P], -1.0, None, ALU.mult))
                    if g >= 1:
                        dve.wait_ge(m_out, 16 * 2 * g)
                    link(dve.tensor_copy(mxp[:, 0, :], mxn[:, :]))
                    tt(mxp[:, 1, :], mxn[:, :], mxp[:, 0, :], ALU.subtract).then_inc(m_parts, 1)

            def attention(a, b):
                for g in range(NG):
                    n = (a * B + b) * NG + g
                    dve.wait_ge(num_out[g % 2], 16 * ((a * B + b) * (NG // 2) + g // 2))
                    for i in range(2):
                        dve.wait_ge(group_done, n * GG + GG - 1 + i)
                        dve.tensor_copy(num[g % 2][:, i * 512:(i + 1) * 512], acc[:, i, :]).then_inc(acc_read, 1)

            def attention_phase(a):
                with dve.Fori(0, B) as b:
                    fresh()
                    dve.wait_ge(flag_ready, a * B + b + 1)
                    with dve.If(dve.value_load(flags[0:1, bass.ds(b + a * B, 1)], min_val=0, max_val=1)):
                        exact(a, b)
                    attention(a, b)

            def combine(jobs, a, b, dst):
                for t in range(T):
                    bank = bank_of(jobs, b, ("num", t))
                    nb = bank.rearrange("p (h v) -> p h v", v=VW)[:, :, 0:9]
                    if a == 0:
                        link(tt(tot[:, :, :], sfx[:, t, :].rearrange("p (h f) -> p h f", f=9),
                                emr[:, t, :].unsqueeze(2).broadcast_to([P, H, 9]), ALU.mult))
                        freeing(tt(tot[:, :, :], nb, tot[:, :, :], ALU.add), jobs, b, ("num", t))
                    else:
                        freeing(dve.tensor_copy(tot[:, :, :], nb), jobs, b, ("num", t))
                    link(dve.reciprocal(rden[:, :], tot[:, :, 8]))
                    tt(att[:, :].rearrange("p (h f) -> p h f", f=HE), tot[:, :, 0:HE],
                       rden[:, :].unsqueeze(2).broadcast_to([P, H, HE]), ALU.mult).then_inc(att_ready, 1)
                    bank = bank_of(jobs, b, ("att", t))
                    freeing(dve.tensor_copy(attT[:, :], bank[:, 0:P]), jobs, b, ("att", t))
                    bank = bank_of(jobs, b, ("out", t))
                    freeing(tt(dst[:, t, :], bank[:, 0:D], xrow[:, t, :], ALU.add), jobs, b, ("out", t))

            dve.wait_ge(weights_in, 16 * n_weights)
            dve.wait_ge(filled, FILLS)

            for t, landing, _d in NARROW:
                dve.tensor_copy(t[:, :], landing).then_inc(narrowed, 1)
            dve.wait_ge(narrowed, len(NARROW))

            with dve.Fori(0, B) as b:
                fresh()
                dve.wait_ge(x_in, 16 * (b + 1))
                layernorm(xrow, b)
                for t in range(T - 1):
                    link(normalised(xnorm, xrow, t))
                normalised(xnorm, xrow, T - 1).then_inc(rows_ready, 1)
                dve.wait_ge(rows_ready, b + 1)
                project(P1, 0, b, bqk, bv)
                link(dve.tensor_copy(vsum[:, T - 2, :], vc[:, T - 1, :]))
                for t in range(T - 3, 0, -1):
                    link(tt(vsum[:, t, :], vsum[:, t + 1, :], vc[:, t + 1, :], ALU.add))
                tt(vsum[:, 0, :], vsum[:, 1, :], vc[:, 1, :], ALU.add).then_inc(vsum_ready, 1)
                dve.wait_ge(sfx_out, 16 * b)
                for k in range(3):
                    bank = bank_of(P1, b, ("suffix", k))
                    nt_ = min(3, T - 3 * k)
                    freeing(dve.tensor_copy(sfx[:, 3 * k:3 * k + nt_, :].rearrange("p t f -> p (t f)"), bank[:, 0:nt_ * 144]),
                            P1, b, ("suffix", k))
                bound(P1, 0, b)
            attention_phase(0)
            with dve.Fori(0, B) as b:
                fresh()
                dve.wait_ge(sh2_in, 16 * (b + 1))
                tt(esum[:, :], sh2[:, 0, :], sh2[:, 1, :], ALU.add).then_inc(esum_ready, 1)
                dve.wait_ge(x_in, 16 * (B + b + 1))
                link(tt(xrow[:, :, :], xrow[:, :, :], over_tiles(br), ALU.add))
                bank = bank_of(P2, b, ("em", 0))
                freeing(dve.tensor_copy(emr[:, :, :].rearrange("p t h -> p (t h)"), bank[:, 0:P]), P2, b, ("em", 0))
                skip(P2, b, ("pad", 0))
                dve.wait_ge(sfx_in, 16 * (b + 1))
                dve.wait_ge(rows_out, 32 * b)
                combine(P2, 0, b, x2)
                layernorm(x2, B + b)
                for t in range(T):
                    link(normalised(xnorm, x2, t))
                pairs = xnorm[:, :, :].rearrange("p t (h f two) -> p t h f two", h=H, two=2)
                turned = rope[:, :, :].rearrange("p t (h f two) -> p t h f two", h=H, two=2)
                c4, s4 = (w[:, :, :].unsqueeze(2).broadcast_to([P, T, H, HE // 2]) for w in (cos, sin))
                tmp = [r.rearrange("p (t h f) -> p t h f", t=T, h=H) for r in rtmp]
                link(tt(tmp[0], pairs[:, :, :, :, 0], c4, ALU.mult))
                link(tt(tmp[1], pairs[:, :, :, :, 1], s4, ALU.mult))
                link(tt(turned[:, :, :, :, 0], tmp[0], tmp[1], ALU.subtract))
                link(tt(tmp[2], pairs[:, :, :, :, 0], s4, ALU.mult))
                link(tt(tmp[3], pairs[:, :, :, :, 1], c4, ALU.mult))
                tt(turned[:, :, :, :, 1], tmp[2], tmp[3], ALU.add).then_inc(rows_ready, 1)
                dve.wait_ge(rows_ready, B + b + 1)
                project(P2, 1, b, binqk, binv)
                bound(P2, 1, b)
                skip(P2, b, ("pad", 1))
            attention_phase(1)
            with dve.Fori(0, B) as b:
                fresh()
                dve.wait_ge(xn_in, 32 * (b + 1))
                link(tt(xrow[:, :, :], xrow[:, :, :], over_tiles(bo), ALU.add))
                combine(P3, 1, b, xnorm)
                layernorm(xnorm, 2 * B + 2 * b)
                for t in range(T):
                    link(normalised(x1, xnorm, t))
                link(tt(x1[:, :, :], x1[:, :, :], over_tiles(l1w), ALU.mult))
                tt(x1[:, :, :], x1[:, :, :], over_tiles(l1b), ALU.add).then_inc(x1_ready, 1)
                for j in range(NQ):
                    bank = bank_of(P3, b, ("x1T", j))
                    freeing(dve.tensor_copy(x1T[:, j * TQ:(j + 1) * TQ, :].rearrange("p t s -> p (t s)"), bank[:, 0:QW]),
                            P3, b, ("x1T", j))

                def wide(v):
                    return v[:, :].unsqueeze(2).broadcast_to([P, T, NE])

                bank = bank_of(P3, b, ("gate", 0))
                freeing(tt(gl[:, :, :], bank[:, 0:T * NE].rearrange("p (t e) -> p t e", e=NE), over_tiles(bg), ALU.add),
                        P3, b, ("gate", 0))
                link(dve.tensor_reduce(gsum[:, :], gl[:, :, :], AX.X, ALU.max))
                tt(gl[:, :, :], gl[:, :, :], wide(gsum), ALU.subtract).then_inc(gates_shifted, 1)
                dve.wait_ge(gates_exp, b + 1)
                link(dve.tensor_reduce(gsum[:, :], ga[:, :, :], AX.X, ALU.add))
                link(dve.reciprocal(gsum[:, :], gsum[:, :]))
                link(tt(ga[:, :, :], ga[:, :, :], wide(gsum), ALU.mult))
                link(dve.tensor_copy(gb[:, :, :], ga[:, :, :]))
                for k in range(2):
                    link(dve.tensor_reduce(gsum[:, :], gb[:, :, :], AX.X, ALU.max))
                    link(tt(G[:, :, :], gb[:, :, :], wide(gsum), ALU.is_equal))
                    link(tt(G[:, :, :], G[:, :, :], over_tiles(iota8), ALU.mult))
                    link(dve.tensor_reduce(gidx[:, :], G[:, :, :], AX.X, ALU.min))
                    one = gmask if k == 0 else G
                    link(tt(one[:, :, :], over_tiles(iota8), wide(gidx), ALU.is_equal))
                    if k == 0:
                        link(dve.scalar_tensor_tensor(out=gb[:, :, :], in0=gmask[:, :, :], scalar=-2.0,
                                                      in1=gb[:, :, :], op0=ALU.mult, op1=ALU.add))
                link(tt(gmask[:, :, :], gmask[:, :, :], G[:, :, :], ALU.add))
                tt(G[:, :, :], ga[:, :, :], gmask[:, :, :], ALU.mult).then_inc(G_ready, 1)
                dve.wait_ge(G_ready, b + 1)
                for i in range(2):
                    bank = bank_of(P3, b, ("GT", i))
                    freeing(dve.tensor_copy(GT[:, 4 * i:4 * i + 4, :].rearrange("e t s -> e (t s)"), bank[0:NE, :]),
                            P3, b, ("GT", i))
                for t in range(T):
                    bank = bank_of(P3, b, ("bias", t))
                    freeing(tt(moe[:, :], bank[:, 0:D], x1[:, t, :], ALU.add), P3, b, ("bias", t))
                    for i in range(2):
                        bank = bank_of(P3, b, (f"e{i}", t))
                        for e in range(4):
                            dst = xnorm[:, t, :] if (i, e) == (1, 3) else moe[:, :]
                            ins = dve.scalar_tensor_tensor(out=dst, in0=bank[:, e * D:(e + 1) * D],
                                                           scalar=G[:, t, 4 * i + e:4 * i + e + 1], in1=moe[:, :],
                                                           op0=ALU.mult, op1=ALU.add)
                            if e < 3:
                                link(ins)
                            else:
                                freeing(ins, P3, b, (f"e{i}", t))
                skip(P3, b, ("pad", 0))
                layernorm(xnorm, 2 * B + 2 * b + 1)
                dve.wait_ge(y_out, 16 * b)
                for t in range(T):
                    link(normalised(yout, xnorm, t))
                link(tt(yout[:, :, :], yout[:, :, :], over_tiles(l2w), ALU.mult))
                link(tt(yout[:, :, :], yout[:, :, :], over_tiles(l2b), ALU.add))
                tt(yout[:, :, :], yout[:, :, :], x2[:, :, :], ALU.add).then_inc(y_ready, 1)


def host_arrays(i):
    import numpy as np

    order = np.arange(D).reshape(NG, HG, HE).transpose(0, 2, 1).reshape(D)
    wq, bq = i["L0_attn_Wqkv"], i["L0_attn_bqkv"]
    wqkv = np.zeros((D, 3, D), wq.dtype)
    for h in range(H):
        r = slice(h * HE, (h + 1) * HE)
        for c in range(3):
            wqkv[r, c, r] = wq[:, c * HE:(c + 1) * HE]
    wqkv = np.concatenate([wqkv[:, 0:2][:, :, order], wqkv[:, 2:3]], axis=1)
    bqk = np.stack([np.tile(bq[c * HE:(c + 1) * HE], H)[order] for c in range(2)], axis=1)
    win = i["L0_ffn_in_proj_w"].T.reshape(D, 3, D)
    win = np.concatenate([win[:, 0:2][:, :, order], win[:, 2:3]], axis=1)
    binp = i["L0_ffn_in_proj_b"].reshape(3, D)
    angles = (np.arange(S, dtype=np.float32)[:, None]
              * (1.0 / 10000.0 ** (np.arange(0, HE, 2, dtype=np.float32) / HE)).astype(np.float32)[None, :])
    row, col = np.arange(P)[:, None], np.arange(P)[None, :]
    head = (np.arange(P) // (HG * HE)) * HG + np.arange(P) % HG
    return {
        "x": i["L0_attn_x"], "wqkv": wqkv, "bqk": bqk, "bv": np.tile(bq[2 * HE:], H),
        "wr": i["L0_attn_Wr"], "br": i["L0_attn_br"],
        "win": win, "binqk": np.stack([binp[0][order], binp[1][order]], axis=1), "binv": binp[2],
        "wo": i["L0_ffn_out_proj_w"].T, "bo": i["L0_ffn_out_proj_b"],
        "wg": i["L0_ffn_gate_w"].T, "bg": i["L0_ffn_gate_b"],
        "we": i["L0_ffn_expert_w"].transpose(2, 0, 1).reshape(D, NE * D), "be": i["L0_ffn_expert_b"],
        "l1w": i["L0_ffn_ln1_w"], "l1b": i["L0_ffn_ln1_b"], "l2w": i["L0_ffn_ln2_w"], "l2b": i["L0_ffn_ln2_b"],
        "cos": np.cos(angles).astype(np.float32), "sin": np.sin(angles).astype(np.float32),
        "ident": np.eye(P, dtype=np.float32),
        "hide": np.stack([np.where(col >= row, NEG, 0.0), np.where(col > row, NEG, 0.0)]).astype(np.float32),
        "later": (row >= col).astype(np.float32),
        "headsum": (head[:, None] == np.arange(H)[None, :]).astype(np.float32),
        "iota8": np.arange(NE, dtype=np.float32) - NE,
    }


def kernel(**inputs):
    import numpy as np
    import concourse.bacc as bacc
    from concourse.bass_utils import run_bass_kernel_spmd

    nc = bacc.Bacc("TRN2", target_bir_lowering=False, num_devices=1)
    arrays, args = {}, []
    for name, a in host_arrays({k: np.asarray(v) for k, v in inputs.items()}).items():
        a = np.ascontiguousarray(a)
        arrays[f"in_{name}"] = a
        args.append(nc.dram_tensor(f"in_{name}", a.shape, mybir.dt.from_np(a.dtype), kind="ExternalInput").ap())
    args.append(nc.dram_tensor("out_rows", (B, S, D), F32, kind="ExternalOutput").ap())
    build(nc, *args)
    r = run_bass_kernel_spmd(nc, [arrays], core_ids=[0])
    return r.results[0]["out_rows"]
```

```python
from contextlib import ExitStack

import concourse.bass as bass
from concourse import mybir

B, S, D, H = 4, 1024, 128, 16
HE = D // H
NE = 8
P = 128
T = S // P
TQ = 2
NQ = T // TQ
QW = TQ * P
HG = 4
NG = H // HG
VW = 32
NPART = 3
KROWS = NPART * NPART * HE
SROW = KROWS
KPAD = 96
SCALE = float(HE) ** -0.5
EPS = 1e-5
NEG = -1e30
LIMIT = 110.0 / SCALE
SQUARE_LIMIT = 1e16

KINDS = [
    [[(0, 0, 0, 512)], [(0, 512, 512, 512)]],
    [[(1, 0, 512, 512)], [(1, 512, 128, 384), (7, 896, 896, 128)]],
    [[(2, 0, 512, 512)], [(2, 512, 256, 256), (6, 768, 768, 256)]],
    [[(3, 0, 512, 512)], [(3, 512, 384, 128), (5, 640, 640, 384)]],
    [[(4, 0, 512, 512)]],
]
DIAGONALS = [(0, 0), (512, 384), (512, 256), (512, 128), (0, 512)]
UG = 18
UB = UG * NG
GG = 9
GB = GG * NG
NSC = 2
FILLS = 10
NPB = 9
PV_LAG = 5

F32 = mybir.dt.float32
BF16 = mybir.dt.bfloat16
I32 = mybir.dt.int32
ACT = mybir.ActivationFunctionType
ALU = mybir.AluOpType
AX = mybir.AxisListType


def unit_kind(n):
    u = n % UG
    if u < 16:
        return u // 4, [(u % 4, 0)]
    return 4, [(2 * (u - 16), 0), (2 * (u - 16) + 1, 512)]


def group_of(g):
    return (g // 2, g % 2) if g < 8 else (4, 0)


def groups_before(kind):
    return min(2 * kind + 2, GG)


JOB_KINDS = ("em", "num", "att", "out", "xT", "qk", "v", "norm", "ktop", "kspread", "suffix", "shift", "x1T", "gate",
             "GT", "bias", "e0", "e1", "pad")


def rests(n):
    return [("rest", i) for i in range(n)]


def projection_turns(a):
    turns = [("xT", 0)] + rests(5)
    for j in range(NQ):
        turns += [("qk", j)] + rests(1) + [("v", j)] + rests(1) + ([("xT", j + 1)] if j + 1 < NQ else [])
        turns += rests(3) + [("norm", j)] + rests(2 + a)
    return turns


def combination_turns():
    turns = []
    for t in range(T + 2):
        turns += [("num", t)] * (t < T) + rests(1) + [("att", t - 1)] * (0 <= t - 1 < T) + rests(1)
        turns += [("out", t - 2)] * (t >= 2)
    return turns


P1_TURNS = (rests(12) + [("root", 0)] + rests(8) + projection_turns(0)
            + [("ktop", 0)] + rests(5) + [("suffix", 0)] + rests(1) + [("kspread", 0)] + rests(1) + [("suffix", 1)]
            + rests(1) + [("roots", 0)] + rests(1) + [("suffix", 2)] + rests(3) + [("shift", 0)] + rests(2)
            + [("store", 0)])
P2_TURNS = (rests(8) + [("exp", 0)] + rests(5) + [("em", 0)] + rests(1) + combination_turns()
            + rests(9) + [("root", 0)] + rests(14) + projection_turns(1)
            + [("ktop", 0)] + rests(2) + [("kspread", 0)] + rests(2) + [("roots", 0)] + rests(4) + [("shift", 0)]
            + rests(2) + [("store", 0)])
P3_TURNS = (rests(14) + combination_turns() + rests(9) + [("root", 0)] + rests(11)
            + sum(([("x1T", j)] + rests(1) for j in range(NQ)), []) + rests(1) + [("gate", 0)]
            + rests(4) + [("exp", 0)] + rests(12) + [("GT", 0)] + rests(1) + [("GT", 1)] + rests(2)
            + sum(([("bias", t)] + rests(1) + [("e0", t)] + rests(2) + [("e1", t)] + rests(1) for t in range(T)), [])
            + [("pad", 0)] + rests(8) + [("root", 1)] + rests(14) + [("store", 0)])


class Jobs:

    def __init__(self, turns):
        names = [t for t in turns if t[0] in JOB_KINDS]
        assert len(names) % 2 == 0 and len(set(names)) == len(names)
        self.index = {name: i for i, name in enumerate(names)}
        self.half = len(names) // 2

    def bank(self, name):
        return self.index[name] % 2

    def done(self, half, name):
        return 2 * half + self.index[name] + 1

    def freed(self, half, name):
        return half + self.index[name] // 2

    def last_freed(self, half, names):
        last = {self.bank(n): n for n in sorted(names, key=self.index.get)}
        return [(i, self.freed(half, n) + 1) for i, n in last.items()]


def finish(work):
    for _ in work:
        pass


def turns_after(n, total):
    return min(n + 1, SPAN) * total // SPAN - min(n, SPAN) * total // SPAN


def advance(works, turns):
    for _ in range(turns):
        while works and next(works[0], DONE) is DONE:
            works.pop(0)


DONE = object()
SPAN = 62
NEXT_LOAD = 62


def build(nc, x_d, wqkv_d, bqk_d, bv_d, wr_d, br_d, win_d, binqk_d, binv_d, wo_d, bo_d, wg_d, bg_d, we_d, be_d,
          l1w_d, l1b_d, l2w_d, l2b_d, cos_d, sin_d, ident_d, hide_d, later_d, headsum_d, iota8_d, out_d):
    ctx = ExitStack()
    with ctx:
        def sb(name, shape, dt=F32):
            return ctx.enter_context(nc.sbuf_tensor(name, shape, dt))

        def sem(name):
            return ctx.enter_context(nc.semaphore(name))

        def dram(name, shape, dt=F32):
            return nc.dram_tensor(f"{name}_dram", shape, dt, kind="Internal").ap()

        parts_d = [dram(f"parts{a}", [B, 2, NPART, P, S], BF16) for a in range(2)]
        shift_d = [dram(f"shift{a}", [B, 2, H, S], BF16) for a in range(2)]
        values_d = [dram(f"values{a}", [B, NG, P, T, HG * VW]) for a in range(2)]
        num_d = [dram(f"num{a}", [B, NG, P, S]) for a in range(2)]
        suffix_d = dram("suffix", [B, P, T, H * 9])
        x2_d = dram("x2", [B, P, T, D])
        xn_d = dram("xn", [B, P, T, D])

        ident = sb("ident", [P, P])
        ident_b = sb("ident_b", [P, P], BF16)
        hide = [sb(f"hide{a}", [P, P], BF16) for a in range(2)]
        later = sb("later", [P, P])
        ones = sb("ones", [P, P])
        headsum = sb("headsum", [P, H], BF16)
        wqkv = sb("wqkv", [P, 3, P])
        bqk = sb("bqk", [P, 2])
        bv = sb("bv", [P, D])
        wr = sb("wr", [P, D])
        br = sb("br", [P, D])
        win = sb("win", [P, 3, P])
        binqk = sb("binqk", [P, 2])
        binv = sb("binv", [P, D])
        wo = sb("wo", [P, D])
        bo = sb("bo", [P, D])
        wg = sb("wg", [P, NE])
        bg = sb("bg", [P, NE])
        we = sb("we", [P, NE * D])
        be = sb("be", [NE, D])
        l1w = sb("l1w", [P, D])
        l1b = sb("l1b", [P, D])
        l2w = sb("l2w", [P, D])
        l2b = sb("l2b", [P, D])
        cos = sb("cos", [P, T, HE // 2])
        sin = sb("sin", [P, T, HE // 2])
        iota8 = sb("iota8", [P, NE])

        qs = [sb(f"qs{i}", [KPAD, HG, S], BF16) for i in range(2)]
        ks = [sb(f"ks{i}", [KPAD, HG, S], BF16) for i in range(2)]
        vs = [sb(f"vs{i}", [P, T, HG * VW]) for i in range(2)]
        probs = [sb(f"probs{i}", [P, S]) for i in range(NPB)]
        num = [sb(f"num{i}", [P, S]) for i in range(2)]
        mx = sb("mx", [P, HG * T])
        mxn = sb("mxn", [HG * T, P])
        mxr = sb("mxr", [HG * T, P])
        mxp = sb("mxp", [HG * T, 2, P], BF16)

        xrow = sb("xrow", [P, T, D])
        xnorm = sb("xnorm", [P, T, D])
        rope = sb("rope", [P, T, D])
        stats = sb("stats", [P, T, 6])
        mv = sb("mv", [P, T, 2])
        var = sb("var", [P, T])
        lnv = sb("lnv", [P, T])
        r0 = sb("r0", [P, T])
        rt = sb("rt", [P, T])
        rstd = sb("rstd", [P, T])
        xT = sb("xT", [P, 2, QW])
        qk = sb("qk", [P, 2, QW])
        qkr = sb("qkr", [P, 2, QW])
        part = [sb(f"part{i}", [P, NPART, 2, QW], BF16) for i in range(2)]
        sq = sb("sq", [P, 3, QW], BF16)
        nrm = sb("nrm", [P, 3, H, T])
        ktop = sb("ktop", [P, H, T])
        kmx = sb("kmx", [P, 1])
        kdiag = sb("kdiag", [P, P])
        c2 = sb("c2", [P, H, T])
        cl = sb("cl", [P, H, T])
        cc = sb("cc", [P, H, T])
        ns = sb("ns", [P, H, T])
        gm = sb("gm", [P, 2])
        gm1 = sb("gm1", [1, 1])
        shb = sb("shb", [P, 2, P], BF16)
        flags = sb("flags", [1, 2 * B], I32)
        vq = [sb(f"vq{i}", [P, TQ, H * VW]) for i in range(2)]
        vc = sb("vc", [P, T, H * 9])
        vsum = sb("vsum", [P, T, H * 9])
        sfx = sb("sfx", [P, T, H * 9])
        sh2 = sb("sh2", [P, 2, P], BF16)
        esum = sb("esum", [P, P])
        em = sb("em", [P, P])
        emr = sb("emr", [P, H, T])
        nt = [sb(f"nt{i}", [P, NG, QW]) for i in range(2)]
        tot = sb("tot", [P, 2, H, 9])
        rden = sb("rden", [P, 2, H])
        att = sb("att", [P, 2, D])
        attT = sb("attT", [P, 2, D])
        x2 = sb("x2s", [P, T, D])
        x1 = sb("x1", [P, T, D])
        x1T = rope
        gl = sb("gl", [P, T, NE])
        ga = sb("ga", [P, T, NE])
        gb = sb("gb", [P, T, NE])
        gmask = sb("gmask", [P, T, NE])
        gidx = sb("gidx", [P, T])
        gsum = sb("gsum", [P, T])
        G = sb("G", [P, T, NE])
        GT = sb("GT", [NE, T, P])
        moe = sb("moe", [P, D])
        yout = sb("yout", [P, T, D])
        rtmp = [w[:, 4 * i:4 * i + 4, :].rearrange("p t d -> p (t d)") for w in (yout, x1) for i in range(2)]

        scores = ctx.enter_context(nc.psum_tensor("scores", [P, NSC, 2, 512], F32))
        acc = ctx.enter_context(nc.psum_tensor("acc", [P, 2, 512], F32))
        side = ctx.enter_context(nc.psum_tensor("side", [P, 2, 512], F32))

        first_weights_in = sem("first_weights_in")
        weights_in = sem("weights_in")
        filled = sem("filled")
        narrowed = sem("narrowed")
        passed = [sem(f"passed_{e}") for e in ("sync", "pool", "tensor")]
        dve_step = sem("dve_step")
        act_step = sem("act_step")
        side_done = sem("side_done")
        side_free = [sem(f"side_free{i}") for i in range(2)]
        x_in = [sem(f"x_in{i}") for i in range(2)]
        var_ready = [sem(f"var_ready{i}") for i in range(3)]
        r0_ready = [sem(f"r0_ready{i}") for i in range(3)]
        rows_ready = [sem(f"rows_ready{i}") for i in range(2)]
        part_ready = sem("part_ready")
        part_out = [sem(f"part_out{i}") for i in range(2)]
        sq_ready = sem("sq_ready")
        vq_out = [sem(f"vq_out{i}") for i in range(2)]
        square_ready = sem("square_ready")
        root_ready = sem("root_ready")
        keys_spread = sem("keys_spread")
        gap_ready = sem("gap_ready")
        shift_ready = sem("shift_ready")
        shift_out = sem("shift_out")
        flag_ready = sem("flag_ready")
        vsum_ready = sem("vsum_ready")
        sfx_out = sem("sfx_out")
        qs_in = [sem(f"qs_in{i}") for i in range(2)]
        vs_in = [sem(f"vs_in{i}") for i in range(2)]
        scores_ready = sem("scores_ready")
        probs_raw = sem("probs_raw")
        probs_ready = sem("probs_ready")
        group_done = sem("group_done")
        acc_read = sem("acc_read")
        num_out = [sem(f"num_out{i}") for i in range(2)]
        m_in = sem("m_in")
        m_scores = sem("m_scores")
        m_read = sem("m_read")
        m_rows = sem("m_rows")
        m_turned = sem("m_turned")
        m_parts = sem("m_parts")
        m_out = sem("m_out")
        m_restored = sem("m_restored")
        sh2_in = sem("sh2_in")
        sfx_in = sem("sfx_in")
        nt_in = [sem(f"nt_in{i}") for i in range(2)]
        xn_in = sem("xn_in")
        esum_ready = sem("esum_ready")
        em_ready = sem("em_ready")
        att_ready = [sem(f"att_ready{i}") for i in range(2)]
        rows_out = sem("rows_out")
        x1_ready = sem("x1_ready")
        gates_shifted = sem("gates_shifted")
        gates_exp = sem("gates_exp")
        G_ready = sem("G_ready")
        y_ready = sem("y_ready")
        y_out = sem("y_out")

        RAISED = [rows_ready[1], rows_out, y_ready, y_out, att_ready[0], att_ready[1]]

        P1, P2, P3 = Jobs(P1_TURNS), Jobs(P2_TURNS), Jobs(P3_TURNS)

        pair = P1.half + P2.half

        def p1_at(b, s=None):
            return (b, b * P1.half) if s is None else (2 * s + 2, 2 * P1.half + s * pair)

        def p2_at(b, s=None):
            return (b + 4, 4 * P1.half + b * P2.half) if s is None else (2 * s + 3, 3 * P1.half + s * pair)

        def p3_at(b):
            return 4 * P1.half + 4 * P2.half + b * P3.half

        def kept_at(a, b):
            return {(0, 0): 0, (0, 3): 4, (1, 0): 3}[a, b]

        NARROW = [(ident_b, xnorm[:, 0, :], ident_d), (hide[0], xnorm[:, 1, :], hide_d[0]),
                  (hide[1], xnorm[:, 2, :], hide_d[1]), (headsum, xnorm[:, 3, 0:H], headsum_d)]
        FIRST = [(ident, ident_d), (wqkv, wqkv_d), (bqk, bqk_d), (later, later_d)]
        WEIGHTS = [(wr, wr_d), (win, win_d), (binqk, binqk_d), (wo, wo_d), (wg, wg_d), (we, we_d), (be, be_d)]
        ROWS = [(binv, binv_d), (br, br_d), (bo, bo_d), (bg, bg_d), (l1w, l1w_d), (l1b, l1b_d),
                (l2w, l2w_d), (l2b, l2b_d), (iota8, iota8_d)]
        n_first = len(FIRST) + len(NARROW) + 1
        n_weights = len(WEIGHTS) + len(ROWS) + 2
        QS_DMAS = 2 * NPART + 1
        M_DMAS = 2 * NPART

        block = ctx.enter_context(nc.Block())

        @block.sync
        def _(sp):
            def wait(semaphore, value):
                sp.wait_ge(semaphore, value)
                sp.sem_inc(passed[0], 1)

            def bc(ap):
                return ap.unsqueeze(0).broadcast_to([P, ap.shape[0]])

            def rows_of(dst, b):
                return dst[b].rearrange("(t p) d -> p t d", p=P)

            def after(jobs, half, *names):
                for i, v in jobs.last_freed(half, names):
                    wait(side_free[i], v)

            def projected_out(jobs, a, b, k, half, j):
                wait(part_ready, k * NQ + j + 1)
                for c in range(2):
                    sp.dma_start(parts_d[a][b, c].rearrange("i p s -> p i s")[:, :, j * QW:(j + 1) * QW],
                                 part[j % 2][:, :, c, :]).then_inc(part_out[j % 2], 16)
                after(jobs, half, ("v", j))
                for g in range(NG):
                    sp.dma_start(values_d[a][b, g][:, j * TQ:(j + 1) * TQ, :],
                                 vq[j % 2][:, :, g * HG * VW:(g + 1) * HG * VW]).then_inc(vq_out[j % 2], 16)

            def shift_store(a, b, k):
                wait(shift_ready, k + 1)
                sp.dma_start(shift_d[a][b].rearrange("i h (t s) -> (h t) i s", s=P), shb[:, :, :]).then_inc(shift_out, 16)

            def p1(b, k, half):
                sp.dma_start(xrow[:, :, :], rows_of(x_d, b)).then_inc(x_in[0], 16)
                for turn, j in P1_TURNS:
                    if turn == "norm":
                        projected_out(P1, 0, b, k, half, j)
                    if turn == "shift":
                        after(P1, half, ("suffix", 1), ("suffix", 2))
                        sp.dma_start(suffix_d[b], sfx[:, :, :]).then_inc(sfx_out, 16)
                    if turn == "store":
                        shift_store(0, b, k)
                    yield

            def numerators_in(a, b, j):
                wait(att_ready[a], 1 + (b * T + (j - 1) * TQ if j >= 2 else b * T))
                sp.dma_start(nt[j % 2][:, :, :],
                             num_d[a][b].rearrange("g p s -> p g s")[:, :, j * QW:(j + 1) * QW]).then_inc(nt_in[j % 2], 16)

            def p2(b, k, half, p1s):
                sp.dma_start(sh2[:, :, :], shift_d[0][b].rearrange("i h (t s) -> (h t) i s", s=P)).then_inc(sh2_in, 16)
                for i in range(2):
                    wait(num_out[i], 16 * 2 * (b + 1))
                numerators_in(0, b, 0)
                wait(sfx_out, 16 * p1s)
                sp.dma_start(sfx[:, :, :], suffix_d[b]).then_inc(sfx_in, 16)
                wait(rows_ready[0], p1s)
                sp.dma_start(xrow[:, :, :], rows_of(x_d, b)).then_inc(x_in[1], 16)
                numerators_in(0, b, 1)
                for turn, j in P2_TURNS:
                    if turn == "att" and j % 2 and j // 2 + 2 < NQ:
                        numerators_in(0, b, j // 2 + 2)
                    if (turn, j) == ("xT", 0):
                        wait(rows_ready[1], b + 2)
                        sp.dma_start(x2_d[b], x2[:, :, :]).then_inc(rows_out, 16)
                        sp.dma_start(xn_d[b], xnorm[:, :, :]).then_inc(rows_out, 16)
                    if turn == "norm":
                        projected_out(P2, 1, b, k, half, j)
                    if turn == "store":
                        shift_store(1, b, k)
                    yield

            def p3(b):
                for i in range(2):
                    wait(num_out[i], 16 * 2 * (B + b + 1))
                numerators_in(1, b, 0)
                wait(y_ready, b + 1)
                sp.dma_start(xrow[:, :, :], xn_d[b]).then_inc(xn_in, 16)
                sp.dma_start(x2[:, :, :], x2_d[b]).then_inc(xn_in, 16)
                numerators_in(1, b, 1)
                for turn, j in P3_TURNS:
                    if turn == "att" and j % 2 and j // 2 + 2 < NQ:
                        numerators_in(1, b, j // 2 + 2)
                    if turn == "store":
                        wait(y_ready, b + 2)
                        sp.dma_start(rows_of(out_d, b), yout[:, :, :]).then_inc(y_out, 16)
                    yield

            def parts_in(a, b, g, u, landed):
                heads = slice(g * HG * HE, (g + 1) * HG * HE)
                for i in range(NPART):
                    r = slice(i * NPART * HE, (i + 1) * NPART * HE)
                    q1 = parts_d[a][b, 0, i, heads].rearrange("(e h) s -> e (h s)", e=HE)
                    k3 = parts_d[a][b, 1, :, heads].rearrange("j (e h) s -> j e (h s)", e=HE)
                    sp.dma_start(qs[u][r, :, :].rearrange("r h s -> r (h s)"),
                                 q1.unsqueeze(0).broadcast_to([NPART, HE, HG * S])).then_inc(landed, 16)
                    sp.dma_start(ks[u][r, :, :].rearrange("r h s -> r (h s)"), k3).then_inc(landed, 16)

            def shift_in(a, b, g, u, landed):
                sp.dma_start(qs[u][SROW:SROW + 2, :, :],
                             shift_d[a][b, :, g * HG:(g + 1) * HG]).then_inc(landed, 16)

            def load(a, b, g):
                u = g % 2
                if g >= 2 or not isinstance(b, int) or a * B + b > 0:
                    wait(group_done, ((a * B + b) * NG + g - 1) * GG)
                parts_in(a, b, g, u, qs_in[u])
                shift_in(a, b, g, u, qs_in[u])
                sp.dma_start(vs[u][:, :, :], values_d[a][b, g]).then_inc(vs_in[u], 16)

            def first_load(a, b, k):
                for i in range(2):
                    wait(part_out[i], 16 * 4 * (k + 1))
                    wait(vq_out[i], 16 * 2 * NG * (k + 1))
                wait(shift_out, 16 * (k + 1))
                load(a, b, 0)

            def exact(a, b):
                for i in range(2):
                    wait(qs_in[i], 16 * QS_DMAS * 2 * (a * B + b) + (0 if i else 16 * QS_DMAS))
                for g in range(NG):
                    parts_in(a, b, g, 0, m_in)
                    wait(m_parts, g + 1)
                    for i in range(2):
                        sp.dma_start(shift_d[a][b, i, g * HG:(g + 1) * HG].rearrange("h (t s) -> (h t) s", t=T),
                                     mxp[:, i, :]).then_inc(m_out, 16)
                    wait(m_out, 16 * 2 * (g + 1))
                parts_in(a, b, 0, 0, m_in)
                shift_in(a, b, 0, 0, m_in)
                wait(m_restored, 1)
                for s in (m_in, m_scores, m_read, m_rows, m_turned, m_parts, m_out, m_restored):
                    sp.sem_clear(s)

            def store(a, b, g):
                wait(acc_read, 2 * ((a * B + b) * NG + g) + 2)
                sp.dma_start(num_d[a][b, g], num[g % 2][:, :]).then_inc(num_out[g % 2], 16)

            def slot(a, b, k, following, sides, total):
                wait(flag_ready, k + 1)
                with sp.If(sp.value_load(flags[0:1, bass.ds(k, 1)], min_val=0, max_val=1)):
                    exact(a, b)
                for n in range(UB):
                    g, u = n // UG, n % UG
                    if n == 1:
                        load(a, b, 1)
                    if g >= 1 and u == PV_LAG and g + 1 < NG:
                        load(a, b, g + 1)
                    if g >= 1 and u == PV_LAG + 3:
                        store(a, b, g - 1)
                    advance(sides, turns_after(n, total))
                    if n == NEXT_LOAD and following is not None:
                        first_load(*following)
                for w in sides:
                    finish(w)
                store(a, b, NG - 1)

            sp.wait_ge(filled, FILLS)
            head = p1(0, *p1_at(0))
            next(head)
            for _t, landing, d in NARROW:
                sp.dma_start(landing, d).then_inc(first_weights_in, 16)
            for t, d in FIRST:
                sp.dma_start(t[:], d).then_inc(first_weights_in, 16)
            sp.dma_start(bv[:, :], bc(bv_d)).then_inc(first_weights_in, 16)
            finish(head)
            first_load(0, 0, 0)
            wait(rows_ready[0], 1)
            slot(0, 0, 0, (0, 1, 1), [p1(1, *p1_at(1))], len(P1_TURNS))
            with sp.Fori(0, 2) as s:
                wait(rows_ready[0], s + 2)
                wait(rows_ready[1], s + 1)
                slot(0, s + 1, s + 1, (0, s + 2, 2 * s + 2), [p1(s + 2, *p1_at(0, s)), p2(s, *p2_at(0, s), s + 3)],
                     len(P1_TURNS) + len(P2_TURNS))
            slot(0, 3, 4, (1, 0, 3), [p2(2, *p2_at(2), B)], len(P2_TURNS))
            slot(1, 0, 3, (1, 1, 5), [p2(3, *p2_at(3), B)], len(P2_TURNS))
            with sp.Fori(0, 2) as s:
                slot(1, s + 1, s + 5, (1, s + 2, s + 6), [p3(s)], len(P3_TURNS))
            slot(1, 3, 7, None, [p3(2)], len(P3_TURNS))
            finish(p3(3))
            wait(y_out, 16 * B + 1)

        @block.tensor
        def _(pe):
            pe.wait_ge(first_weights_in, 16 * n_first)
            pe.wait_ge(filled, FILLS)
            pe.wait_ge(narrowed, len(NARROW))

            def start_job(jobs, half, name):
                i = jobs.bank(name)
                pe.wait_ge(side_free[i], jobs.freed(half, name))
                return side[:, i, :]

            def after(jobs, half, *names):
                for i, v in jobs.last_freed(half, names):
                    pe.wait_ge(side_free[i], v)

            def transposed(bank, col, src, rows, last=False):
                if rows < P:
                    pe.sem_inc(passed[2], 1)
                ins = pe.transpose(bank[0:src.shape[1], col:col + rows], src, ident[0:rows, 0:rows])
                if last:
                    ins.then_inc(side_done, 1)

            def project(jobs, a, b, k, half, w, rotated, turn, j):
                if turn == "xT":
                    bank = start_job(jobs, half, ("xT", j))
                    if j == 0:
                        pe.wait_ge(rows_ready[a], b + 1 + a)
                    for t in range(TQ):
                        transposed(bank, t * P, xnorm[:, j * TQ + t, :], P, last=(rotated is None and t == TQ - 1))
                    if rotated is not None:
                        for t in range(TQ):
                            transposed(bank, QW + t * P, rotated[:, j * TQ + t, :], P, last=(t == TQ - 1))
                if turn == "qk":
                    bank = start_job(jobs, half, ("qk", j))
                    after(jobs, half, ("xT", j))
                    src = xT[:, 0 if rotated is None else 1, :]
                    for c in range(2):
                        ins = pe.matmul(bank[:, c * QW:(c + 1) * QW], w[:, c, :], src, start=True, stop=True)
                    ins.then_inc(side_done, 1)
                if turn == "v":
                    bank = start_job(jobs, half, ("v", j))
                    for t in range(TQ):
                        ins = pe.matmul(bank[:, t * D:(t + 1) * D], xT[:, 0, t * P:(t + 1) * P], w[:, 2, :],
                                        start=True, stop=True)
                    ins.then_inc(side_done, 1)
                if turn == "norm":
                    bank = start_job(jobs, half, ("norm", j))
                    pe.wait_ge(sq_ready, k * NQ + j + 1)
                    for c in range(2 + a):
                        for t in range(TQ):
                            col = (c * TQ + t) * H
                            ins = pe.matmul(bank[:, col:col + H], sq[:, c, t * P:(t + 1) * P], headsum[:, :],
                                            start=True, stop=True)
                    ins.then_inc(side_done, 1)
                if turn == "ktop":
                    bank = start_job(jobs, half, ("ktop", 0))
                    after(jobs, half, ("norm", NQ - 1))
                    transposed(bank, 0, nrm[:, 1, :, :].rearrange("p h t -> p (h t)"), P, last=True)
                if turn == "kspread":
                    bank = start_job(jobs, half, ("kspread", 0))
                    pe.wait_ge(keys_spread, k + 1)
                    pe.matmul(bank[:, 0:P], ones[:, :], kdiag[:, :], start=True, stop=True).then_inc(side_done, 1)
                if turn == "shift":
                    bank = start_job(jobs, half, ("shift", 0))
                    pe.wait_ge(gap_ready, k + 1)
                    transposed(bank, P, gm[:, 0:1], P)
                    transposed(bank, 0, ns[:, :, :].rearrange("p h t -> p (h t)"), P, last=True)

            def combine(jobs, a, b, half, w, turn, t):
                if turn == "num":
                    j = t // TQ
                    bank = start_job(jobs, half, ("num", t))
                    if t % TQ == 0:
                        pe.wait_ge(nt_in[j % 2], 16 * ((a * B + b) * 2 + j // 2 + 1))
                    for g in range(NG):
                        transposed(bank, g * P, nt[j % 2][:, g, (t % TQ) * P:(t % TQ + 1) * P], P, last=(g == NG - 1))
                if turn == "att":
                    bank = start_job(jobs, half, ("att", t))
                    pe.wait_ge(att_ready[a], b * T + t + 2)
                    transposed(bank, 0, att[:, t % 2, :], P, last=True)
                if turn == "out":
                    bank = start_job(jobs, half, ("out", t))
                    after(jobs, half, ("att", t))
                    pe.matmul(bank[:, 0:D], attT[:, t % 2, :], w[:, :], start=True, stop=True).then_inc(side_done, 1)

            def p1(b, k, half):
                for turn, i in P1_TURNS:
                    project(P1, 0, b, k, half, wqkv, None, turn, i)
                    if turn == "suffix":
                        bank = start_job(P1, half, ("suffix", i))
                        if i == 0:
                            pe.wait_ge(vsum_ready, b + 1)
                        for c, t in enumerate(range(3 * i, min(3 * i + 3, T))):
                            o = bank[:, c * 144:(c + 1) * 144]
                            ins = pe.matmul(o, later[:, :], vc[:, t, :], start=True, stop=(t == T - 1))
                            if t < T - 1:
                                ins = pe.matmul(o, ones[:, :], vsum[:, t, :], start=False, stop=True)
                        ins.then_inc(side_done, 1)
                    yield

            def p2(b, k, half):
                for turn, i in P2_TURNS:
                    if turn == "em":
                        bank = start_job(P2, half, ("em", 0))
                        pe.wait_ge(em_ready, b + 1)
                        transposed(bank, 0, em[:, :], P, last=True)
                    combine(P2, 0, b, half, wr, turn, i)
                    project(P2, 1, b, k, half, win, rope, turn, i)
                    yield

            def p3(b, half):
                for turn, i in P3_TURNS:
                    combine(P3, 1, b, half, wo, turn, i)
                    if turn == "x1T":
                        bank = start_job(P3, half, ("x1T", i))
                        if i == 0:
                            pe.wait_ge(x1_ready, b + 1)
                        for t in range(TQ):
                            transposed(bank, t * P, x1[:, i * TQ + t, :], P, last=(t == TQ - 1))
                    if turn == "gate":
                        bank = start_job(P3, half, ("gate", 0))
                        after(P3, half, ("x1T", 2), ("x1T", 3))
                        for t in range(T):
                            ins = pe.matmul(bank[:, t * NE:(t + 1) * NE], x1T[:, t, :], wg[:, :], start=True, stop=True)
                        ins.then_inc(side_done, 1)
                    if turn == "GT":
                        bank = start_job(P3, half, ("GT", i))
                        if i == 0:
                            pe.wait_ge(G_ready, b + 1)
                        for t in range(4):
                            transposed(bank, t * P, G[:, 4 * i + t, :], P, last=(t == 3))
                    if turn == "bias":
                        if i == 0:
                            after(P3, half, ("GT", 0), ("GT", 1))
                        bank = start_job(P3, half, ("bias", i))
                        pe.matmul(bank[:, 0:D], GT[:, i, :], be[:, :], start=True, stop=True).then_inc(side_done, 1)
                    if turn in ("e0", "e1"):
                        bank = start_job(P3, half, (turn, i))
                        first = 512 * int(turn[1])
                        pe.matmul(bank, x1T[:, i, :], we[:, first:first + 512], start=True, stop=True)\
                          .then_inc(side_done, 1)
                    if turn == "pad":
                        bank = start_job(P3, half, ("pad", 0))
                        pe.transpose(bank[:, 0:P], ident[:, :], ident[:, :]).then_inc(side_done, 1)
                    yield

            def scores_unit(a, b, n):
                g, u = n // UG, (n // UG) % 2
                gn = (a * B + b) * UB + n
                kind, heads = unit_kind(n)
                if n % UG == 0:
                    pe.wait_ge(qs_in[u], 16 * QS_DMAS * ((a * B + b) * 2 + g // 2 + 1))
                if n >= NSC:
                    pe.wait_ge(probs_raw, gn - NSC + 1)
                else:
                    pe.wait_ge(probs_raw, (a * B + b) * UB)
                buf = scores[:, n % NSC, :, :]
                for h, c0 in heads:
                    for pieces in KINDS[kind]:
                        for kt, col, q0, w in pieces:
                            c = c0 + col
                            ins = pe.matmul(buf[:, c // 512, c % 512:c % 512 + w],
                                            ks[u][:, h, kt * P:(kt + 1) * P], qs[u][:, h, q0:q0 + w],
                                            start=True, stop=True)
                ins.then_inc(scores_ready, 1)

            def value_group(a, b, gi):
                hg, g = gi // GG, gi % GG
                u = hg % 2
                kind, pos = group_of(g)
                base = (a * B + b) * UB + hg * UG
                if g == 0:
                    pe.wait_ge(vs_in[u], 16 * ((a * B + b) * 2 + hg // 2 + 1))
                pe.wait_ge(probs_ready, base + min(4 * kind + 4, UG))
                if g < 2:
                    pe.wait_ge(acc_read, 2 * ((a * B + b) * NG + hg) - 1 + g if (hg or g) else 2 * (a * B + b) * NG)
                for kt, col, q0, w in KINDS[kind][pos]:
                    for h in range(HG):
                        if kind < 4:
                            un, c = hg * UG + 4 * kind + h, col
                        else:
                            un, c = hg * UG + 16 + h // 2, (h % 2) * 512
                        ins = pe.matmul(acc[h * VW:(h + 1) * VW, q0 // 512, q0 % 512:q0 % 512 + w],
                                        vs[u][:, kt, h * VW:(h + 1) * VW], probs[un % NPB][:, c:c + w],
                                        start=(kt == 0), stop=(kt, q0) in ((3, 384), (4, 512)),
                                        skip_group_check=True)
                ins.then_inc(group_done, 1)

            def exact(a, b):
                i = 0
                for g in range(NG):
                    pe.wait_ge(m_in, 16 * M_DMAS * (g + 1))
                    for h in range(HG):
                        for t in range(T):
                            if i >= NSC:
                                pe.wait_ge(m_read, i - NSC + 1)
                            elif g == 0 and (b if isinstance(b, int) else 1):
                                pe.wait_ge(probs_raw, (a * B + b) * UB)
                                pe.wait_ge(acc_read, 2 * (a * B + b) * NG)
                            w = (t + 1) * P
                            for c in range(0, w, 512):
                                cw = min(512, w - c)
                                last = c + cw == w
                                buf = scores[:, i % NSC, c // 512, :]
                                q1 = qs[0][0:KROWS, h, t * P:(t + 1) * P]
                                seen = cw - P if last else cw
                                if seen:
                                    pe.matmul(buf[:, 0:seen], q1, ks[0][0:KROWS, h, c:c + seen],
                                              start=True, stop=True)
                                if last:
                                    pe.matmul(buf[:, seen:cw], q1, ks[0][0:KROWS, h, c + seen:c + cw],
                                              start=True, stop=False)
                                    pe.matmul(buf[:, seen:cw], ident_b[:, :], hide[a][:, :], start=False,
                                              stop=True).then_inc(m_scores, 1)
                            i += 1
                    pe.wait_ge(m_rows, g + 1)
                    pe.transpose(acc[0:HG * T, 0, 0:P], mx[:, :], ident[:, :]).then_inc(m_turned, 1)
                pe.wait_ge(m_in, 16 * (M_DMAS * (NG + 1) + 1))
                pe.sem_inc(m_restored, 1)

            def slot(a, b, k, sides, total):
                pe.wait_ge(flag_ready, k + 1)
                with pe.If(pe.value_load(flags[0:1, bass.ds(k, 1)], min_val=0, max_val=1)):
                    exact(a, b)
                for n in range(UB):
                    scores_unit(a, b, n)
                    if n >= PV_LAG and (n - PV_LAG) % 2 == 0:
                        value_group(a, b, (n - PV_LAG) // 2)
                    advance(sides, turns_after(n, total))
                for gi in range((UB - 1 - PV_LAG) // 2 + 1, GB):
                    value_group(a, b, gi)
                for w in sides:
                    finish(w)

            finish(p1(0, *p1_at(0)))
            pe.wait_ge(weights_in, 16 * n_weights)
            slot(0, 0, 0, [p1(1, *p1_at(1))], len(P1_TURNS))
            with pe.Fori(0, 2) as s:
                slot(0, s + 1, s + 1, [p1(s + 2, *p1_at(0, s)), p2(s, *p2_at(0, s))], len(P1_TURNS) + len(P2_TURNS))
            slot(0, 3, 4, [p2(2, *p2_at(2))], len(P2_TURNS))
            slot(1, 0, 3, [p2(3, *p2_at(3))], len(P2_TURNS))
            with pe.Fori(0, 3) as s:
                slot(1, s + 1, s + 5, [p3(s, p3_at(s))], len(P3_TURNS))
            finish(p3(3, p3_at(3)))

        @block.scalar
        def _(act):
            step = [0]

            def link(ins):
                step[0] += 1
                ins.then_inc(act_step, 1)
                act.wait_ge(act_step, step[0])

            def fresh():
                act.sem_clear(act_step)
                step[0] = 0

            def copied(jobs, half, name, dst, cols, rows=P):
                act.wait_ge(side_done, jobs.done(half, name))
                i = jobs.bank(name)
                act.activation(dst, side[0:rows, i, 0:cols], ACT.Copy).then_inc(side_free[i], 1)

            def first_root(phase, n):
                act.wait_ge(var_ready[phase], n + 1)
                link(act.activation(lnv[:, :], var[:, :], ACT.Ln))
                act.activation(r0[:, :], lnv[:, :], ACT.Exp, scale=-0.5).then_inc(r0_ready[phase], 1)

            def project(jobs, a, k, half, turn, j):
                if turn == "xT":
                    copied(jobs, half, ("xT", j), xT[:, 0:a + 1, :].rearrange("p c s -> p (c s)"), (a + 1) * QW)
                if turn == "roots":
                    act.wait_ge(square_ready, k + 1)
                    link(act.activation(cl[:, :, :], c2[:, :, :], ACT.Ln))
                    act.activation(cc[:, :, :], cl[:, :, :], ACT.Exp, scale=0.5).then_inc(root_ready, 1)

            def p1(b, k, half):
                fresh()
                for turn, j in P1_TURNS:
                    if turn == "root":
                        first_root(0, b)
                    project(P1, 0, k, half, turn, j)
                    yield

            def p2(b, k, half):
                fresh()
                for turn, j in P2_TURNS:
                    if turn == "exp":
                        act.wait_ge(esum_ready, b + 1)
                        act.activation(em[:, :], esum[:, :], ACT.Exp, scale=SCALE).then_inc(em_ready, 1)
                    if turn == "root":
                        first_root(1, b)
                    project(P2, 1, k, half, turn, j)
                    yield

            def p3(b, half):
                fresh()
                for turn, i in P3_TURNS:
                    if turn == "root":
                        first_root(2, 2 * b + i)
                    if turn == "exp":
                        act.wait_ge(gates_shifted, b + 1)
                        act.activation(ga[:, :, :], gl[:, :, :], ACT.Exp).then_inc(gates_exp, 1)
                    yield

            def sums_out(a, b, h):
                g, i = h // 2, h % 2
                n = (a * B + b) * NG + g
                if i == 0:
                    act.wait_ge(num_out[g % 2], 16 * ((a * B + b) * (NG // 2) + g // 2))
                act.wait_ge(group_done, n * GG + GG - 1 + i)
                act.activation(num[g % 2][:, i * 512:(i + 1) * 512], acc[:, i, :], ACT.Copy).then_inc(acc_read, 1)

            def slot(a, b, sides, total):
                for n in range(UB):
                    gn = (a * B + b) * UB + n
                    act.wait_ge(scores_ready, gn + 1)
                    if n >= NPB:
                        m = n - NPB
                        act.wait_ge(group_done, ((a * B + b) * NG + m // UG) * GG + groups_before(unit_kind(m)[0]))
                    else:
                        act.wait_ge(group_done, (a * B + b) * GB)
                    act.activation(probs[n % NPB][:, :], scores[:, n % NSC, :, :].rearrange("p c s -> p (c s)"),
                                   ACT.Exp, scale=SCALE).then_inc(probs_raw, 1)
                    if n >= UG and n % UG in (3, 5):
                        sums_out(a, b, 2 * (n // UG) - 2 + (n % UG == 5))
                    advance(sides, turns_after(n, total))
                for h in (2 * NG - 2, 2 * NG - 1):
                    sums_out(a, b, h)
                for w in sides:
                    finish(w)

            act.preload_act_table_set("natural_log_exp_and_others")
            for t, d in WEIGHTS:
                act.dma_start(t[:], d).then_inc(weights_in, 16)
            for t, d in ROWS:
                act.dma_start(t[:, :], d.unsqueeze(0).broadcast_to([P, d.shape[0]])).then_inc(weights_in, 16)
            for t, d in ((cos, cos_d), (sin, sin_d)):
                act.dma_start(t[:, :, :], d.rearrange("(t p) f -> p t f", p=P)).then_inc(weights_in, 16)
            finish(p1(0, *p1_at(0)))
            slot(0, 0, [p1(1, *p1_at(1))], len(P1_TURNS))
            with act.Fori(0, 2) as s:
                slot(0, s + 1, [p1(s + 2, *p1_at(0, s)), p2(s, *p2_at(0, s))], len(P1_TURNS) + len(P2_TURNS))
            slot(0, 3, [p2(2, *p2_at(2))], len(P2_TURNS))
            slot(1, 0, [p2(3, *p2_at(3))], len(P2_TURNS))
            with act.Fori(0, 3) as s:
                slot(1, s + 1, [p3(s, p3_at(s))], len(P3_TURNS))
            finish(p3(3, p3_at(3)))

        @block.gpsimd
        def _(pool):
            def ones_of(v):
                return v[:, :, :].rearrange("p t (h v) -> p (t h) v", v=VW)[:, :, HE:HE + 1]

            fills = [(ones[:, :], 1.0), (qs[0][64:KPAD, :, :], 0.0), (qs[1][64:KPAD, :, :], 0.0),
                     (ks[0][64:KPAD, :, :], 1.0), (ks[1][64:KPAD, :, :], 1.0), (vq[0][:, :, :], 0.0),
                     (vq[1][:, :, :], 0.0), (vc[:, :, :], 1.0), (ones_of(vq[0]), 1.0), (ones_of(vq[1]), 1.0)]
            assert len(fills) == FILLS
            for i, (tile, value) in enumerate(fills):
                if i:
                    pool.wait_ge(filled, i)
                pool.memset(tile, value).then_inc(filled, 1)

            for s in RAISED:
                pool.sem_inc(s, 1)
            for a in range(2):
                with pool.Fori(0, B) as b:
                    for n in range(UB):
                        gn = (a * B + b) * UB + n
                        kind, _heads = unit_kind(n)
                        c0, step = DIAGONALS[kind]
                        buf = probs[n % NPB]
                        if step:
                            first = min(c0, S - 2 * step)
                            diag = buf[:, first:first + 2 * step].rearrange("p (k s) -> p k s", k=2)
                            diag = diag[:, :, c0 - first:c0 - first + P]
                        else:
                            diag = buf[:, c0:c0 + P].unsqueeze(1)
                        pool.wait_ge(probs_raw, gn + 1)
                        pool.sem_inc(passed[1], 1)
                        pool.affine_select(out=diag, in_=diag, compare_op=ALU.is_ge, fill=0.0, base=a - 1,
                                           pattern=[[0, diag.shape[1]], [1, P]], channel_multiplier=-1)\
                            .then_inc(probs_ready, 1)

        @block.vector
        def _(dve):
            step = [0]

            def link(ins):
                step[0] += 1
                ins.then_inc(dve_step, 1)
                dve.wait_ge(dve_step, step[0])

            def fresh():
                dve.sem_clear(dve_step)
                step[0] = 0

            def bank_of(jobs, half, name):
                dve.wait_ge(side_done, jobs.done(half, name))
                return side[:, jobs.bank(name), :]

            def freeing(ins, jobs, half, name):
                ins.then_inc(side_free[jobs.bank(name)], 1)
                after(jobs, half, name)

            def after(jobs, half, *names):
                for i, v in jobs.last_freed(half, names):
                    dve.wait_ge(side_free[i], v)

            def skip(jobs, half, name):
                bank_of(jobs, half, name)
                freeing(dve.memset(gsum[0:1, 0:1], 0.0), jobs, half, name)

            def tt(out, in0, in1, op):
                return dve.tensor_tensor(out, in0, in1, op)

            def layernorm(src, phase, n):
                for t in range(T):
                    ins = dve.bn_stats(stats[:, t, :], src[:, t, :])
                link(ins)
                for t in range(T):
                    ins = dve.bn_aggr(mv[:, t, :], stats[:, t, :])
                link(ins)
                dve.tensor_scalar(var[:, :], mv[:, :, 1], EPS, None, ALU.add).then_inc(var_ready[phase], 1)
                dve.wait_ge(var_ready[phase], n + 1)
                dve.wait_ge(r0_ready[phase], n + 1)
                link(tt(rt[:, :], r0[:, :], r0[:, :], ALU.mult))
                link(tt(rt[:, :], rt[:, :], var[:, :], ALU.mult))
                link(dve.tensor_scalar(rt[:, :], rt[:, :], -0.5, 1.5, ALU.mult, ALU.add))
                link(tt(rstd[:, :], r0[:, :], rt[:, :], ALU.mult))

            def normalised(dst, src, t):
                return dve.tensor_scalar(dst[:, t, :], src[:, t, :], mv[:, t, 0:1], rstd[:, t:t + 1],
                                         ALU.subtract, ALU.mult)

            def over_tiles(row):
                return row[:, :].unsqueeze(1).broadcast_to([P, T, row.shape[1]])

            def project(jobs, a, k, half, bias, vbias):
                for j in range(NQ):
                    uses = k * 2 + j // 2
                    p = part[j % 2]
                    bank = bank_of(jobs, half, ("qk", j))
                    dve.tensor_scalar(qk[:, 0, :], bank[:, 0:QW], bias[:, 0:1], None, ALU.add)
                    freeing(dve.tensor_scalar(qk[:, 1, :], bank[:, QW:2 * QW], bias[:, 1:2], None, ALU.add),
                            jobs, half, ("qk", j))
                    dve.wait_ge(part_out[j % 2], 16 * 2 * uses)
                    link(dve.tensor_copy(p[:, 0, :, :], qk[:, :, :]))
                    if a == 1:
                        tt(sq[:, 2, :], p[:, 0, 0, :], p[:, 0, 1, :], ALU.mult)
                    tt(sq[:, 0:2, :], p[:, 0, :, :], p[:, 0, :, :], ALU.mult).then_inc(sq_ready, 1)
                    bank = bank_of(jobs, half, ("v", j))
                    dve.wait_ge(vq_out[j % 2], 16 * NG * uses)
                    v = vq[j % 2][:, :, :].rearrange("p t (h v) -> p t h v", v=VW)[:, :, :, 0:HE]
                    vb = vbias[:, :].rearrange("p (h f) -> p h f", f=HE).unsqueeze(1).broadcast_to([P, TQ, H, HE])
                    freeing(tt(v, bank[:, 0:TQ * D].rearrange("p (t h f) -> p t h f", t=TQ, f=HE), vb, ALU.add),
                            jobs, half, ("v", j))
                    link(tt(qkr[:, :, :], qk[:, :, :], p[:, 0, :, :], ALU.subtract))
                    link(dve.tensor_copy(p[:, 1, :, :], qkr[:, :, :]))
                    tt(p[:, 2, :, :], qkr[:, :, :], p[:, 1, :, :], ALU.subtract).then_inc(part_ready, 1)
                    if a == 0:
                        link(dve.tensor_copy(vc[:, j * TQ:(j + 1) * TQ, :].rearrange("p t (h f) -> p (t h) f", f=9)[:, :, 0:HE],
                                             vq[j % 2][:, :, :].rearrange("p t (h v) -> p (t h) v", v=VW)[:, :, 0:HE]))
                    bank = bank_of(jobs, half, ("norm", j))
                    for c in range(2 + a):
                        ins = dve.tensor_copy(nrm[:, c, :, j * TQ:(j + 1) * TQ].rearrange("p h t -> p t h"),
                                              bank[:, c * TQ * H:(c + 1) * TQ * H].rearrange("p (t h) -> p t h", h=H))
                    freeing(ins, jobs, half, ("norm", j))

            def bound_spreads(jobs, k, half):
                bank = bank_of(jobs, half, ("ktop", 0))
                freeing(dve.tensor_reduce(kmx[:, :], bank[:, 0:P], AX.X, ALU.max), jobs, half, ("ktop", 0))
                dve.tensor_scalar(kdiag[:, :], ident[:, :], kmx[:, 0:1], None, ALU.mult).then_inc(keys_spread, 1)

            def bound_squares(jobs, k, half):
                bank = bank_of(jobs, half, ("kspread", 0))
                freeing(dve.tensor_copy(ktop[:, :, :].rearrange("p h t -> p (h t)"), bank[:, 0:P]), jobs, half, ("kspread", 0))
                for t in range(1, T):
                    link(tt(ktop[:, :, t], ktop[:, :, t], ktop[:, :, t - 1], ALU.max))
                link(tt(c2[:, :, :], nrm[:, 0, :, :], ktop[:, :, :], ALU.mult))
                dve.tensor_scalar(c2[:, :, :], c2[:, :, :], 1e-12, None, ALU.max).then_inc(square_ready, 1)
                dve.wait_ge(square_ready, k + 1)
                link(dve.tensor_reduce(gm[:, 1:2], c2[:, :, :], AX.XY, ALU.max))
                link(dve.tensor_scalar(gm[:, 1:2], gm[:, 1:2], 1.0 / SQUARE_LIMIT, None, ALU.mult))

            def bound_ends(jobs, a, k, half):
                dve.wait_ge(root_ready, k + 1)
                if a == 1:
                    dve.scalar_tensor_tensor(out=ns[:, :, :], in0=cc[:, :, :], scalar=1.02, in1=nrm[:, 2, :, :],
                                             op0=ALU.mult, op1=ALU.add)
                    link(dve.scalar_tensor_tensor(out=cc[:, :, :], in0=cc[:, :, :], scalar=1.02, in1=nrm[:, 2, :, :],
                                                  op0=ALU.mult, op1=ALU.subtract))
                    dve.tensor_scalar(ns[:, :, :], ns[:, :, :], -0.5, None, ALU.mult)
                else:
                    dve.tensor_scalar(ns[:, :, :], cc[:, :, :], -0.51, None, ALU.mult)
                    link(dve.tensor_scalar(cc[:, :, :], cc[:, :, :], 1.02, None, ALU.mult))
                link(dve.tensor_reduce(gm[:, 0:1], cc[:, :, :], AX.XY, ALU.max))
                link(dve.tensor_scalar(gm[:, 0:1], gm[:, 0:1], 1.0 / LIMIT, None, ALU.mult))
                tt(gm[:, 0:1], gm[:, 0:1], gm[:, 1:2], ALU.max).then_inc(gap_ready, 1)
                bank = bank_of(jobs, half, ("shift", 0))
                dve.wait_ge(shift_out, 16 * k)
                link(dve.tensor_copy(shb[:, 0, :], bank[:, 0:P]))
                tt(shb[:, 1, :], bank[:, 0:P], shb[:, 0, :], ALU.subtract).then_inc(shift_ready, 1)
                freeing(dve.tensor_reduce(gm1[:, :], bank[0:1, P:2 * P], AX.X, ALU.max), jobs, half, ("shift", 0))
                dve.tensor_scalar(flags[0:1, bass.ds(k, 1)], gm1[:, :], 1.0, None, ALU.is_gt)\
                   .then_inc(flag_ready, 1)

            def exact(a, b):
                i = 0
                for g in range(NG):
                    if g >= 1:
                        dve.wait_ge(m_turned, g)
                    for h in range(HG):
                        for t in range(T):
                            dve.wait_ge(m_scores, i + 1)
                            dve.reduce_max(mx[:, h * T + t:h * T + t + 1],
                                           scores[:, i % NSC, :, :].rearrange("p c s -> p (c s)")[:, 0:(t + 1) * P],
                                           AX.X).then_inc(m_read, 1)
                            i += 1
                    dve.wait_ge(m_read, i)
                    dve.tensor_scalar(mx[:, :], mx[:, :], 0.0 if a == 0 else NEG, None, ALU.max).then_inc(m_rows, 1)
                    dve.wait_ge(m_turned, g + 1)
                    link(dve.tensor_scalar(mxn[:, :], acc[0:HG * T, 0, 0:P], -1.0, None, ALU.mult))
                    if g >= 1:
                        dve.wait_ge(m_out, 16 * 2 * g)
                    link(dve.tensor_copy(mxp[:, 0, :], mxn[:, :]))
                    tt(mxp[:, 1, :], mxn[:, :], mxp[:, 0, :], ALU.subtract).then_inc(m_parts, 1)

            def exact_if(a, b, k):
                fresh()
                dve.wait_ge(flag_ready, k + 1)
                with dve.If(dve.value_load(flags[0:1, bass.ds(k, 1)], min_val=0, max_val=1)):
                    exact(a, b)

            def combine(jobs, a, b, half, dst):
                for t in range(T + 2):
                    if t < T:
                        if a == 0:
                            link(tt(tot[:, t % 2, :, :], sfx[:, t, :].rearrange("p (h f) -> p h f", f=9),
                                    emr[:, :, t].unsqueeze(2).broadcast_to([P, H, 9]), ALU.mult))
                        bank = bank_of(jobs, half, ("num", t))
                        nb = bank.rearrange("p (h v) -> p h v", v=VW)[:, :, 0:9]
                        if a == 0:
                            freeing(tt(tot[:, t % 2, :, :], nb, tot[:, t % 2, :, :], ALU.add), jobs, half, ("num", t))
                        else:
                            freeing(dve.tensor_copy(tot[:, t % 2, :, :], nb), jobs, half, ("num", t))
                        link(dve.reciprocal(rden[:, t % 2, :], tot[:, t % 2, :, 8]))
                        tt(att[:, t % 2, :].rearrange("p (h f) -> p h f", f=HE), tot[:, t % 2, :, 0:HE],
                           rden[:, t % 2, :].unsqueeze(2).broadcast_to([P, H, HE]), ALU.mult).then_inc(att_ready[a], 1)
                    if 0 <= t - 1 < T:
                        bank = bank_of(jobs, half, ("att", t - 1))
                        dve.tensor_copy(attT[:, (t - 1) % 2, :], bank[:, 0:P]).then_inc(side_free[jobs.bank(("att", t - 1))], 1)
                    if t >= 2:
                        bank = bank_of(jobs, half, ("out", t - 2))
                        freeing(tt(dst[:, t - 2, :], bank[:, 0:D], xrow[:, t - 2, :], ALU.add), jobs, half, ("out", t - 2))

            def p1(b, k, half, p2s):
                fresh()
                dve.wait_ge(x_in[0], 16 * (b + 1))
                layernorm(xrow, 0, b)
                dve.wait_ge(rows_out, 32 * p2s + 1)
                for t in range(T - 1):
                    normalised(xnorm, xrow, t)
                normalised(xnorm, xrow, T - 1).then_inc(rows_ready[0], 1)
                dve.wait_ge(rows_ready[0], b + 1)
                project(P1, 0, k, half, bqk, bv)
                link(dve.tensor_copy(vsum[:, T - 2, :], vc[:, T - 1, :]))
                for t in range(T - 3, 0, -1):
                    link(tt(vsum[:, t, :], vsum[:, t + 1, :], vc[:, t + 1, :], ALU.add))
                tt(vsum[:, 0, :], vsum[:, 1, :], vc[:, 1, :], ALU.add).then_inc(vsum_ready, 1)
                bound_spreads(P1, k, half)
                dve.wait_ge(sfx_out, 16 * b)
                for i in range(3):
                    bank = bank_of(P1, half, ("suffix", i))
                    w = min(3, T - 3 * i)
                    freeing(dve.tensor_copy(sfx[:, 3 * i:3 * i + w, :].rearrange("p t f -> p (t f)"), bank[:, 0:w * 144]),
                            P1, half, ("suffix", i))
                    if i == 0:
                        bound_squares(P1, k, half)
                bound_ends(P1, 0, k, half)

            def p2(b, k, half):
                fresh()
                dve.wait_ge(sh2_in, 16 * (b + 1))
                tt(esum[:, :], sh2[:, 0, :], sh2[:, 1, :], ALU.add).then_inc(esum_ready, 1)
                dve.wait_ge(x_in[1], 16 * (b + 1))
                link(tt(xrow[:, :, :], xrow[:, :, :], over_tiles(br), ALU.add))
                bank = bank_of(P2, half, ("em", 0))
                freeing(dve.tensor_copy(emr[:, :, :].rearrange("p h t -> p (h t)"), bank[:, 0:P]), P2, half, ("em", 0))
                dve.wait_ge(sfx_in, 16 * (b + 1))
                dve.wait_ge(rows_out, 32 * b + 1)
                combine(P2, 0, b, half, x2)
                layernorm(x2, 1, b)
                for t in range(T):
                    ins = normalised(xnorm, x2, t)
                link(ins)
                pairs = xnorm[:, :, :].rearrange("p t (h f two) -> p t h f two", h=H, two=2)
                turned = rope[:, :, :].rearrange("p t (h f two) -> p t h f two", h=H, two=2)
                c4, s4 = (w[:, :, :].unsqueeze(2).broadcast_to([P, T, H, HE // 2]) for w in (cos, sin))
                tmp = [r.rearrange("p (t h f) -> p t h f", t=T, h=H) for r in rtmp]
                tt(tmp[0], pairs[:, :, :, :, 0], c4, ALU.mult)
                tt(tmp[2], pairs[:, :, :, :, 0], s4, ALU.mult)
                link(tt(tmp[1], pairs[:, :, :, :, 1], s4, ALU.mult))
                tt(turned[:, :, :, :, 0], tmp[0], tmp[1], ALU.subtract)
                link(tt(tmp[3], pairs[:, :, :, :, 1], c4, ALU.mult))
                tt(turned[:, :, :, :, 1], tmp[2], tmp[3], ALU.add).then_inc(rows_ready[1], 1)
                dve.wait_ge(rows_ready[1], b + 2)
                project(P2, 1, k, half, binqk, binv)
                bound_spreads(P2, k, half)
                bound_squares(P2, k, half)
                bound_ends(P2, 1, k, half)

            def p3(b, half):
                fresh()
                dve.wait_ge(xn_in, 32 * (b + 1))
                link(tt(xrow[:, :, :], xrow[:, :, :], over_tiles(bo), ALU.add))
                combine(P3, 1, b, half, xnorm)
                layernorm(xnorm, 2, 2 * b)
                for t in range(T):
                    ins = normalised(x1, xnorm, t)
                link(ins)
                link(tt(x1[:, :, :], x1[:, :, :], over_tiles(l1w), ALU.mult))
                tt(x1[:, :, :], x1[:, :, :], over_tiles(l1b), ALU.add).then_inc(x1_ready, 1)
                for j in range(NQ):
                    bank = bank_of(P3, half, ("x1T", j))
                    freeing(dve.tensor_copy(x1T[:, j * TQ:(j + 1) * TQ, :].rearrange("p t s -> p (t s)"), bank[:, 0:QW]),
                            P3, half, ("x1T", j))

                def wide(v):
                    return v[:, :].unsqueeze(2).broadcast_to([P, T, NE])

                bank = bank_of(P3, half, ("gate", 0))
                freeing(tt(gl[:, :, :], bank[:, 0:T * NE].rearrange("p (t e) -> p t e", e=NE), over_tiles(bg), ALU.add),
                        P3, half, ("gate", 0))
                link(dve.tensor_reduce(gsum[:, :], gl[:, :, :], AX.X, ALU.max))
                tt(gl[:, :, :], gl[:, :, :], wide(gsum), ALU.subtract).then_inc(gates_shifted, 1)
                dve.wait_ge(gates_exp, b + 1)
                link(dve.tensor_reduce(gsum[:, :], ga[:, :, :], AX.X, ALU.add))
                link(dve.reciprocal(gsum[:, :], gsum[:, :]))
                link(tt(ga[:, :, :], ga[:, :, :], wide(gsum), ALU.mult))
                link(dve.tensor_copy(gb[:, :, :], ga[:, :, :]))
                for i in range(2):
                    link(dve.tensor_reduce(gsum[:, :], gb[:, :, :], AX.X, ALU.max))
                    link(tt(G[:, :, :], gb[:, :, :], wide(gsum), ALU.is_equal))
                    link(tt(G[:, :, :], G[:, :, :], over_tiles(iota8), ALU.mult))
                    link(dve.tensor_reduce(gidx[:, :], G[:, :, :], AX.X, ALU.min))
                    one = G if i else gmask
                    link(tt(one[:, :, :], over_tiles(iota8), wide(gidx), ALU.is_equal))
                    if i == 0:
                        link(dve.scalar_tensor_tensor(out=gb[:, :, :], in0=gmask[:, :, :], scalar=-2.0,
                                                      in1=gb[:, :, :], op0=ALU.mult, op1=ALU.add))
                link(tt(gmask[:, :, :], gmask[:, :, :], G[:, :, :], ALU.add))
                tt(G[:, :, :], ga[:, :, :], gmask[:, :, :], ALU.mult).then_inc(G_ready, 1)
                dve.wait_ge(G_ready, b + 1)
                for i in range(2):
                    bank = bank_of(P3, half, ("GT", i))
                    freeing(dve.tensor_copy(GT[:, 4 * i:4 * i + 4, :].rearrange("e t s -> e (t s)"), bank[0:NE, :]),
                            P3, half, ("GT", i))
                for t in range(T):
                    bank = bank_of(P3, half, ("bias", t))
                    freeing(tt(moe[:, :], bank[:, 0:D], x1[:, t, :], ALU.add), P3, half, ("bias", t))
                    for i in range(2):
                        bank = bank_of(P3, half, (f"e{i}", t))
                        for e in range(4):
                            dst = xnorm[:, t, :] if (i, e) == (1, 3) else moe[:, :]
                            ins = dve.scalar_tensor_tensor(out=dst, in0=bank[:, e * D:(e + 1) * D],
                                                           scalar=G[:, t, 4 * i + e:4 * i + e + 1], in1=moe[:, :],
                                                           op0=ALU.mult, op1=ALU.add)
                            if e < 3:
                                link(ins)
                            else:
                                freeing(ins, P3, half, (f"e{i}", t))
                skip(P3, half, ("pad", 0))
                layernorm(xnorm, 2, 2 * b + 1)
                dve.wait_ge(y_out, 16 * b + 1)
                for t in range(T):
                    ins = normalised(yout, xnorm, t)
                link(ins)
                link(tt(yout[:, :, :], yout[:, :, :], over_tiles(l2w), ALU.mult))
                link(tt(yout[:, :, :], yout[:, :, :], over_tiles(l2b), ALU.add))
                tt(yout[:, :, :], yout[:, :, :], x2[:, :, :], ALU.add).then_inc(y_ready, 1)

            dve.wait_ge(first_weights_in, 16 * n_first)
            dve.wait_ge(filled, FILLS)
            for t, landing, _d in NARROW:
                dve.tensor_copy(t[:, :], landing).then_inc(narrowed, 1)
            dve.wait_ge(narrowed, len(NARROW))

            p1(0, *p1_at(0), 0)
            dve.wait_ge(weights_in, 16 * n_weights)
            exact_if(0, 0, 0)
            p1(1, *p1_at(1), 0)
            with dve.Fori(0, 2) as s:
                exact_if(0, s + 1, s + 1)
                p1(s + 2, *p1_at(0, s), s)
                p2(s, *p2_at(0, s))
            exact_if(0, 3, 4)
            p2(2, *p2_at(2))
            exact_if(1, 0, 3)
            p2(3, *p2_at(3))
            with dve.Fori(0, 3) as s:
                exact_if(1, s + 1, s + 5)
                p3(s, p3_at(s))
            p3(3, p3_at(3))


def host_arrays(i):
    import numpy as np

    order = np.arange(D).reshape(NG, HG, HE).transpose(0, 2, 1).reshape(D)
    wq, bq = i["L0_attn_Wqkv"], i["L0_attn_bqkv"]
    wqkv = np.zeros((D, 3, D), wq.dtype)
    for h in range(H):
        r = slice(h * HE, (h + 1) * HE)
        for c in range(3):
            wqkv[r, c, r] = wq[:, c * HE:(c + 1) * HE]
    wqkv = np.concatenate([wqkv[:, 0:2][:, :, order], wqkv[:, 2:3]], axis=1)
    bqk = np.stack([np.tile(bq[c * HE:(c + 1) * HE], H)[order] for c in range(2)], axis=1)
    win = i["L0_ffn_in_proj_w"].T.reshape(D, 3, D)
    win = np.concatenate([win[:, 0:2][:, :, order], win[:, 2:3]], axis=1)
    binp = i["L0_ffn_in_proj_b"].reshape(3, D)
    angles = (np.arange(S, dtype=np.float32)[:, None]
              * (1.0 / 10000.0 ** (np.arange(0, HE, 2, dtype=np.float32) / HE)).astype(np.float32)[None, :])
    row, col = np.arange(P)[:, None], np.arange(P)[None, :]
    head = (np.arange(P) // (HG * HE)) * HG + np.arange(P) % HG
    return {
        "x": i["L0_attn_x"], "wqkv": wqkv, "bqk": bqk, "bv": np.tile(bq[2 * HE:], H),
        "wr": i["L0_attn_Wr"], "br": i["L0_attn_br"],
        "win": win, "binqk": np.stack([binp[0][order], binp[1][order]], axis=1), "binv": binp[2],
        "wo": i["L0_ffn_out_proj_w"].T, "bo": i["L0_ffn_out_proj_b"],
        "wg": i["L0_ffn_gate_w"].T, "bg": i["L0_ffn_gate_b"],
        "we": i["L0_ffn_expert_w"].transpose(2, 0, 1).reshape(D, NE * D), "be": i["L0_ffn_expert_b"],
        "l1w": i["L0_ffn_ln1_w"], "l1b": i["L0_ffn_ln1_b"], "l2w": i["L0_ffn_ln2_w"], "l2b": i["L0_ffn_ln2_b"],
        "cos": np.cos(angles).astype(np.float32), "sin": np.sin(angles).astype(np.float32),
        "ident": np.eye(P, dtype=np.float32),
        "hide": np.stack([np.where(col >= row, NEG, 0.0), np.where(col > row, NEG, 0.0)]).astype(np.float32),
        "later": (row >= col).astype(np.float32),
        "headsum": (head[:, None] == np.arange(H)[None, :]).astype(np.float32),
        "iota8": np.arange(NE, dtype=np.float32) - NE,
    }


def kernel(**inputs):
    import numpy as np
    import concourse.bacc as bacc
    from concourse.bass_utils import run_bass_kernel_spmd

    nc = bacc.Bacc("TRN2", target_bir_lowering=False, num_devices=1)
    arrays, args = {}, []
    for name, a in host_arrays({k: np.asarray(v) for k, v in inputs.items()}).items():
        a = np.ascontiguousarray(a)
        arrays[f"in_{name}"] = a
        args.append(nc.dram_tensor(f"in_{name}", a.shape, mybir.dt.from_np(a.dtype), kind="ExternalInput").ap())
    args.append(nc.dram_tensor("out_rows", (B, S, D), F32, kind="ExternalOutput").ap())
    build(nc, *args)
    r = run_bass_kernel_spmd(nc, [arrays], core_ids=[0])
    return r.results[0]["out_rows"]
```

```python
from contextlib import ExitStack

import concourse.bass as bass
from concourse import mybir

B, S, D, H = 4, 1024, 128, 16
HE = D // H
NE = 8
P = 128
T = S // P
TQ = 2
NQ = T // TQ
QW = TQ * P
HG = 4
NG = H // HG
VW = 32
NPART = 3
KROWS = NPART * NPART * HE
SROW = KROWS
KPAD = 96
SCALE = float(HE) ** -0.5
EPS = 1e-5
NEG = -1e30
LIMIT = 110.0 / SCALE
SQUARE_LIMIT = 1e16

KINDS = [
    [[(0, 0, 0, 512)], [(0, 512, 512, 512)]],
    [[(1, 0, 512, 512)], [(1, 512, 128, 384), (7, 896, 896, 128)]],
    [[(2, 0, 512, 512)], [(2, 512, 256, 256), (6, 768, 768, 256)]],
    [[(3, 0, 512, 512)], [(3, 512, 384, 128), (5, 640, 640, 384)]],
    [[(4, 0, 512, 512)]],
]
DIAGONALS = [(0, 0), (512, 384), (512, 256), (512, 128), (0, 512)]
UG = 18
UB = UG * NG
GG = 9
GB = GG * NG
NSC = 2
FILLS = 10
FILLS_FIRST = 6
NPB = 11
PV_LAG = 7

F32 = mybir.dt.float32
BF16 = mybir.dt.bfloat16
I32 = mybir.dt.int32
ACT = mybir.ActivationFunctionType
ALU = mybir.AluOpType
AX = mybir.AxisListType


def unit_kind(n):
    u = n % UG
    if u < 16:
        return u // 4, [(u % 4, 0)]
    return 4, [(2 * (u - 16), 0), (2 * (u - 16) + 1, 512)]


def group_of(g):
    return (g // 2, g % 2) if g < 8 else (4, 0)


def groups_after(n):
    left = UB - 1 - n
    return GB - 1 - 2 * left if left < 2 else max((n - PV_LAG) // 2 + 1, 0)


def groups_before(kind):
    return min(2 * kind + 2, GG)


JOB_KINDS = ("em", "num", "att", "out", "xT", "qk", "v", "norm", "ktop", "kspread", "suffix", "shift", "x1T", "gate",
             "GT", "bias", "e0", "e1", "pad")


def rests(n):
    return [("rest", i) for i in range(n)]


def projection_turns(a):
    turns = [("xT", 0)] + rests(5)
    for j in range(NQ):
        turns += [("qk", j), ("v", j)] + [("norm", j - 1)] * (j > 0) + rests(1)
        turns += [("xT", j + 1)] * (j + 1 < NQ) + [("rest", 0), ("split", j), ("parts", j)] + rests(1 + a)
    return turns + rests(3) + [("norm", NQ - 1)] + rests(1)


def combination_turns():
    turns = []
    for t in range(T + 2):
        turns += [("num", t)] * (t < T) + rests(1) + [("att", t - 1)] * (0 <= t - 1 < T) + rests(1)
        turns += [("out", t - 2)] * (t >= 2)
    return turns


P1_TURNS = (rests(1) + [("root", 0)] + rests(5) + projection_turns(0)
            + [("ktop", 0)] + rests(4) + [("kspread", 0)] + rests(2) + [("roots", 0)] + rests(3) + [("shift", 0)]
            + [("store", 0)] + rests(1) + [("suffix", 0)] + [("suffix", 1)]
            + [("suffix", 2)] + rests(2) + [("store", 1)])
P2_TURNS = (rests(2) + [("exp", 0)] + rests(4) + [("em", 0)] + rests(1) + combination_turns()
            + rests(9) + [("root", 0)] + rests(17) + projection_turns(1)
            + [("ktop", 0)] + rests(2) + [("kspread", 0)] + rests(2) + [("roots", 0)] + rests(4) + [("shift", 0)]
            + rests(2) + [("store", 0)])
P3_TURNS = (rests(17) + combination_turns() + rests(9) + [("root", 0)] + rests(15)
            + sum(([("x1T", j)] + rests(1) for j in range(NQ)), []) + rests(1) + [("gate", 0)]
            + rests(5) + [("exp", 0)] + rests(15) + [("GT", 0)] + rests(1) + [("GT", 1)] + rests(2)
            + sum(([("bias", t)] + rests(1) + [("e0", t)] + rests(2) + [("e1", t)] + rests(1) for t in range(T)), [])
            + [("pad", 0)] + rests(9) + [("root", 1)] + rests(14) + [("store", 0)])


class Jobs:

    def __init__(self, turns):
        names = [t for t in turns if t[0] in JOB_KINDS]
        assert len(names) % 2 == 0 and len(set(names)) == len(names)
        self.index = {name: i for i, name in enumerate(names)}
        self.half = len(names) // 2

    def bank(self, name):
        return self.index[name] % 2

    def done(self, half, name):
        return 2 * half + self.index[name] + 1

    def freed(self, half, name):
        return half + self.index[name] // 2

    def last_freed(self, half, names):
        last = {self.bank(n): n for n in sorted(names, key=self.index.get)}
        return [(i, self.freed(half, n) + 1) for i, n in last.items()]


def idle(turns):
    for _ in range(turns):
        yield


def finish(work):
    for _ in work:
        pass


def pace(turns, span):
    counts, done = [], 0
    for n in range(UB):
        start = done
        while done < len(turns) and (done * span < (n + 1) * len(turns) or n >= span):
            done += 1
        counts.append(done - start)
    return counts


def advance(works, turns):
    for _ in range(turns):
        while works and next(works[0], DONE) is DONE:
            works.pop(0)


DONE = object()
START = 8
NEXT_LOAD = 62
PACE1 = pace(P1_TURNS, NEXT_LOAD)
PACE12 = pace(P1_TURNS + P2_TURNS, UB)
PACE2 = pace(rests(START) + P2_TURNS, UB)
PACE3 = pace(P3_TURNS, UB)


def build(nc, x_d, wqkv_d, bqk_d, bv_d, wr_d, br_d, win_d, binqk_d, binv_d, wo_d, bo_d, wg_d, bg_d, we_d, be_d,
          l1w_d, l1b_d, l2w_d, l2b_d, cos_d, sin_d, ident_d, hide_d, later_d, headsum_d, iota8_d, out_d):
    ctx = ExitStack()
    with ctx:
        def sb(name, shape, dt=F32):
            return ctx.enter_context(nc.sbuf_tensor(name, shape, dt))

        def sem(name):
            return ctx.enter_context(nc.semaphore(name))

        def dram(name, shape, dt=F32):
            return nc.dram_tensor(f"{name}_dram", shape, dt, kind="Internal").ap()

        parts_d = [dram(f"parts{a}", [B, 2, NPART, P, S], BF16) for a in range(2)]
        shift_d = [dram(f"shift{a}", [B, 2, H, S], BF16) for a in range(2)]
        values_d = [dram(f"values{a}", [B, NG, P, T, HG * VW]) for a in range(2)]
        num_d = [dram(f"num{a}", [B, NG, P, S]) for a in range(2)]
        suffix_d = dram("suffix", [B, P, T, H * 9])
        x2_d = dram("x2", [B, P, T, D])
        xn_d = dram("xn", [B, P, T, D])

        ident = sb("ident", [P, P])
        ident_b = sb("ident_b", [P, P], BF16)
        hide = [sb(f"hide{a}", [P, P], BF16) for a in range(2)]
        later = sb("later", [P, P])
        ones = sb("ones", [P, P])
        headsum = sb("headsum", [P, H], BF16)
        wqkv = sb("wqkv", [P, 3, P])
        bqk = sb("bqk", [P, 2])
        bv = sb("bv", [P, D])
        wr = sb("wr", [P, D])
        br = sb("br", [P, D])
        win = sb("win", [P, 3, P])
        binqk = sb("binqk", [P, 2])
        binv = sb("binv", [P, D])
        wo = sb("wo", [P, D])
        bo = sb("bo", [P, D])
        wg = sb("wg", [P, NE])
        bg = sb("bg", [P, NE])
        we = sb("we", [P, NE * D])
        be = sb("be", [NE, D])
        l1w = sb("l1w", [P, D])
        l1b = sb("l1b", [P, D])
        l2w = sb("l2w", [P, D])
        l2b = sb("l2b", [P, D])
        cos = sb("cos", [P, T, HE // 2])
        sin = sb("sin", [P, T, HE // 2])
        iota8 = sb("iota8", [P, NE])

        qs = [sb(f"qs{i}", [KPAD, HG, S], BF16) for i in range(2)]
        ks = [sb(f"ks{i}", [KPAD, HG, S], BF16) for i in range(2)]
        vs = [sb(f"vs{i}", [P, T, HG * VW]) for i in range(2)]
        probs = [sb(f"probs{i}", [P, S]) for i in range(NPB)]
        num = [sb(f"num{i}", [P, S]) for i in range(2)]
        mx = sb("mx", [P, HG * T])
        mxn = sb("mxn", [HG * T, P])
        mxp = sb("mxp", [HG * T, 2, P], BF16)

        xrow0 = sb("xrow0", [P, T, D])
        xrow = sb("xrow", [P, T, D])
        xnorm = sb("xnorm", [P, T, D])
        rope = sb("rope", [P, T, D])
        stats = sb("stats", [P, T, 6])
        mv = sb("mv", [P, T, 2])
        var = sb("var", [P, T])
        lnv = sb("lnv", [P, T])
        r0 = sb("r0", [P, T])
        rt = sb("rt", [P, T])
        rstd = sb("rstd", [P, T])
        xT = sb("xT", [P, 2, QW])
        qk = [sb(f"qk{i}", [P, 2, QW]) for i in range(2)]
        qkr = [sb(f"qkr{i}", [P, 2, QW]) for i in range(2)]
        part = [sb(f"part{i}", [P, NPART, 2, QW], BF16) for i in range(2)]
        sq = [sb(f"sq{i}", [P, 3, QW], BF16) for i in range(2)]
        nrm = sb("nrm", [P, 3, H, T])
        ktop = sb("ktop", [P, H, T])
        kmx = sb("kmx", [P, 1])
        kdiag = sb("kdiag", [P, P])
        c2 = sb("c2", [P, H, T])
        cl = sb("cl", [P, H, T])
        cc = sb("cc", [P, H, T])
        ns = sb("ns", [P, H, T])
        gm = sb("gm", [P, 2])
        gm1 = sb("gm1", [1, 1])
        shb = sb("shb", [P, 2, P], BF16)
        flags = sb("flags", [1, 2 * B], I32)
        vq = [sb(f"vq{i}", [P, TQ, H * VW]) for i in range(2)]
        vc = sb("vc", [P, T, H * 9])
        vsum = sb("vsum", [P, T, H * 9])
        sfx0 = sb("sfx0", [P, T, H * 9])
        sfx = sb("sfx", [P, T, H * 9])
        sh2 = sb("sh2", [P, 2, P], BF16)
        esum = kdiag
        em = sb("em", [P, P])
        emr = sb("emr", [P, H, T])
        nt = [sb(f"nt{i}", [P, NG, QW]) for i in range(2)]
        tot = sb("tot", [P, 2, H, 9])
        rden = sb("rden", [P, 2, H])
        att = sb("att", [P, 2, D])
        attT = sb("attT", [P, 2, D])
        x2 = sb("x2s", [P, T, D])
        x1 = sb("x1", [P, T, D])
        x1T = rope
        gl = sb("gl", [P, T, NE])
        ga = sb("ga", [P, T, NE])
        gb = sb("gb", [P, T, NE])
        gmask = sb("gmask", [P, T, NE])
        gidx = sb("gidx", [P, T])
        gsum = sb("gsum", [P, T])
        G = sb("G", [P, T, NE])
        GT = sb("GT", [NE, T, P])
        x1b = sb("x1b", [P, 2, D])
        prod, psum4 = (w[:, :, :].rearrange("p t f -> p (t f)")[:, 0:NE * D].rearrange("p (i e d) -> p i e d", i=2, d=D)
                       for w in (sfx, vsum))
        moe = att
        moe1 = sb("moe1", [P, D])
        yout = sb("yout", [P, T, D])
        rtmp = [w[:, 4 * i:4 * i + 4, :].rearrange("p t d -> p (t d)") for w in (yout, x1) for i in range(2)]

        scores = ctx.enter_context(nc.psum_tensor("scores", [P, NSC, 2, 512], F32))
        acc = ctx.enter_context(nc.psum_tensor("acc", [P, 2, 512], F32))
        side = ctx.enter_context(nc.psum_tensor("side", [P, 2, 512], F32))

        first_weights_in = sem("first_weights_in")
        weights_in = sem("weights_in")
        filled = sem("filled")
        narrowed = sem("narrowed")
        passed = [sem(f"passed_{e}") for e in ("sync", "pool", "tensor")]
        dve_step = sem("dve_step")
        act_step = sem("act_step")
        side_done = sem("side_done")
        side_free = [sem(f"side_free{i}") for i in range(2)]
        x_in = [sem(f"x_in{i}") for i in range(2)]
        var_ready = [sem(f"var_ready{i}") for i in range(3)]
        r0_ready = [sem(f"r0_ready{i}") for i in range(3)]
        rows_ready = [sem(f"rows_ready{i}") for i in range(2)]
        first_part_ready = sem("first_part_ready")
        pool_step = sem("pool_step")
        part_ready = sem("part_ready")
        part_out = [sem(f"part_out{i}") for i in range(2)]
        sq_ready = sem("sq_ready")
        vq_out = [sem(f"vq_out{i}") for i in range(2)]
        square_ready = sem("square_ready")
        root_ready = sem("root_ready")
        keys_spread = sem("keys_spread")
        gap_ready = sem("gap_ready")
        shift_ready = sem("shift_ready")
        shift_out = sem("shift_out")
        flag_ready = sem("flag_ready")
        vc_ready = sem("vc_ready")
        vsum_ready = sem("vsum_ready")
        sfx_out = sem("sfx_out")
        qs_in = [sem(f"qs_in{i}") for i in range(2)]
        vs_in = [sem(f"vs_in{i}") for i in range(2)]
        scores_ready = sem("scores_ready")
        probs_raw = sem("probs_raw")
        probs_ready = sem("probs_ready")
        group_done = sem("group_done")
        acc_read = sem("acc_read")
        num_out = [sem(f"num_out{i}") for i in range(2)]
        m_in = sem("m_in")
        m_scores = sem("m_scores")
        m_read = sem("m_read")
        m_rows = sem("m_rows")
        m_turned = sem("m_turned")
        m_parts = sem("m_parts")
        m_out = sem("m_out")
        m_restored = sem("m_restored")
        sh2_in = sem("sh2_in")
        sfx_in = sem("sfx_in")
        nt_in = [sem(f"nt_in{i}") for i in range(2)]
        xn_in = sem("xn_in")
        esum_ready = sem("esum_ready")
        em_ready = sem("em_ready")
        att_ready = [sem(f"att_ready{i}") for i in range(2)]
        rows_out = sem("rows_out")
        x1_ready = sem("x1_ready")
        gates_shifted = sem("gates_shifted")
        gates_exp = sem("gates_exp")
        G_ready = sem("G_ready")
        products_ready = sem("products_ready")
        moe_ready = sem("moe_ready")
        rows_biased = sem("rows_biased")
        y_ready = sem("y_ready")
        y_out = sem("y_out")

        RAISED = [rows_ready[1], rows_out, y_ready, y_out, att_ready[0], att_ready[1]]

        P1, P2, P3 = Jobs(P1_TURNS), Jobs(P2_TURNS), Jobs(P3_TURNS)

        pair = P1.half + P2.half

        def p1_at(b, s=None):
            return (b, b * P1.half) if s is None else (2 * s + 2, 2 * P1.half + s * pair)

        def p2_at(b, s=None):
            return (b + 4, 4 * P1.half + b * P2.half) if s is None else (2 * s + 3, 3 * P1.half + s * pair)

        def p3_at(b):
            return 4 * P1.half + 4 * P2.half + b * P3.half

        NARROW = [(ident_b, xnorm[:, 0, :], ident_d), (hide[0], xnorm[:, 1, :], hide_d[0]),
                  (hide[1], xnorm[:, 2, :], hide_d[1]), (headsum, xnorm[:, 3, 0:H], headsum_d)]
        FIRST = [(ident, ident_d), (wqkv, wqkv_d), (bqk, bqk_d), (later, later_d)]
        WEIGHTS = [(wr, wr_d), (win, win_d), (binqk, binqk_d), (wo, wo_d), (wg, wg_d), (we, we_d), (be, be_d)]
        ROWS = [(binv, binv_d), (br, br_d), (bo, bo_d), (bg, bg_d), (l1w, l1w_d), (l1b, l1b_d),
                (l2w, l2w_d), (l2b, l2b_d), (iota8, iota8_d)]
        n_first = len(FIRST) + len(NARROW) + 1
        n_weights = len(WEIGHTS) + len(ROWS) + 2
        QS_DMAS = 2 * NPART + 1
        M_DMAS = 2 * NPART

        block = ctx.enter_context(nc.Block())

        @block.sync
        def _(sp):
            def wait(semaphore, value):
                sp.wait_ge(semaphore, value)
                sp.sem_inc(passed[0], 1)

            def bc(ap):
                return ap.unsqueeze(0).broadcast_to([P, ap.shape[0]])

            def rows_of(dst, b):
                return dst[b].rearrange("(t p) d -> p t d", p=P)

            def after(jobs, half, *names):
                for i, v in jobs.last_freed(half, names):
                    wait(side_free[i], v)

            def projected_out(jobs, a, b, k, half, j):
                wait(part_ready, k * NQ + j + 1)
                for c in range(2):
                    sp.dma_start(parts_d[a][b, c].rearrange("i p s -> p i s")[:, :, j * QW:(j + 1) * QW],
                                 part[j % 2][:, :, c, :]).then_inc(part_out[j % 2], 16)
                after(jobs, half, ("v", j))
                for g in range(NG):
                    sp.dma_start(values_d[a][b, g][:, j * TQ:(j + 1) * TQ, :],
                                 vq[j % 2][:, :, g * HG * VW:(g + 1) * HG * VW]).then_inc(vq_out[j % 2], 16)

            def shift_store(a, b, k):
                wait(shift_ready, k + 1)
                sp.dma_start(shift_d[a][b].rearrange("i h (t s) -> (h t) i s", s=P), shb[:, :, :]).then_inc(shift_out, 16)

            def p1_rows(b, before):
                if b != 0:
                    wait(rows_ready[0], before)
                sp.dma_start(xrow0[:, :, :], rows_of(x_d, b)).then_inc(x_in[0], 16)

            def p1(b, k, half):
                for turn, j in P1_TURNS:
                    if turn == "norm":
                        projected_out(P1, 0, b, k, half, j)
                    if (turn, j) == ("store", 0):
                        shift_store(0, b, k)
                    if (turn, j) == ("store", 1):
                        after(P1, half, ("suffix", 1), ("suffix", 2))
                        sp.dma_start(suffix_d[b], sfx0[:, :, :]).then_inc(sfx_out, 16)
                    yield

            def numerators_in(a, b, j):
                wait(att_ready[a], 1 + (b * T + (j - 1) * TQ if j >= 2 else b * T))
                sp.dma_start(nt[j % 2][:, :, :],
                             num_d[a][b].rearrange("g p s -> p g s")[:, :, j * QW:(j + 1) * QW]).then_inc(nt_in[j % 2], 16)

            def p2_operands(b):
                wait(rows_ready[1], b + 1)
                sp.dma_start(sh2[:, :, :], shift_d[0][b].rearrange("i h (t s) -> (h t) i s", s=P)).then_inc(sh2_in, 16)
                for i in range(2):
                    wait(num_out[i], 16 * 2 * (b + 1))
                sp.dma_start(xrow[:, :, :], rows_of(x_d, b)).then_inc(x_in[1], 16)
                numerators_in(0, b, 0)
                wait(sfx_out, 16 * (b + 1))
                sp.dma_start(sfx[:, :, :], suffix_d[b]).then_inc(sfx_in, 16)
                numerators_in(0, b, 1)

            def p2(b, k, half):
                for turn, j in P2_TURNS:
                    if turn == "att" and j % 2 and j // 2 + 2 < NQ:
                        numerators_in(0, b, j // 2 + 2)
                    if (turn, j) == ("xT", 0):
                        wait(rows_ready[1], b + 2)
                        sp.dma_start(x2_d[b], x2[:, :, :]).then_inc(rows_out, 16)
                        sp.dma_start(xn_d[b], xnorm[:, :, :]).then_inc(rows_out, 16)
                    if turn == "norm":
                        projected_out(P2, 1, b, k, half, j)
                    if turn == "store":
                        shift_store(1, b, k)
                    yield

            def p3_operands(b):
                wait(y_ready, b + 1)
                sp.dma_start(xrow[:, :, :], xn_d[b]).then_inc(xn_in, 16)
                sp.dma_start(x2[:, :, :], x2_d[b]).then_inc(xn_in, 16)
                for i in range(2):
                    wait(num_out[i], 16 * 2 * (B + b + 1))
                numerators_in(1, b, 0)
                numerators_in(1, b, 1)

            def p3(b):
                for turn, j in P3_TURNS:
                    if turn == "att" and j % 2 and j // 2 + 2 < NQ:
                        numerators_in(1, b, j // 2 + 2)
                    if turn == "store":
                        wait(y_ready, b + 2)
                        sp.dma_start(rows_of(out_d, b), yout[:, :, :]).then_inc(y_out, 16)
                    yield

            def parts_in(a, b, g, u, landed):
                heads = slice(g * HG * HE, (g + 1) * HG * HE)
                for i in range(NPART):
                    r = slice(i * NPART * HE, (i + 1) * NPART * HE)
                    q1 = parts_d[a][b, 0, i, heads].rearrange("(e h) s -> e (h s)", e=HE)
                    k3 = parts_d[a][b, 1, :, heads].rearrange("j (e h) s -> j e (h s)", e=HE)
                    sp.dma_start(qs[u][r, :, :].rearrange("r h s -> r (h s)"),
                                 q1.unsqueeze(0).broadcast_to([NPART, HE, HG * S])).then_inc(landed, 16)
                    sp.dma_start(ks[u][r, :, :].rearrange("r h s -> r (h s)"), k3).then_inc(landed, 16)

            def shift_in(a, b, g, u, landed):
                sp.dma_start(qs[u][SROW:SROW + 2, :, :],
                             shift_d[a][b, :, g * HG:(g + 1) * HG]).then_inc(landed, 16)

            def load(a, b, g):
                u = g % 2
                if g >= 2 or not isinstance(b, int) or a * B + b > 0:
                    wait(group_done, ((a * B + b) * NG + g - 1) * GG)
                parts_in(a, b, g, u, qs_in[u])
                shift_in(a, b, g, u, qs_in[u])
                sp.dma_start(vs[u][:, :, :], values_d[a][b, g]).then_inc(vs_in[u], 16)

            def first_load(a, b, k):
                for i in range(2):
                    wait(part_out[i], 16 * 4 * (k + 1))
                    wait(vq_out[i], 16 * 2 * NG * (k + 1))
                wait(shift_out, 16 * (k + 1))
                load(a, b, 0)

            def exact(a, b):
                for i in range(2):
                    wait(qs_in[i], 16 * QS_DMAS * 2 * (a * B + b) + (0 if i else 16 * QS_DMAS))
                for g in range(NG):
                    parts_in(a, b, g, 0, m_in)
                    wait(m_parts, g + 1)
                    for i in range(2):
                        sp.dma_start(shift_d[a][b, i, g * HG:(g + 1) * HG].rearrange("h (t s) -> (h t) s", t=T),
                                     mxp[:, i, :]).then_inc(m_out, 16)
                    wait(m_out, 16 * 2 * (g + 1))
                parts_in(a, b, 0, 0, m_in)
                shift_in(a, b, 0, 0, m_in)
                wait(m_restored, 1)
                for s in (m_in, m_scores, m_read, m_rows, m_turned, m_parts, m_out, m_restored):
                    sp.sem_clear(s)

            def store(a, b, g):
                wait(acc_read, 2 * ((a * B + b) * NG + g) + 2)
                sp.dma_start(num_d[a][b, g], num[g % 2][:, :]).then_inc(num_out[g % 2], 16)

            def slot(a, b, k, following, sides, paced, operands=None, rows=None):
                wait(flag_ready, k + 1)
                with sp.If(sp.value_load(flags[0:1, bass.ds(k, 1)], min_val=0, max_val=1)):
                    exact(a, b)
                for n in range(UB):
                    g, u = n // UG, n % UG
                    if n == 0 and operands is not None:
                        operands()
                    if n == 1:
                        load(a, b, 1)
                    if g >= 1 and u == PV_LAG and g + 1 < NG:
                        load(a, b, g + 1)
                    if g >= 1 and u == PV_LAG + 3:
                        store(a, b, g - 1)
                    advance(sides, paced[n])
                    if n == NEXT_LOAD and rows is not None:
                        p1_rows(*rows)
                    if n == NEXT_LOAD and following is not None:
                        first_load(*following)
                for w in sides:
                    finish(w)
                store(a, b, NG - 1)

            p1_rows(0, 0)
            for _t, landing, d in NARROW:
                sp.dma_start(landing, d).then_inc(first_weights_in, 16)
            for t, d in FIRST:
                sp.dma_start(t[:], d).then_inc(first_weights_in, 16)
            sp.dma_start(bv[:, :], bc(bv_d)).then_inc(first_weights_in, 16)
            p1_rows(1, 1)
            finish(p1(0, *p1_at(0)))
            sp.wait_ge(filled, FILLS)
            first_load(0, 0, 0)
            slot(0, 0, 0, (0, 1, 1), [p1(1, *p1_at(1))], PACE1, rows=(2, 2))
            with sp.Fori(0, 2) as s:
                slot(0, s + 1, s + 1, (0, s + 2, 2 * s + 2), [p1(s + 2, *p1_at(0, s)), p2(s, *p2_at(0, s))],
                     PACE12, lambda: p2_operands(s), (B - 1, s + 3))
            slot(0, 3, 4, (1, 0, 3), [idle(START), p2(2, *p2_at(2))], PACE2, lambda: p2_operands(2))
            slot(1, 0, 3, (1, 1, 5), [idle(START), p2(3, *p2_at(3))], PACE2, lambda: p2_operands(3))
            with sp.Fori(0, 2) as s:
                slot(1, s + 1, s + 5, (1, s + 2, s + 6), [p3(s)], PACE3, lambda: p3_operands(s))
            slot(1, 3, 7, None, [p3(2)], PACE3, lambda: p3_operands(2))
            p3_operands(3)
            finish(p3(3))
            wait(y_out, 16 * B + 1)

        @block.tensor
        def _(pe):
            pe.wait_ge(first_weights_in, 16 * n_first)
            pe.wait_ge(filled, FILLS_FIRST)
            pe.wait_ge(narrowed, len(NARROW))

            def start_job(jobs, half, name):
                i = jobs.bank(name)
                pe.wait_ge(side_free[i], jobs.freed(half, name))
                return side[:, i, :]

            def after(jobs, half, *names):
                for i, v in jobs.last_freed(half, names):
                    pe.wait_ge(side_free[i], v)

            def transposed(bank, col, src, rows, last=False):
                if rows < P:
                    pe.sem_inc(passed[2], 1)
                ins = pe.transpose(bank[0:src.shape[1], col:col + rows], src, ident[0:rows, 0:rows])
                if last:
                    ins.then_inc(side_done, 1)

            def project(jobs, a, b, k, half, w, rotated, turn, j):
                if turn == "xT":
                    bank = start_job(jobs, half, ("xT", j))
                    if j == 0:
                        pe.wait_ge(rows_ready[a], b + 1 + a)
                    for t in range(TQ):
                        transposed(bank, t * P, xnorm[:, j * TQ + t, :], P, last=(rotated is None and t == TQ - 1))
                    if rotated is not None:
                        for t in range(TQ):
                            transposed(bank, QW + t * P, rotated[:, j * TQ + t, :], P, last=(t == TQ - 1))
                if turn == "qk":
                    bank = start_job(jobs, half, ("qk", j))
                    after(jobs, half, ("xT", j))
                    src = xT[:, 0 if rotated is None else 1, :]
                    for c in range(2):
                        ins = pe.matmul(bank[:, c * QW:(c + 1) * QW], w[:, c, :], src, start=True, stop=True)
                    ins.then_inc(side_done, 1)
                if turn == "v":
                    bank = start_job(jobs, half, ("v", j))
                    for t in range(TQ):
                        ins = pe.matmul(bank[:, t * D:(t + 1) * D], xT[:, 0, t * P:(t + 1) * P], w[:, 2, :],
                                        start=True, stop=True)
                    ins.then_inc(side_done, 1)
                if turn == "norm":
                    bank = start_job(jobs, half, ("norm", j))
                    pe.wait_ge(sq_ready, k * NQ + j + 1)
                    for c in range(2 + a):
                        for t in range(TQ):
                            col = (c * TQ + t) * H
                            ins = pe.matmul(bank[:, col:col + H], sq[j % 2][:, c, t * P:(t + 1) * P], headsum[:, :],
                                            start=True, stop=True)
                    ins.then_inc(side_done, 1)
                if turn == "ktop":
                    bank = start_job(jobs, half, ("ktop", 0))
                    after(jobs, half, ("norm", NQ - 1))
                    transposed(bank, 0, nrm[:, 1, :, :].rearrange("p h t -> p (h t)"), P, last=True)
                if turn == "kspread":
                    bank = start_job(jobs, half, ("kspread", 0))
                    pe.wait_ge(keys_spread, k + 1)
                    pe.matmul(bank[:, 0:P], ones[:, :], kdiag[:, :], start=True, stop=True).then_inc(side_done, 1)
                if turn == "shift":
                    bank = start_job(jobs, half, ("shift", 0))
                    pe.wait_ge(gap_ready, k + 1)
                    transposed(bank, P, gm[:, 0:1], P)
                    transposed(bank, 0, ns[:, :, :].rearrange("p h t -> p (h t)"), P, last=True)

            def combine(jobs, a, b, half, w, turn, t):
                if turn == "num":
                    j = t // TQ
                    bank = start_job(jobs, half, ("num", t))
                    if t % TQ == 0:
                        pe.wait_ge(nt_in[j % 2], 16 * ((a * B + b) * 2 + j // 2 + 1))
                    for g in range(NG):
                        transposed(bank, g * P, nt[j % 2][:, g, (t % TQ) * P:(t % TQ + 1) * P], P, last=(g == NG - 1))
                if turn == "att":
                    bank = start_job(jobs, half, ("att", t))
                    pe.wait_ge(att_ready[a], b * T + t + 2)
                    transposed(bank, 0, att[:, t % 2, :], P, last=True)
                if turn == "out":
                    bank = start_job(jobs, half, ("out", t))
                    after(jobs, half, ("att", t))
                    pe.matmul(bank[:, 0:D], attT[:, t % 2, :], w[:, :], start=True, stop=True).then_inc(side_done, 1)

            def p1(b, k, half):
                for turn, i in P1_TURNS:
                    project(P1, 0, b, k, half, wqkv, None, turn, i)
                    if turn == "suffix":
                        bank = start_job(P1, half, ("suffix", i))
                        if i == 0:
                            pe.wait_ge(vsum_ready, b + 1)
                        for c, t in enumerate(range(3 * i, min(3 * i + 3, T))):
                            o = bank[:, c * 144:(c + 1) * 144]
                            ins = pe.matmul(o, later[:, :], vc[:, t, :], start=True, stop=(t == T - 1))
                            if t < T - 1:
                                ins = pe.matmul(o, ones[:, :], vsum[:, t, :], start=False, stop=True)
                        ins.then_inc(side_done, 1)
                    yield

            def p2(b, k, half):
                for turn, i in P2_TURNS:
                    if turn == "em":
                        bank = start_job(P2, half, ("em", 0))
                        pe.wait_ge(em_ready, b + 1)
                        transposed(bank, 0, em[:, :], P, last=True)
                    combine(P2, 0, b, half, wr, turn, i)
                    project(P2, 1, b, k, half, win, rope, turn, i)
                    yield

            def p3(b, half):
                for turn, i in P3_TURNS:
                    combine(P3, 1, b, half, wo, turn, i)
                    if turn == "x1T":
                        bank = start_job(P3, half, ("x1T", i))
                        if i == 0:
                            pe.wait_ge(x1_ready, b + 1)
                        for t in range(TQ):
                            transposed(bank, t * P, x1[:, i * TQ + t, :], P, last=(t == TQ - 1))
                    if turn == "gate":
                        bank = start_job(P3, half, ("gate", 0))
                        after(P3, half, ("x1T", 2), ("x1T", 3))
                        for t in range(T):
                            ins = pe.matmul(bank[:, t * NE:(t + 1) * NE], x1T[:, t, :], wg[:, :], start=True, stop=True)
                        ins.then_inc(side_done, 1)
                    if turn == "GT":
                        bank = start_job(P3, half, ("GT", i))
                        if i == 0:
                            pe.wait_ge(G_ready, b + 1)
                        for t in range(4):
                            transposed(bank, t * P, G[:, 4 * i + t, :], P, last=(t == 3))
                    if turn == "bias":
                        if i == 0:
                            after(P3, half, ("GT", 0), ("GT", 1))
                        bank = start_job(P3, half, ("bias", i))
                        pe.matmul(bank[:, 0:D], GT[:, i, :], be[:, :], start=True, stop=True).then_inc(side_done, 1)
                    if turn in ("e0", "e1"):
                        bank = start_job(P3, half, (turn, i))
                        first = 512 * int(turn[1])
                        pe.matmul(bank, x1T[:, i, :], we[:, first:first + 512], start=True, stop=True)\
                          .then_inc(side_done, 1)
                    if turn == "pad":
                        bank = start_job(P3, half, ("pad", 0))
                        pe.transpose(bank[:, 0:P], ident[:, :], ident[:, :]).then_inc(side_done, 1)
                    yield

            def scores_unit(a, b, n):
                g, u = n // UG, (n // UG) % 2
                gn = (a * B + b) * UB + n
                kind, heads = unit_kind(n)
                if n % UG == 0:
                    pe.wait_ge(qs_in[u], 16 * QS_DMAS * ((a * B + b) * 2 + g // 2 + 1))
                if n >= NSC:
                    pe.wait_ge(probs_raw, gn - NSC + 1)
                else:
                    pe.wait_ge(probs_raw, (a * B + b) * UB)
                buf = scores[:, n % NSC, :, :]
                for h, c0 in heads:
                    for pieces in KINDS[kind]:
                        for kt, col, q0, w in pieces:
                            c = c0 + col
                            ins = pe.matmul(buf[:, c // 512, c % 512:c % 512 + w],
                                            ks[u][:, h, kt * P:(kt + 1) * P], qs[u][:, h, q0:q0 + w],
                                            start=True, stop=True)
                ins.then_inc(scores_ready, 1)

            def value_group(a, b, gi):
                hg, g = gi // GG, gi % GG
                u = hg % 2
                kind, pos = group_of(g)
                base = (a * B + b) * UB + hg * UG
                if g == 0:
                    pe.wait_ge(vs_in[u], 16 * ((a * B + b) * 2 + hg // 2 + 1))
                pe.wait_ge(probs_ready, base + min(4 * kind + 4, UG))
                if g < 2:
                    pe.wait_ge(acc_read, 2 * ((a * B + b) * NG + hg) - 1 + g if (hg or g) else 2 * (a * B + b) * NG)
                for kt, col, q0, w in KINDS[kind][pos]:
                    for h in range(HG):
                        if kind < 4:
                            un, c = hg * UG + 4 * kind + h, col
                        else:
                            un, c = hg * UG + 16 + h // 2, (h % 2) * 512
                        ins = pe.matmul(acc[h * VW:(h + 1) * VW, q0 // 512, q0 % 512:q0 % 512 + w],
                                        vs[u][:, kt, h * VW:(h + 1) * VW], probs[un % NPB][:, c:c + w],
                                        start=(kt == 0), stop=(kt, q0) in ((3, 384), (4, 512)),
                                        skip_group_check=True)
                ins.then_inc(group_done, 1)

            def exact(a, b):
                i = 0
                for g in range(NG):
                    pe.wait_ge(m_in, 16 * M_DMAS * (g + 1))
                    for h in range(HG):
                        for t in range(T):
                            if i >= NSC:
                                pe.wait_ge(m_read, i - NSC + 1)
                            elif g == 0 and (b if isinstance(b, int) else 1):
                                pe.wait_ge(probs_raw, (a * B + b) * UB)
                                pe.wait_ge(acc_read, 2 * (a * B + b) * NG)
                            w = (t + 1) * P
                            for c in range(0, w, 512):
                                cw = min(512, w - c)
                                last = c + cw == w
                                buf = scores[:, i % NSC, c // 512, :]
                                q1 = qs[0][0:KROWS, h, t * P:(t + 1) * P]
                                seen = cw - P if last else cw
                                if seen:
                                    pe.matmul(buf[:, 0:seen], q1, ks[0][0:KROWS, h, c:c + seen],
                                              start=True, stop=True)
                                if last:
                                    pe.matmul(buf[:, seen:cw], q1, ks[0][0:KROWS, h, c + seen:c + cw],
                                              start=True, stop=False)
                                    pe.matmul(buf[:, seen:cw], ident_b[:, :], hide[a][:, :], start=False,
                                              stop=True).then_inc(m_scores, 1)
                            i += 1
                    pe.wait_ge(m_rows, g + 1)
                    pe.transpose(acc[0:HG * T, 0, 0:P], mx[:, :], ident[:, :]).then_inc(m_turned, 1)
                pe.wait_ge(m_in, 16 * (M_DMAS * (NG + 1) + 1))
                pe.sem_inc(m_restored, 1)

            def slot(a, b, k, sides, paced):
                pe.wait_ge(flag_ready, k + 1)
                with pe.If(pe.value_load(flags[0:1, bass.ds(k, 1)], min_val=0, max_val=1)):
                    exact(a, b)
                for n in range(UB):
                    scores_unit(a, b, n)
                    for gi in range(groups_after(n - 1), groups_after(n)):
                        value_group(a, b, gi)
                    advance(sides, paced[n])
                value_group(a, b, GB - 1)
                for w in sides:
                    finish(w)

            finish(p1(0, *p1_at(0)))
            pe.wait_ge(weights_in, 16 * n_weights)
            pe.wait_ge(filled, FILLS)
            slot(0, 0, 0, [p1(1, *p1_at(1))], PACE1)
            with pe.Fori(0, 2) as s:
                slot(0, s + 1, s + 1, [p1(s + 2, *p1_at(0, s)), p2(s, *p2_at(0, s))], PACE12)
            slot(0, 3, 4, [idle(START), p2(2, *p2_at(2))], PACE2)
            slot(1, 0, 3, [idle(START), p2(3, *p2_at(3))], PACE2)
            with pe.Fori(0, 3) as s:
                slot(1, s + 1, s + 5, [p3(s, p3_at(s))], PACE3)
            finish(p3(3, p3_at(3)))

        @block.scalar
        def _(act):
            step = [0]

            def link(ins):
                step[0] += 1
                ins.then_inc(act_step, 1)
                act.wait_ge(act_step, step[0])

            def fresh():
                act.sem_clear(act_step)
                step[0] = 0

            def copied(jobs, half, name, dst, cols, rows=P):
                act.wait_ge(side_done, jobs.done(half, name))
                i = jobs.bank(name)
                act.activation(dst, side[0:rows, i, 0:cols], ACT.Copy).then_inc(side_free[i], 1)

            def first_root(phase, n):
                act.wait_ge(var_ready[phase], n + 1)
                link(act.activation(lnv[:, :], var[:, :], ACT.Ln))
                act.activation(r0[:, :], lnv[:, :], ACT.Exp, scale=-0.5).then_inc(r0_ready[phase], 1)

            def project(jobs, a, k, half, turn, j):
                if turn == "xT":
                    copied(jobs, half, ("xT", j), xT[:, 0:a + 1, :].rearrange("p c s -> p (c s)"), (a + 1) * QW)
                if turn == "roots":
                    act.wait_ge(square_ready, k + 1)
                    link(act.activation(cl[:, :, :], c2[:, :, :], ACT.Ln))
                    act.activation(cc[:, :, :], cl[:, :, :], ACT.Exp, scale=0.5).then_inc(root_ready, 1)

            def p1(b, k, half):
                fresh()
                for turn, j in P1_TURNS:
                    if turn == "root":
                        first_root(0, b)
                    project(P1, 0, k, half, turn, j)
                    yield

            def p2(b, k, half):
                fresh()
                for turn, j in P2_TURNS:
                    if turn == "exp":
                        act.wait_ge(esum_ready, b + 1)
                        act.activation(em[:, :], esum[:, :], ACT.Exp, scale=SCALE).then_inc(em_ready, 1)
                    if turn == "root":
                        first_root(1, b)
                    project(P2, 1, k, half, turn, j)
                    yield

            def p3(b, half):
                fresh()
                for turn, i in P3_TURNS:
                    if turn == "root":
                        first_root(2, 2 * b + i)
                    if turn == "exp":
                        act.wait_ge(gates_shifted, b + 1)
                        act.activation(ga[:, :, :], gl[:, :, :], ACT.Exp).then_inc(gates_exp, 1)
                    yield

            def sums_out(a, b, h):
                g, i = h // 2, h % 2
                n = (a * B + b) * NG + g
                if i == 0:
                    act.wait_ge(num_out[g % 2], 16 * ((a * B + b) * (NG // 2) + g // 2))
                act.wait_ge(group_done, n * GG + GG - 1 + i)
                act.activation(num[g % 2][:, i * 512:(i + 1) * 512], acc[:, i, :], ACT.Copy).then_inc(acc_read, 1)

            def slot(a, b, sides, paced):
                for n in range(UB):
                    gn = (a * B + b) * UB + n
                    act.wait_ge(scores_ready, gn + 1)
                    if n >= NPB:
                        m = n - NPB
                        act.wait_ge(group_done, ((a * B + b) * NG + m // UG) * GG + groups_before(unit_kind(m)[0]))
                    else:
                        act.wait_ge(group_done, (a * B + b) * GB)
                    act.activation(probs[n % NPB][:, :], scores[:, n % NSC, :, :].rearrange("p c s -> p (c s)"),
                                   ACT.Exp, scale=SCALE).then_inc(probs_raw, 1)
                    if n >= UG and n % UG in (PV_LAG - 2, PV_LAG):
                        sums_out(a, b, 2 * (n // UG) - 2 + (n % UG == PV_LAG))
                    advance(sides, paced[n])
                for h in (2 * NG - 2, 2 * NG - 1):
                    sums_out(a, b, h)
                for w in sides:
                    finish(w)

            act.preload_act_table_set("natural_log_exp_and_others")
            for t, d in WEIGHTS:
                act.dma_start(t[:], d).then_inc(weights_in, 16)
            for t, d in ROWS:
                act.dma_start(t[:, :], d.unsqueeze(0).broadcast_to([P, d.shape[0]])).then_inc(weights_in, 16)
            for t, d in ((cos, cos_d), (sin, sin_d)):
                act.dma_start(t[:, :, :], d.rearrange("(t p) f -> p t f", p=P)).then_inc(weights_in, 16)
            finish(p1(0, *p1_at(0)))
            slot(0, 0, [p1(1, *p1_at(1))], PACE1)
            with act.Fori(0, 2) as s:
                slot(0, s + 1, [p1(s + 2, *p1_at(0, s)), p2(s, *p2_at(0, s))], PACE12)
            slot(0, 3, [idle(START), p2(2, *p2_at(2))], PACE2)
            slot(1, 0, [idle(START), p2(3, *p2_at(3))], PACE2)
            with act.Fori(0, 3) as s:
                slot(1, s + 1, [p3(s, p3_at(s))], PACE3)
            finish(p3(3, p3_at(3)))

        @block.gpsimd
        def _(pool):
            def ones_of(v):
                return v[:, :, :].rearrange("p t (h v) -> p (t h) v", v=VW)[:, :, HE:HE + 1]

            for s in RAISED:
                pool.sem_inc(s, 1)
            fills = [(ones[:, :], 1.0), (vq[0][:, :, :], 0.0), (vq[1][:, :, :], 0.0), (vc[:, :, :], 1.0),
                     (ones_of(vq[0]), 1.0), (ones_of(vq[1]), 1.0),
                     (qs[0][64:KPAD, :, :], 0.0), (ks[0][64:KPAD, :, :], 1.0),
                     (qs[1][64:KPAD, :, :], 0.0), (ks[1][64:KPAD, :, :], 1.0)]
            assert len(fills) == FILLS
            for i, (tile, value) in enumerate(fills[:FILLS_FIRST]):
                if i:
                    pool.wait_ge(filled, i)
                pool.memset(tile, value).then_inc(filled, 1)


            step = [0]

            def link(ins):
                step[0] += 1
                ins.then_inc(pool_step, 1)
                pool.wait_ge(pool_step, step[0])

            def fresh():
                pool.sem_clear(pool_step)
                step[0] = 0

            def project(jobs, a, k, half, turn, j):
                p, f = part[j % 2], qk[j % 2]
                if turn == "split":
                    pool.wait_ge(first_part_ready, k * NQ + j + 1)
                    pool.tensor_tensor(qkr[j % 2][:, :, :], f[:, :, :], p[:, 0, :, :], ALU.subtract)
                    link(pool.tensor_tensor(p[:, 1, :, :], f[:, :, :], p[:, 0, :, :], ALU.subtract))
                if turn == "parts":
                    pool.tensor_tensor(p[:, 2, :, :], qkr[j % 2][:, :, :], p[:, 1, :, :], ALU.subtract).then_inc(part_ready, 1)

            def p1(b, k, half):
                fresh()
                for turn, j in P1_TURNS:
                    project(P1, 0, k, half, turn, j)
                    if turn == "ktop":
                        pool.wait_ge(vc_ready, (b + 1) * NQ)
                        pool.sem_inc(passed[1], 1)
                        link(pool.tensor_copy(vsum[:, T - 2, :], vc[:, T - 1, :]))
                        for t in range(T - 3, -1, -1):
                            ins = pool.tensor_tensor(vsum[:, t, :], vsum[:, t + 1, :], vc[:, t + 1, :], ALU.add)
                            if t:
                                link(ins)
                            else:
                                ins.then_inc(vsum_ready, 1)
                    yield

            def p2(b, k, half):
                fresh()
                for turn, j in P2_TURNS:
                    project(P2, 1, k, half, turn, j)
                    yield

            def moe_tile(b, t):
                pool.wait_ge(products_ready, b * T + t + 1)
                link(pool.tensor_tensor(moe[:, :, :], psum4[:, t % 2, 0:2, :], psum4[:, t % 2, 2:4, :], ALU.add))
                link(pool.tensor_tensor(moe1[:, :], moe[:, 0, :], moe[:, 1, :], ALU.add))
                pool.tensor_tensor(xnorm[:, t, :], moe1[:, :], x1b[:, t % 2, :], ALU.add).then_inc(moe_ready, 1)

            def p3(b):
                fresh()
                for turn, t in P3_TURNS:
                    if turn == "gate":
                        pool.wait_ge(xn_in, 32 * (b + 1))
                        bias = l2b[:, :].unsqueeze(1).broadcast_to([P, T, D])
                        pool.tensor_tensor(x2[:, :, :], x2[:, :, :], bias, ALU.add).then_inc(rows_biased, 1)
                    if turn == "e0" and t:
                        moe_tile(b, t - 1)
                    if turn == "pad":
                        moe_tile(b, T - 1)
                    yield

            def slot(a, b, sides, paced):
                for n in range(UB):
                    gn = (a * B + b) * UB + n
                    kind, _heads = unit_kind(n)
                    c0, step = DIAGONALS[kind]
                    buf = probs[n % NPB]
                    if step:
                        first = min(c0, S - 2 * step)
                        diag = buf[:, first:first + 2 * step].rearrange("p (k s) -> p k s", k=2)
                        diag = diag[:, :, c0 - first:c0 - first + P]
                    else:
                        diag = buf[:, c0:c0 + P].unsqueeze(1)
                    pool.wait_ge(probs_raw, gn + 1)
                    pool.sem_inc(passed[1], 1)
                    pool.affine_select(out=diag, in_=diag, compare_op=ALU.is_ge, fill=0.0, base=a - 1,
                                       pattern=[[0, diag.shape[1]], [1, P]], channel_multiplier=-1)\
                        .then_inc(probs_ready, 1)
                    advance(sides, paced[n])
                for w in sides:
                    finish(w)

            for i, (tile, value) in enumerate(fills[FILLS_FIRST:]):
                pool.wait_ge(filled, FILLS_FIRST + i)
                pool.memset(tile, value).then_inc(filled, 1)
            pool.wait_ge(filled, FILLS)
            finish(p1(0, *p1_at(0)))
            pool.wait_ge(weights_in, 16 * n_weights)
            slot(0, 0, [p1(1, *p1_at(1))], PACE1)
            with pool.Fori(0, 2) as s:
                slot(0, s + 1, [p1(s + 2, *p1_at(0, s)), p2(s, *p2_at(0, s))], PACE12)
            slot(0, 3, [idle(START), p2(2, *p2_at(2))], PACE2)
            slot(1, 0, [idle(START), p2(3, *p2_at(3))], PACE2)
            with pool.Fori(0, 3) as s:
                slot(1, s + 1, [p3(s)], PACE3)
            finish(p3(3))

        @block.vector
        def _(dve):
            step = [0]

            def link(ins):
                step[0] += 1
                ins.then_inc(dve_step, 1)
                dve.wait_ge(dve_step, step[0])

            def fresh():
                dve.sem_clear(dve_step)
                step[0] = 0

            def bank_of(jobs, half, name):
                dve.wait_ge(side_done, jobs.done(half, name))
                return side[:, jobs.bank(name), :]

            def freeing(ins, jobs, half, name):
                ins.then_inc(side_free[jobs.bank(name)], 1)
                after(jobs, half, name)

            def after(jobs, half, *names):
                for i, v in jobs.last_freed(half, names):
                    dve.wait_ge(side_free[i], v)

            def skip(jobs, half, name):
                bank_of(jobs, half, name)
                freeing(dve.memset(gsum[0:1, 0:1], 0.0), jobs, half, name)

            def tt(out, in0, in1, op):
                return dve.tensor_tensor(out, in0, in1, op)

            def layernorm(src, phase, n, first=0):
                for t in range(first, T):
                    ins = dve.bn_stats(stats[:, t, :], src[:, t, :])
                link(ins)
                for t in range(T):
                    ins = dve.bn_aggr(mv[:, t, :], stats[:, t, :])
                link(ins)
                dve.tensor_scalar(var[:, :], mv[:, :, 1], EPS, None, ALU.add).then_inc(var_ready[phase], 1)
                dve.wait_ge(var_ready[phase], n + 1)
                dve.wait_ge(r0_ready[phase], n + 1)
                link(tt(rt[:, :], r0[:, :], r0[:, :], ALU.mult))
                link(tt(rt[:, :], rt[:, :], var[:, :], ALU.mult))
                link(dve.tensor_scalar(rt[:, :], rt[:, :], -0.5, 1.5, ALU.mult, ALU.add))
                link(tt(rstd[:, :], r0[:, :], rt[:, :], ALU.mult))

            def normalised(dst, src, t):
                return dve.tensor_scalar(dst[:, t, :], src[:, t, :], mv[:, t, 0:1], rstd[:, t:t + 1],
                                         ALU.subtract, ALU.mult)

            def normalised_with(dst, src, weight, added):
                for t in range(T):
                    ins = dve.scalar_tensor_tensor(out=dst[:, t, :], in0=src[:, t, :], scalar=mv[:, t, 0:1], in1=weight[:, :],
                                                   op0=ALU.subtract, op1=ALU.mult)
                link(ins)
                for t in range(T):
                    ins = dve.scalar_tensor_tensor(out=dst[:, t, :], in0=dst[:, t, :], scalar=rstd[:, t:t + 1], in1=added(t),
                                                   op0=ALU.mult, op1=ALU.add)
                return ins

            def over_tiles(row):
                return row[:, :].unsqueeze(1).broadcast_to([P, T, row.shape[1]])

            def norms_out(jobs, a, half, j):
                bank = bank_of(jobs, half, ("norm", j))
                for c in range(2 + a):
                    ins = dve.tensor_copy(nrm[:, c, :, j * TQ:(j + 1) * TQ].rearrange("p h t -> p t h"),
                                          bank[:, c * TQ * H:(c + 1) * TQ * H].rearrange("p (t h) -> p t h", h=H))
                freeing(ins, jobs, half, ("norm", j))

            def project(jobs, a, k, half, bias, vbias):
                for j in range(NQ):
                    uses = k * 2 + j // 2
                    p, f = part[j % 2], qk[j % 2]
                    bank = bank_of(jobs, half, ("qk", j))
                    dve.wait_ge(part_out[j % 2], 16 * 2 * uses)
                    dve.tensor_scalar(f[:, 0, :], bank[:, 0:QW], bias[:, 0:1], None, ALU.add)
                    freeing(dve.tensor_scalar(f[:, 1, :], bank[:, QW:2 * QW], bias[:, 1:2], None, ALU.add),
                            jobs, half, ("qk", j))
                    dve.tensor_copy(p[:, 0, :, :], f[:, :, :]).then_inc(first_part_ready, 1)
                    bank = bank_of(jobs, half, ("v", j))
                    dve.wait_ge(vq_out[j % 2], 16 * NG * uses)
                    v = vq[j % 2][:, :, :].rearrange("p t (h v) -> p t h v", v=VW)[:, :, :, 0:HE]
                    vb = vbias[:, :].rearrange("p (h f) -> p h f", f=HE).unsqueeze(1).broadcast_to([P, TQ, H, HE])
                    freeing(tt(v, bank[:, 0:TQ * D].rearrange("p (t h f) -> p t h f", t=TQ, f=HE), vb, ALU.add),
                            jobs, half, ("v", j))
                    dve.wait_ge(first_part_ready, k * NQ + j + 1)
                    if a == 1:
                        tt(sq[j % 2][:, 2, :], p[:, 0, 0, :], p[:, 0, 1, :], ALU.mult)
                    tt(sq[j % 2][:, 0:2, :], p[:, 0, :, :], p[:, 0, :, :], ALU.mult).then_inc(sq_ready, 1)
                    if j:
                        norms_out(jobs, a, half, j - 1)
                    if a == 0:
                        dve.tensor_copy(vc[:, j * TQ:(j + 1) * TQ, :].rearrange("p t (h f) -> p (t h) f", f=9)[:, :, 0:HE],
                                        vq[j % 2][:, :, :].rearrange("p t (h v) -> p (t h) v", v=VW)[:, :, 0:HE])\
                           .then_inc(vc_ready, 1)

            def bound_spreads(jobs, k, half):
                bank = bank_of(jobs, half, ("ktop", 0))
                freeing(dve.tensor_reduce(kmx[:, :], bank[:, 0:P], AX.X, ALU.max), jobs, half, ("ktop", 0))
                dve.tensor_scalar(kdiag[:, :], ident[:, :], kmx[:, 0:1], None, ALU.mult).then_inc(keys_spread, 1)

            def bound_squares(jobs, k, half):
                bank = bank_of(jobs, half, ("kspread", 0))
                freeing(dve.tensor_copy(ktop[:, :, :].rearrange("p h t -> p (h t)"), bank[:, 0:P]), jobs, half, ("kspread", 0))
                for t in range(1, T):
                    link(tt(ktop[:, :, t], ktop[:, :, t], ktop[:, :, t - 1], ALU.max))
                link(tt(c2[:, :, :], nrm[:, 0, :, :], ktop[:, :, :], ALU.mult))
                dve.tensor_scalar(c2[:, :, :], c2[:, :, :], 1e-12, None, ALU.max).then_inc(square_ready, 1)
                dve.wait_ge(square_ready, k + 1)
                link(dve.tensor_reduce(gm[:, 1:2], c2[:, :, :], AX.XY, ALU.max))
                link(dve.tensor_scalar(gm[:, 1:2], gm[:, 1:2], 1.0 / SQUARE_LIMIT, None, ALU.mult))

            def bound_ends(jobs, a, k, half):
                dve.wait_ge(root_ready, k + 1)
                if a == 1:
                    dve.scalar_tensor_tensor(out=ns[:, :, :], in0=cc[:, :, :], scalar=1.02, in1=nrm[:, 2, :, :],
                                             op0=ALU.mult, op1=ALU.add)
                    link(dve.scalar_tensor_tensor(out=cc[:, :, :], in0=cc[:, :, :], scalar=1.02, in1=nrm[:, 2, :, :],
                                                  op0=ALU.mult, op1=ALU.subtract))
                    dve.tensor_scalar(ns[:, :, :], ns[:, :, :], -0.5, None, ALU.mult)
                else:
                    dve.tensor_scalar(ns[:, :, :], cc[:, :, :], -0.51, None, ALU.mult)
                    link(dve.tensor_scalar(cc[:, :, :], cc[:, :, :], 1.02, None, ALU.mult))
                link(dve.tensor_reduce(gm[:, 0:1], cc[:, :, :], AX.XY, ALU.max))
                link(dve.tensor_scalar(gm[:, 0:1], gm[:, 0:1], 1.0 / LIMIT, None, ALU.mult))
                tt(gm[:, 0:1], gm[:, 0:1], gm[:, 1:2], ALU.max).then_inc(gap_ready, 1)
                bank = bank_of(jobs, half, ("shift", 0))
                dve.wait_ge(shift_out, 16 * k)
                link(dve.tensor_copy(shb[:, 0, :], bank[:, 0:P]))
                tt(shb[:, 1, :], bank[:, 0:P], shb[:, 0, :], ALU.subtract).then_inc(shift_ready, 1)
                freeing(dve.tensor_reduce(gm1[:, :], bank[0:1, P:2 * P], AX.X, ALU.max), jobs, half, ("shift", 0))
                dve.tensor_scalar(flags[0:1, bass.ds(k, 1)], gm1[:, :], 1.0, None, ALU.is_gt)\
                   .then_inc(flag_ready, 1)

            def exact(a, b):
                i = 0
                for g in range(NG):
                    if g >= 1:
                        dve.wait_ge(m_turned, g)
                    for h in range(HG):
                        for t in range(T):
                            dve.wait_ge(m_scores, i + 1)
                            dve.reduce_max(mx[:, h * T + t:h * T + t + 1],
                                           scores[:, i % NSC, :, :].rearrange("p c s -> p (c s)")[:, 0:(t + 1) * P],
                                           AX.X).then_inc(m_read, 1)
                            i += 1
                    dve.wait_ge(m_read, i)
                    dve.tensor_scalar(mx[:, :], mx[:, :], 0.0 if a == 0 else NEG, None, ALU.max).then_inc(m_rows, 1)
                    dve.wait_ge(m_turned, g + 1)
                    link(dve.tensor_scalar(mxn[:, :], acc[0:HG * T, 0, 0:P], -1.0, None, ALU.mult))
                    if g >= 1:
                        dve.wait_ge(m_out, 16 * 2 * g)
                    link(dve.tensor_copy(mxp[:, 0, :], mxn[:, :]))
                    tt(mxp[:, 1, :], mxn[:, :], mxp[:, 0, :], ALU.subtract).then_inc(m_parts, 1)

            def exact_if(a, b, k):
                fresh()
                dve.wait_ge(flag_ready, k + 1)
                with dve.If(dve.value_load(flags[0:1, bass.ds(k, 1)], min_val=0, max_val=1)):
                    exact(a, b)

            def combine(jobs, a, b, half, dst):
                for t in range(T + 2):
                    if t < T:
                        if a == 0:
                            link(tt(tot[:, t % 2, :, :], sfx[:, t, :].rearrange("p (h f) -> p h f", f=9),
                                    emr[:, :, t].unsqueeze(2).broadcast_to([P, H, 9]), ALU.mult))
                        bank = bank_of(jobs, half, ("num", t))
                        nb = bank.rearrange("p (h v) -> p h v", v=VW)[:, :, 0:9]
                        if a == 0:
                            freeing(tt(tot[:, t % 2, :, :], nb, tot[:, t % 2, :, :], ALU.add), jobs, half, ("num", t))
                        else:
                            freeing(dve.tensor_copy(tot[:, t % 2, :, :], nb), jobs, half, ("num", t))
                        link(dve.reciprocal(rden[:, t % 2, :], tot[:, t % 2, :, 8]))
                        tt(att[:, t % 2, :].rearrange("p (h f) -> p h f", f=HE), tot[:, t % 2, :, 0:HE],
                           rden[:, t % 2, :].unsqueeze(2).broadcast_to([P, H, HE]), ALU.mult).then_inc(att_ready[a], 1)
                    if 0 <= t - 1 < T:
                        bank = bank_of(jobs, half, ("att", t - 1))
                        dve.tensor_copy(attT[:, (t - 1) % 2, :], bank[:, 0:P]).then_inc(side_free[jobs.bank(("att", t - 1))], 1)
                    if t >= 2:
                        bank = bank_of(jobs, half, ("out", t - 2))
                        freeing(tt(dst[:, t - 2, :], bank[:, 0:D], xrow[:, t - 2, :], ALU.add), jobs, half, ("out", t - 2))

            def narrow():
                dve.wait_ge(first_weights_in, 16 * n_first)
                dve.wait_ge(filled, FILLS_FIRST)
                for t, landing, _d in NARROW:
                    dve.tensor_copy(t[:, :], landing).then_inc(narrowed, 1)
                dve.wait_ge(narrowed, len(NARROW))

            def p1(b, k, half, p2s, first=False):
                fresh()
                dve.wait_ge(x_in[0], 16 * (b + 1))
                layernorm(xrow0, 0, b)
                if first:
                    narrow()
                dve.wait_ge(rows_out, 32 * p2s + 1)
                for t in range(T - 1):
                    normalised(xnorm, xrow0, t)
                normalised(xnorm, xrow0, T - 1).then_inc(rows_ready[0], 1)
                dve.wait_ge(rows_ready[0], b + 1)
                project(P1, 0, k, half, bqk, bv)
                norms_out(P1, 0, half, NQ - 1)
                bound_spreads(P1, k, half)
                bound_squares(P1, k, half)
                bound_ends(P1, 0, k, half)
                dve.wait_ge(sfx_out, 16 * b)
                for i in range(3):
                    bank = bank_of(P1, half, ("suffix", i))
                    w = min(3, T - 3 * i)
                    dve.tensor_copy(sfx0[:, 3 * i:3 * i + w, :].rearrange("p t f -> p (t f)"), bank[:, 0:w * 144])\
                       .then_inc(side_free[P1.bank(("suffix", i))], 1)

            def p2(b, k, half):
                fresh()
                dve.wait_ge(sh2_in, 16 * (b + 1))
                tt(esum[:, :], sh2[:, 0, :], sh2[:, 1, :], ALU.add).then_inc(esum_ready, 1)
                dve.wait_ge(x_in[1], 16 * (b + 1))
                link(tt(xrow[:, :, :], xrow[:, :, :], over_tiles(br), ALU.add))
                bank = bank_of(P2, half, ("em", 0))
                freeing(dve.tensor_copy(emr[:, :, :].rearrange("p h t -> p (h t)"), bank[:, 0:P]), P2, half, ("em", 0))
                dve.wait_ge(sfx_in, 16 * (b + 1))
                dve.wait_ge(rows_out, 32 * b + 1)
                combine(P2, 0, b, half, x2)
                layernorm(x2, 1, b)
                for t in range(T):
                    ins = normalised(xnorm, x2, t)
                link(ins)
                pairs = xnorm[:, :, :].rearrange("p t (h f two) -> p t h f two", h=H, two=2)
                turned = rope[:, :, :].rearrange("p t (h f two) -> p t h f two", h=H, two=2)
                c4, s4 = (w[:, :, :].unsqueeze(2).broadcast_to([P, T, H, HE // 2]) for w in (cos, sin))
                tmp = [r.rearrange("p (t h f) -> p t h f", t=T, h=H) for r in rtmp]
                tt(tmp[0], pairs[:, :, :, :, 0], c4, ALU.mult)
                tt(tmp[2], pairs[:, :, :, :, 0], s4, ALU.mult)
                link(tt(tmp[1], pairs[:, :, :, :, 1], s4, ALU.mult))
                tt(turned[:, :, :, :, 0], tmp[0], tmp[1], ALU.subtract)
                link(tt(tmp[3], pairs[:, :, :, :, 1], c4, ALU.mult))
                tt(turned[:, :, :, :, 1], tmp[2], tmp[3], ALU.add).then_inc(rows_ready[1], 1)
                dve.wait_ge(rows_ready[1], b + 2)
                project(P2, 1, k, half, binqk, binv)
                norms_out(P2, 1, half, NQ - 1)
                bound_spreads(P2, k, half)
                bound_squares(P2, k, half)
                bound_ends(P2, 1, k, half)

            def p3(b, half):
                fresh()
                dve.wait_ge(xn_in, 32 * (b + 1))
                link(tt(xrow[:, :, :], xrow[:, :, :], over_tiles(bo), ALU.add))
                combine(P3, 1, b, half, xnorm)
                layernorm(xnorm, 2, 2 * b)
                normalised_with(x1, xnorm, l1w, lambda t: l1b[:, :]).then_inc(x1_ready, 1)
                for j in range(NQ):
                    bank = bank_of(P3, half, ("x1T", j))
                    freeing(dve.tensor_copy(x1T[:, j * TQ:(j + 1) * TQ, :].rearrange("p t s -> p (t s)"), bank[:, 0:QW]),
                            P3, half, ("x1T", j))

                def wide(v):
                    return v[:, :].unsqueeze(2).broadcast_to([P, T, NE])

                bank = bank_of(P3, half, ("gate", 0))
                freeing(tt(gl[:, :, :], bank[:, 0:T * NE].rearrange("p (t e) -> p t e", e=NE), over_tiles(bg), ALU.add),
                        P3, half, ("gate", 0))
                link(dve.tensor_reduce(gsum[:, :], gl[:, :, :], AX.X, ALU.max))
                tt(gl[:, :, :], gl[:, :, :], wide(gsum), ALU.subtract).then_inc(gates_shifted, 1)
                dve.wait_ge(gates_exp, b + 1)
                link(dve.tensor_reduce(gsum[:, :], ga[:, :, :], AX.X, ALU.add))
                link(dve.reciprocal(gsum[:, :], gsum[:, :]))
                link(tt(ga[:, :, :], ga[:, :, :], wide(gsum), ALU.mult))
                link(dve.tensor_copy(gb[:, :, :], ga[:, :, :]))
                for i in range(2):
                    link(dve.tensor_reduce(gsum[:, :], gb[:, :, :], AX.X, ALU.max))
                    link(tt(G[:, :, :], gb[:, :, :], wide(gsum), ALU.is_equal))
                    link(tt(G[:, :, :], G[:, :, :], over_tiles(iota8), ALU.mult))
                    link(dve.tensor_reduce(gidx[:, :], G[:, :, :], AX.X, ALU.min))
                    one = G if i else gmask
                    link(tt(one[:, :, :], over_tiles(iota8), wide(gidx), ALU.is_equal))
                    if i == 0:
                        link(dve.scalar_tensor_tensor(out=gb[:, :, :], in0=gmask[:, :, :], scalar=-2.0,
                                                      in1=gb[:, :, :], op0=ALU.mult, op1=ALU.add))
                link(tt(gmask[:, :, :], gmask[:, :, :], G[:, :, :], ALU.add))
                tt(G[:, :, :], ga[:, :, :], gmask[:, :, :], ALU.mult).then_inc(G_ready, 1)
                dve.wait_ge(G_ready, b + 1)
                for i in range(2):
                    bank = bank_of(P3, half, ("GT", i))
                    freeing(dve.tensor_copy(GT[:, 4 * i:4 * i + 4, :].rearrange("e t s -> e (t s)"), bank[0:NE, :]),
                            P3, half, ("GT", i))
                for t in range(T):
                    bank = bank_of(P3, half, ("bias", t))
                    if t >= 2:
                        dve.wait_ge(moe_ready, b * T + t - 1)
                    freeing(tt(x1b[:, t % 2, :], bank[:, 0:D], x1[:, t, :], ALU.add), P3, half, ("bias", t))
                    for i in range(2):
                        bank = bank_of(P3, half, (f"e{i}", t))
                        freeing(tt(prod[:, i, :, :], bank.rearrange("p (e d) -> p e d", d=D),
                                   G[:, t, 4 * i:4 * i + 4].unsqueeze(2).broadcast_to([P, 4, D]), ALU.mult),
                                P3, half, (f"e{i}", t))
                    tt(psum4[:, t % 2, :, :], prod[:, 0, :, :], prod[:, 1, :, :], ALU.add).then_inc(products_ready, 1)
                    if t >= 2:
                        dve.bn_stats(stats[:, t - 2, :], xnorm[:, t - 2, :])
                skip(P3, half, ("pad", 0))
                dve.wait_ge(moe_ready, b * T + T)
                layernorm(xnorm, 2, 2 * b + 1, T - 2)
                dve.wait_ge(rows_biased, b + 1)
                dve.wait_ge(y_out, 16 * b + 1)
                normalised_with(yout, xnorm, l2w, lambda t: x2[:, t, :]).then_inc(y_ready, 1)

            p1(0, *p1_at(0), 0, first=True)
            dve.wait_ge(weights_in, 16 * n_weights)
            exact_if(0, 0, 0)
            p1(1, *p1_at(1), 0)
            with dve.Fori(0, 2) as s:
                exact_if(0, s + 1, s + 1)
                p1(s + 2, *p1_at(0, s), s)
                p2(s, *p2_at(0, s))
            exact_if(0, 3, 4)
            p2(2, *p2_at(2))
            exact_if(1, 0, 3)
            p2(3, *p2_at(3))
            with dve.Fori(0, 3) as s:
                exact_if(1, s + 1, s + 5)
                p3(s, p3_at(s))
            p3(3, p3_at(3))


def host_arrays(i):
    import numpy as np

    order = np.arange(D).reshape(NG, HG, HE).transpose(0, 2, 1).reshape(D)
    wq, bq = i["L0_attn_Wqkv"], i["L0_attn_bqkv"]
    wqkv = np.zeros((D, 3, D), wq.dtype)
    for h in range(H):
        r = slice(h * HE, (h + 1) * HE)
        for c in range(3):
            wqkv[r, c, r] = wq[:, c * HE:(c + 1) * HE]
    wqkv = np.concatenate([wqkv[:, 0:2][:, :, order], wqkv[:, 2:3]], axis=1)
    bqk = np.stack([np.tile(bq[c * HE:(c + 1) * HE], H)[order] for c in range(2)], axis=1)
    win = i["L0_ffn_in_proj_w"].T.reshape(D, 3, D)
    win = np.concatenate([win[:, 0:2][:, :, order], win[:, 2:3]], axis=1)
    binp = i["L0_ffn_in_proj_b"].reshape(3, D)
    angles = (np.arange(S, dtype=np.float32)[:, None]
              * (1.0 / 10000.0 ** (np.arange(0, HE, 2, dtype=np.float32) / HE)).astype(np.float32)[None, :])
    row, col = np.arange(P)[:, None], np.arange(P)[None, :]
    head = (np.arange(P) // (HG * HE)) * HG + np.arange(P) % HG
    return {
        "x": i["L0_attn_x"], "wqkv": wqkv, "bqk": bqk, "bv": np.tile(bq[2 * HE:], H),
        "wr": i["L0_attn_Wr"], "br": i["L0_attn_br"],
        "win": win, "binqk": np.stack([binp[0][order], binp[1][order]], axis=1), "binv": binp[2],
        "wo": i["L0_ffn_out_proj_w"].T, "bo": i["L0_ffn_out_proj_b"],
        "wg": i["L0_ffn_gate_w"].T, "bg": i["L0_ffn_gate_b"],
        "we": i["L0_ffn_expert_w"].transpose(2, 0, 1).reshape(D, NE * D), "be": i["L0_ffn_expert_b"],
        "l1w": i["L0_ffn_ln1_w"], "l1b": i["L0_ffn_ln1_b"], "l2w": i["L0_ffn_ln2_w"], "l2b": i["L0_ffn_ln2_b"],
        "cos": np.cos(angles).astype(np.float32), "sin": np.sin(angles).astype(np.float32),
        "ident": np.eye(P, dtype=np.float32),
        "hide": np.stack([np.where(col >= row, NEG, 0.0), np.where(col > row, NEG, 0.0)]).astype(np.float32),
        "later": (row >= col).astype(np.float32),
        "headsum": (head[:, None] == np.arange(H)[None, :]).astype(np.float32),
        "iota8": np.arange(NE, dtype=np.float32) - NE,
    }


def kernel(**inputs):
    import numpy as np
    import concourse.bacc as bacc
    from concourse.bass_utils import run_bass_kernel_spmd

    nc = bacc.Bacc("TRN2", target_bir_lowering=False, num_devices=1)
    arrays, args = {}, []
    for name, a in host_arrays({k: np.asarray(v) for k, v in inputs.items()}).items():
        a = np.ascontiguousarray(a)
        arrays[f"in_{name}"] = a
        args.append(nc.dram_tensor(f"in_{name}", a.shape, mybir.dt.from_np(a.dtype), kind="ExternalInput").ap())
    args.append(nc.dram_tensor("out_rows", (B, S, D), F32, kind="ExternalOutput").ap())
    build(nc, *args)
    r = run_bass_kernel_spmd(nc, [arrays], core_ids=[0])
    return r.results[0]["out_rows"]
```
